# Optimizing a Trainium2 kernel written in Bass

```python
import numpy as np
import jax
import jax.numpy as jnp

def _softmax(x, axis=-1):
    return jax.nn.softmax(x, axis=axis)

def _gelu(x):
    return jax.nn.gelu(x, approximate=True)

def _silu(x):
    return jax.nn.silu(x)

def _sigmoid(x):
    return jax.nn.sigmoid(x)

def _layernorm(x, axis=-1, eps=1e-05):
    m = jnp.mean(x, axis=axis, keepdims=True)
    v = jnp.var(x, axis=axis, keepdims=True)
    return (x - m) / jnp.sqrt(v + eps)

def _scatter_add(tgt, idx, src, axis=0):
    return tgt.at[idx].add(src)

def _segment_sum(src, seg, n):
    return jax.ops.segment_sum(src, seg, n)
kernel_name = 'mk_gnn_preln_d4_gnn_r8_a073ec'

def setup_inputs(seed: int=0):
    np.random.seed(seed)
    _w = jnp.asarray

    def _rec_inputs():
        import jax
        import jax.numpy as jnp
        _gk = jax.random.key(seed)
        x = -0.000202 + 1 * jax.random.normal(jax.random.fold_in(_gk, 1), (12500, 128), jnp.float32)
        src = jax.random.randint(jax.random.fold_in(_gk, 2), (200000,), 0, 12500, jnp.int32)
        dst = jax.random.randint(jax.random.fold_in(_gk, 3), (200000,), 0, 12500, jnp.int32)
        _o = jnp.argsort(dst, stable=True)
        src = src[_o]
        dst = dst[_o]
        edge_attr_128 = 9.41057e-06 + 1 * jax.random.normal(jax.random.fold_in(_gk, 12), (200000, 128), jnp.float32)
        edge_attr_13 = 0.000262222 + 1.00012 * jax.random.normal(jax.random.fold_in(_gk, 13), (200000, 13), jnp.float32)
        edge_attr_16 = 0.000254156 + 0.999948 * jax.random.normal(jax.random.fold_in(_gk, 14), (200000, 16), jnp.float32)
        edge_type_8 = jax.random.randint(jax.random.fold_in(_gk, 16), (200000,), 0, 8, jnp.int32)
        return (x, src, dst, edge_attr_128, edge_attr_13, edge_attr_16, edge_type_8)
    x, src, dst, edge_attr_128, edge_attr_13, edge_attr_16, edge_type_8 = _rec_inputs()

    def _L0_gnn_setup():
        import jax, jax.numpy as jnp
        import numpy as np
        N_NODES = 6250
        N_EDGES = 100000
        IN_C = 128
        OUT_C = 128
        EDGE_F = 16
        NEG_SLOPE = 0.2
        BN_EPS = 1e-05
        key = jax.random.key(seed)
        ks = jax.random.split(key, 8)
        x = jax.random.normal(ks[0], (N_NODES, IN_C), dtype=jnp.float32)
        edge_index = jax.random.randint(ks[1], (2, N_EDGES), 0, N_NODES, dtype=jnp.int64)
        edge_attr = jax.random.normal(ks[2], (N_EDGES, EDGE_F), dtype=jnp.float32)
        W = jax.random.normal(ks[3], (IN_C, OUT_C), dtype=jnp.float32) / np.sqrt(IN_C)
        att_src = jax.random.normal(ks[4], (OUT_C,), dtype=jnp.float32) / np.sqrt(OUT_C)
        att_dst = jax.random.normal(ks[5], (OUT_C,), dtype=jnp.float32) / np.sqrt(OUT_C)
        bias = jnp.zeros((OUT_C,), dtype=jnp.float32)
        gamma = jnp.ones((OUT_C,), dtype=jnp.float32)
        beta = jnp.zeros((OUT_C,), dtype=jnp.float32)
        return {'x': x, 'edge_index': edge_index, 'edge_attr': edge_attr, 'W': W, 'att_src': att_src, 'att_dst': att_dst, 'bias': bias, 'gamma': gamma, 'beta': beta}
    _L0_gnn_all = _L0_gnn_setup()
    _L0_gnn_in = {k: v for k, v in _L0_gnn_all.items() if k in ('W', 'att_src', 'att_dst', 'bias', 'gamma', 'beta')}
    del _L0_gnn_all

    def _L1_gnn_setup():
        import jax, jax.numpy as jnp
        import numpy as np
        N, E, IN, H, C, ED = (12500, 200000, 128, 4, 32, 13)
        NEG_SLOPE = 0.2
        LN_EPS = 1e-05
        key = jax.random.key(seed)
        ks = jax.random.split(key, 11)
        s = 0.05
        return {'x': jax.random.normal(ks[0], (N, IN), jnp.float32), 'edge_index': jax.random.randint(ks[1], (2, E), 0, N, jnp.int64), 'edge_attr': jax.random.normal(ks[2], (E, ED), jnp.float32), 'W': jax.random.normal(ks[3], (IN, H * C), jnp.float32) * s, 'att_src': jax.random.normal(ks[4], (H, C), jnp.float32) * s, 'att_dst': jax.random.normal(ks[5], (H, C), jnp.float32) * s, 'W_edge': jax.random.normal(ks[6], (ED, H * C), jnp.float32) * s, 'att_edge': jax.random.normal(ks[7], (H, C), jnp.float32) * s, 'bias': jax.random.normal(ks[8], (H * C,), jnp.float32) * s, 'ln_gamma': jnp.ones((H * C,), jnp.float32), 'ln_beta': jnp.zeros((H * C,), jnp.float32)}
    _L1_gnn_all = _L1_gnn_setup()
    _L1_gnn_in = {k: v for k, v in _L1_gnn_all.items() if k in ('W', 'att_src', 'att_dst', 'W_edge', 'att_edge', 'bias', 'ln_gamma', 'ln_beta')}
    del _L1_gnn_all

    def _L2_gnn_setup():
        import jax, jax.numpy as jnp
        import numpy as np
        N_NODES = 12500
        N_EDGES = 200000
        N_GRAPHS = 64
        D_X = 128
        D_E = 128
        D_U = 128
        HIDDEN = 128
        OUT = 128
        IN_SIZE = D_X + D_E + D_U
        key = jax.random.key(seed)
        ks = jax.random.split(key, 10)
        x = jax.random.normal(ks[0], (N_NODES, D_X), dtype=jnp.float32)
        edge_index = jax.random.randint(ks[1], (2, N_EDGES), 0, N_NODES, dtype=jnp.int64)
        edge_attr = jax.random.normal(ks[2], (N_EDGES, D_E), dtype=jnp.float32)
        u = jax.random.normal(ks[3], (N_GRAPHS, D_U), dtype=jnp.float32)
        batch = jnp.sort(jax.random.randint(ks[4], (N_NODES,), 0, N_GRAPHS, dtype=jnp.int64))
        W1 = jax.random.normal(ks[5], (IN_SIZE, HIDDEN), dtype=jnp.float32) * (1.0 / np.sqrt(IN_SIZE))
        b1 = jnp.zeros((HIDDEN,), dtype=jnp.float32)
        W2 = jax.random.normal(ks[6], (HIDDEN, HIDDEN), dtype=jnp.float32) * (1.0 / np.sqrt(HIDDEN))
        b2 = jnp.zeros((HIDDEN,), dtype=jnp.float32)
        W3 = jax.random.normal(ks[7], (HIDDEN, OUT), dtype=jnp.float32) * (1.0 / np.sqrt(HIDDEN))
        b3 = jnp.zeros((OUT,), dtype=jnp.float32)
        return {'x': x, 'edge_index': edge_index, 'edge_attr': edge_attr, 'u': u, 'batch': batch, 'W1': W1, 'b1': b1, 'W2': W2, 'b2': b2, 'W3': W3, 'b3': b3}
    _L2_gnn_all = _L2_gnn_setup()
    _L2_gnn_in = {k: v for k, v in _L2_gnn_all.items() if k in ('u', 'W1', 'b1', 'W2', 'b2', 'W3', 'b3')}
    del _L2_gnn_all

    def _L3_gnn_setup():
        import jax, jax.numpy as jnp
        import numpy as np
        N, E, D_IN, D_OUT, R = (6250, 100000, 128, 128, 8)
        key = jax.random.key(seed)
        ks = jax.random.split(key, 6)
        x = jax.random.normal(ks[0], (N, D_IN), dtype=jnp.float32)
        W_rel = jax.random.normal(ks[1], (R, D_IN, D_OUT), dtype=jnp.float32) * (1.0 / np.sqrt(D_IN))
        W_self_w = jax.random.normal(ks[2], (D_OUT, D_IN), dtype=jnp.float32) * (1.0 / np.sqrt(D_IN))
        W_self_b = jax.random.normal(ks[3], (D_OUT,), dtype=jnp.float32) * 0.01
        edge_index = jax.random.randint(ks[4], (2, E), 0, N, dtype=jnp.int32)
        edge_type = jax.random.randint(ks[5], (E,), 0, R, dtype=jnp.int32)
        return {'x': x, 'W_rel': W_rel, 'W_self_w': W_self_w, 'W_self_b': W_self_b, 'edge_index': edge_index, 'edge_type': edge_type}
    _L3_gnn_all = _L3_gnn_setup()
    _L3_gnn_in = {k: v for k, v in _L3_gnn_all.items() if k in ('W_rel', 'W_self_w', 'W_self_b')}
    del _L3_gnn_all
    return {'x': x, 'src': src, 'dst': dst, 'edge_attr_128': edge_attr_128, 'edge_attr_13': edge_attr_13, 'edge_attr_16': edge_attr_16, 'edge_type_8': edge_type_8, 'L0_gnn_W': _L0_gnn_in['W'], 'L0_gnn_att_src': _L0_gnn_in['att_src'], 'L0_gnn_att_dst': _L0_gnn_in['att_dst'], 'L0_gnn_bias': _L0_gnn_in['bias'], 'L0_gnn_gamma': _L0_gnn_in['gamma'], 'L0_gnn_beta': _L0_gnn_in['beta'], 'L1_gnn_W': _L1_gnn_in['W'], 'L1_gnn_att_src': _L1_gnn_in['att_src'], 'L1_gnn_att_dst': _L1_gnn_in['att_dst'], 'L1_gnn_W_edge': _L1_gnn_in['W_edge'], 'L1_gnn_att_edge': _L1_gnn_in['att_edge'], 'L1_gnn_bias': _L1_gnn_in['bias'], 'L1_gnn_ln_gamma': _L1_gnn_in['ln_gamma'], 'L1_gnn_ln_beta': _L1_gnn_in['ln_beta'], 'L2_gnn_u': _L2_gnn_in['u'], 'L2_gnn_W1': _L2_gnn_in['W1'], 'L2_gnn_b1': _L2_gnn_in['b1'], 'L2_gnn_W2': _L2_gnn_in['W2'], 'L2_gnn_b2': _L2_gnn_in['b2'], 'L2_gnn_W3': _L2_gnn_in['W3'], 'L2_gnn_b3': _L2_gnn_in['b3'], 'L3_gnn_W_rel': _L3_gnn_in['W_rel'], 'L3_gnn_W_self_w': _L3_gnn_in['W_self_w'], 'L3_gnn_W_self_b': _L3_gnn_in['W_self_b']}

def reference(x, src, dst, edge_attr_128, edge_attr_13, edge_attr_16, edge_type_8, L0_gnn_W, L0_gnn_att_src, L0_gnn_att_dst, L0_gnn_bias, L0_gnn_gamma, L0_gnn_beta, L1_gnn_W, L1_gnn_att_src, L1_gnn_att_dst, L1_gnn_W_edge, L1_gnn_att_edge, L1_gnn_bias, L1_gnn_ln_gamma, L1_gnn_ln_beta, L2_gnn_u, L2_gnn_W1, L2_gnn_b1, L2_gnn_W2, L2_gnn_b2, L2_gnn_W3, L2_gnn_b3, L3_gnn_W_rel, L3_gnn_W_self_w, L3_gnn_W_self_b):
    import jax
    import jax.numpy as jnp

    def _L0_gnn_ref(x, edge_index, edge_attr, W, att_src, att_dst, bias, gamma, beta):
        import jax, jax.numpy as jnp
        import numpy as np
        N_NODES = 6250
        N_EDGES = 100000
        IN_C = 128
        OUT_C = 128
        EDGE_F = 16
        NEG_SLOPE = 0.2
        BN_EPS = 1e-05
        N = x.shape[0]
        h = x @ W
        loops = jnp.broadcast_to(jnp.arange(N, dtype=edge_index.dtype)[None, :], (2, N))
        ei = jnp.concatenate([edge_index, loops], axis=1)
        src, dst = (ei[0], ei[1])
        a_src = h @ att_src
        a_dst = h @ att_dst
        e = jax.nn.leaky_relu(a_src[src] + a_dst[dst], NEG_SLOPE)
        m = jax.ops.segment_max(e, dst, num_segments=N)
        ex = jnp.exp(e - m[dst])
        denom = jax.ops.segment_sum(ex, dst, num_segments=N)
        alpha = ex / denom[dst]
        out = jax.ops.segment_sum(alpha[:, None] * h[src], dst, num_segments=N) + bias
        mean = jnp.mean(out, axis=0)
        var = jnp.mean((out - mean) ** 2, axis=0)
        y = (out - mean) * jax.lax.rsqrt(var + BN_EPS) * gamma + beta
        return jax.nn.relu(y)

    def _L1_gnn_ref(x, edge_index, edge_attr, W, att_src, att_dst, W_edge, att_edge, bias, ln_gamma, ln_beta):
        import jax, jax.numpy as jnp
        import numpy as np
        N, E, IN, H, C, ED = (12500, 200000, 128, 4, 32, 13)
        NEG_SLOPE = 0.2
        LN_EPS = 1e-05
        n = x.shape[0]
        src, dst = (edge_index[0], edge_index[1])
        cnt = jax.ops.segment_sum(jnp.ones_like(src, x.dtype), dst, num_segments=n)
        ea_loop = jax.ops.segment_sum(edge_attr, dst, num_segments=n) / jnp.maximum(cnt, 1.0)[:, None]
        loop = jnp.arange(n, dtype=src.dtype)
        src_a = jnp.concatenate([src, loop])
        dst_a = jnp.concatenate([dst, loop])
        ea = jnp.concatenate([edge_attr, ea_loop], 0)
        h = (x @ W).reshape(n, H, C)
        a_src = jnp.einsum('nhc,hc->nh', h, att_src)
        a_dst = jnp.einsum('nhc,hc->nh', h, att_dst)
        e = (ea @ W_edge).reshape(-1, H, C)
        a_edge = jnp.einsum('ehc,hc->eh', e, att_edge)
        alpha = a_src[src_a] + a_dst[dst_a] + a_edge
        alpha = jnp.where(alpha > 0, alpha, NEG_SLOPE * alpha)
        amax = jax.ops.segment_max(alpha, dst_a, num_segments=n)
        alpha = jnp.exp(alpha - amax[dst_a])
        denom = jax.ops.segment_sum(alpha, dst_a, num_segments=n)
        alpha = alpha / (denom[dst_a] + 1e-16)
        out = jax.ops.segment_sum(alpha[:, :, None] * h[src_a], dst_a, num_segments=n)
        out = out.reshape(n, H * C) + bias
        y = out + x
        mu = jnp.mean(y, axis=-1, keepdims=True)
        var = jnp.mean((y - mu) ** 2, axis=-1, keepdims=True)
        y = (y - mu) / jnp.sqrt(var + LN_EPS) * ln_gamma + ln_beta
        return jax.nn.relu(y)

    def _L2_gnn_ref(x, edge_index, edge_attr, u, batch, W1, b1, W2, b2, W3, b3):
        import jax, jax.numpy as jnp
        import numpy as np
        N_NODES = 12500
        N_EDGES = 200000
        N_GRAPHS = 64
        D_X = 128
        D_E = 128
        D_U = 128
        HIDDEN = 128
        OUT = 128
        IN_SIZE = D_X + D_E + D_U
        edge_dst = edge_index[1]
        agg = jax.ops.segment_sum(edge_attr, edge_dst, num_segments=x.shape[0])
        model_in = jnp.concatenate([x, agg, u[batch]], axis=1)
        h = jax.nn.relu(model_in @ W1 + b1)
        h = jax.nn.relu(h @ W2 + b2)
        return h @ W3 + b3

    def _L3_gnn_ref(x, W_rel, W_self_w, W_self_b, edge_index, edge_type):
        import jax, jax.numpy as jnp
        import numpy as np
        N, E, D_IN, D_OUT, R = (6250, 100000, 128, 128, 8)
        n = x.shape[0]
        out = x @ W_self_w.T + W_self_b
        src = edge_index[0]
        dst = edge_index[1]
        h = jnp.einsum('nd,rdo->rno', x, W_rel)
        msg = h[edge_type, src]
        agg = jax.ops.segment_sum(msg, dst, num_segments=n)
        deg = jax.ops.segment_sum(jnp.ones_like(dst, dtype=x.dtype), dst, num_segments=n)
        deg = jnp.maximum(deg, 1.0)[:, None]
        out = jax.nn.relu(out + agg / deg)
        return out
    edge_index = jnp.stack([src, dst])
    batch0 = jnp.zeros((12500,), jnp.int32)
    h = jnp.maximum(_layernorm(x, axis=-1), 0.0)
    x = x + _L0_gnn_ref(h, edge_index, edge_attr_16, L0_gnn_W, L0_gnn_att_src, L0_gnn_att_dst, L0_gnn_bias, L0_gnn_gamma, L0_gnn_beta)
    h = jnp.maximum(_layernorm(x, axis=-1), 0.0)
    x = x + _L1_gnn_ref(h, edge_index, edge_attr_13, L1_gnn_W, L1_gnn_att_src, L1_gnn_att_dst, L1_gnn_W_edge, L1_gnn_att_edge, L1_gnn_bias, L1_gnn_ln_gamma, L1_gnn_ln_beta)
    h = jnp.maximum(_layernorm(x, axis=-1), 0.0)
    x = x + _L2_gnn_ref(h, edge_index, edge_attr_128, L2_gnn_u, batch0, L2_gnn_W1, L2_gnn_b1, L2_gnn_W2, L2_gnn_b2, L2_gnn_W3, L2_gnn_b3)
    h = jnp.maximum(_layernorm(x, axis=-1), 0.0)
    x = x + _L3_gnn_ref(h, L3_gnn_W_rel, L3_gnn_W_self_w, L3_gnn_W_self_b, edge_index, edge_type_8)
    return x

_drawn_inputs = setup_inputs


def setup_inputs(seed=0):
    import zlib

    import numpy as np

    out = dict(_drawn_inputs(seed))
    spreads = {'L0_gnn_bias': (0.0, 2.0),
     'L0_gnn_gamma': (1.0, 0.2),
     'L0_gnn_beta': (0.0, 0.1),
     'L1_gnn_ln_gamma': (1.0, 0.2),
     'L1_gnn_ln_beta': (0.0, 0.349),
     'L2_gnn_b1': (0.0, 0.443),
     'L2_gnn_b2': (0.0, 0.296),
     'L2_gnn_b3': (0.0, 0.1)}
    factors = {'edge_attr_13': 8.0,
     'L1_gnn_att_src': 30.458,
     'L1_gnn_att_dst': 64.0,
     'L1_gnn_W_edge': 8.0,
     'L1_gnn_att_edge': 8.0,
     'L1_gnn_bias': 2.736,
     'L3_gnn_W_self_b': 8.0}
    for name, (base, spread) in spreads.items():
        noise = np.random.default_rng([zlib.crc32(name.encode()), seed]).standard_normal(out[name].shape)
        drawn = base * np.exp(spread * noise) if base else spread * noise
        out[name] = jnp.asarray(drawn.astype(out[name].dtype))
    for name, factor in factors.items():
        out[name] = (out[name] * factor).astype(out[name].dtype)
    return out
```

```python
from contextlib import ExitStack
import math

import numpy as np
import concourse.bass as bass
from concourse import mybir

F32 = mybir.dt.float32
I32 = mybir.dt.int32
ALU = mybir.AluOpType
ACT = mybir.ActivationFunctionType
AX = mybir.AxisListType.X

P = 128
D = 128
GC = 16
BIG = 1.0e30
EPS = 1e-5
SLOPE = 0.2


def padded_sizes(n_nodes, n_edges):
    nj = -(-n_nodes // P)
    ec = -(-n_edges // (P * GC)) * GC
    return nj, ec


def chunk_len(ep):
    return min((d for d in range(1, ep + 1) if ep % d == 0), key=lambda d: abs(d - math.sqrt(ep)))


class Flow:
    ENGINES = ("sync", "scalar", "gpsimd", "vector", "tensor")

    def __init__(self, nc, ctx):
        self.nc, self.ctx = nc, ctx
        self.queue = {e: [] for e in self.ENGINES}
        self.dma_sems = []
        self.n = 0
        self.stage_name = ""
        self.begin("start")

    def begin(self, name):
        self.done = {e: [None, 0] for e in self.ENGINES}
        self.dma_sems = []
        self.stage_name = name

    def sem(self, name):
        self.n += 1
        return self.ctx.enter_context(self.nc.semaphore(f"{self.stage_name}_{name}_{self.n}"))

    def op(self, engine, fn, *waits):
        d = self.done[engine]
        if d[0] is None:
            d[0] = self.sem(engine)
        d[1] += 1
        self.queue[engine].append((waits, fn, d[0], 1))
        return (d[0], d[1])

    def last(self, engine):
        d = self.done[engine]
        return tuple(d) if d[1] else None

    def dma_sem(self, name):
        s = [self.sem(name), 0]
        self.dma_sems.append(s)
        return s

    def dma(self, engine, fn, s, *waits):
        s[1] += 16
        self.queue[engine].append((waits, fn, s[0], 16))
        return (s[0], s[1])

    def barrier(self, name):
        tokens = [tuple(d) for d in self.done.values() if d[1]] + [tuple(s) for s in self.dma_sems if s[1]]
        for e in self.ENGINES:
            self.queue[e].append((tokens, None, None, 0))
        self.begin(name)

    def play(self, name, engine):
        seen = {}
        for waits, fn, s, by in self.queue[name]:
            for w in waits:
                if w is not None and seen.get(w[0].name, 0) < w[1]:
                    engine.wait_ge(w[0], w[1])
                    seen[w[0].name] = w[1]
            if fn is not None:
                fn(engine).then_inc(s, by)


def past(tokens, what, k):
    return tokens[what, k] if k >= 0 else None


def skewed(stages, n):
    for step in range(n + len(stages) - 1):
        for s in reversed(range(len(stages))):
            if 0 <= step - s < n:
                stages[s](step - s)


def build(nc, io, n_nodes, n_edges):
    NJ, EC = padded_sizes(n_nodes, n_edges)
    NP, EP = P * NJ, P * EC
    NG = EC // GC
    CH = chunk_len(EP)
    NCH = EP // CH
    JB = max(d for d in range(1, 8) if NJ % d == 0)
    NK = NJ // JB
    NREL = io["W_rel"].shape[0]
    EF = io["ea13"].shape[-1]

    def dram(name, shape, dt=F32):
        return nc.dram_tensor(name, list(shape), dt).ap()

    class Layer:
        def __init__(self, name, heads, edge_terms):
            self.H, self.C = heads, D // heads
            self.NW = heads * (self.C + 1)
            self.M0 = self.NW
            self.A0 = self.NW + heads
            self.AE = heads if edge_terms else 0
            self.W = self.A0 + self.AE
            self.WN = self.NW + self.AE
            self.table = dram(f"table_{name}", [NP, self.W])
            self.sums = dram(f"sums_{name}", [EP + P, self.W])
            self.dst_logit = dram(f"dst_logit_{name}", [EP + NP, heads])
            self.node_logit = dram(f"node_logit_{name}", [NP, heads])

    A = Layer("a", 1, False)
    B = Layer("b", io["b_att_src"].shape[0], True)
    sums_attr = dram("sums_attr", [EP + P, D])
    table_rel = dram("table_rel", [NP * NREL, D])
    sums_rel = dram("sums_rel", [EP + P, D])
    dst_float = dram("dst_float", [NCH, CH])

    with ExitStack() as ctx:
        flow = Flow(nc, ctx)
        op, dma = flow.op, flow.dma

        def V(fn, *w):
            return op("vector", fn, *w, flow.last("vector"))

        def S(fn, *w): return op("scalar", fn, *w)
        def T(fn, *w): return op("tensor", fn, *w)

        def buffers(where):
            def sb(name, shape, dt=F32):
                flow.n += 1
                return where.enter_context(nc.sbuf_tensor(f"{name}_{flow.n}", list(shape), dt))
            return sb

        sb = sb_kept = buffers(ctx)
        ps = ctx.enter_context(nc.psum_tensor("ps", [P, 8, 512], F32))

        x = sb("x", [P, NJ, D])
        ident = sb("ident", [P, P])
        ones = sb("ones", [P, P])
        src = sb("src_i", [P, EC], I32)
        rel_row = sb("rel_row", [P, EC], I32)
        dst_first = sb("dst_first", [P, 1], I32)
        keep = sb("keep", [P, EC])
        cut = sb("cut", [P, EC])
        keep_all = sb("keep_all", [P, 1])
        cut_all = sb("cut_all", [P, 1])
        head_row = sb("head_row", [P, 1], I32)
        sum_row = sb("sum_row", [P, NJ], I32)
        start_row = sb("start_row", [P, NJ], I32)
        has = sb("has", [P, NJ])
        no_edge = sb("no_edge", [P, NJ])
        inv_deg = sb("inv_deg", [P, NJ])
        mean_rs = sb("mean_rs", [P, NJ])
        mean_nb = sb("mean_nb", [P, NJ])
        stats = sb("stats", [P, 2, JB, 6])
        mv = sb("mv", [P, 2, JB, 2])
        std = sb("std", [P, 2, JB])

        def bc(ap, shape):
            return ap.broadcast_to(shape)

        flow.begin("graph")
        with ExitStack() as local:
            sb = buffers(local)
            dst = sb("dst_i", [P, EC], I32)
            typ = sb("typ_i", [P, EC], I32)
            dst_f = sb("dst_f", [P, EC])
            last_i = sb("last_i", [P, NCH], I32)
            last_f = sb("last_f", [P, NCH])
            zero = sb("zero", [P, EC])
            tmp_e = sb("tmp_e", [P, EC])
            prev_i = sb("prev_i", [P, 1], I32)
            prev_f = sb("prev_f", [P, 1])
            iot = sb("iot", [P, NJ + 1], I32)
            v = sb("v", [P, NJ + 1])
            col_i = sb("col_i", [P, P], I32)
            row_i = sb("row_i", [P, P], I32)
            row_f = sb("row_f", [P, P])
            own_i = sb("own_i", [P, 1], I32)
            own_f = sb("own_f", [P, 1])
            junk = sb("junk", [P, 2, max(NCH, CH)])
            q = sb("q", [P, NJ + 1])
            q_i = sb("q_i", [P, NJ + 1], I32)
            cnt = sb("cnt", [P, NJ + 1])
            NPIECE = 8
            piece = sb("piece", [P, NPIECE, CH])
            big = sb("big", [P, NJ, P])
            s1 = sb("s1", [P, NJ])
            s2 = sb("s2", [P, NJ])
            s3 = sb("s3", [P, NJ])
            s4 = sb("s4", [P, NJ])
            hc = sb("hc", [P, 1])

            sem_dst = flow.dma_sem("dst")
            sem_last = flow.dma_sem("last")
            sem_x = flow.dma_sem("x")
            sem_idx = flow.dma_sem("idx")
            sem_prev = flow.dma_sem("prev")
            sem_zero = flow.dma_sem("zero")
            sem_dstf = flow.dma_sem("dstf")
            t_dst = dma("sync", lambda e: e.dma_start(dst[:, :], io["dst"]), sem_dst)
            t_last = dma("scalar", lambda e: e.dma_start(
                last_i[:, :], io["dst_last"][0:1, :].broadcast_to([P, NCH])), sem_last)
            t_idx = dma("sync", lambda e: e.dma_start(src[:, :], io["src"]), sem_idx)
            t_idx = dma("scalar", lambda e: e.dma_start(typ[:, :], io["edge_type"]), sem_idx)
            dma("sync", lambda e: e.dma_start(x[:, :, :], io["x"]), sem_x)
            t_prev = dma("scalar", lambda e: e.dma_start(prev_i[:, :], io["dst_prev"]), sem_prev)
            t_z = V(lambda e: e.memset(zero[:, :], 0.0))
            for L in (A, B):
                flat = L.dst_logit[0:EP, :].rearrange("(p c) h -> p (c h)", c=EC)
                for k in range(L.H):
                    dma("scalar", lambda e, o=flat[:, k * EC:(k + 1) * EC]: e.dma_start(o, zero[:, :]),
                        sem_zero, t_z)
            t_f = V(lambda e: e.tensor_copy(dst_f[:, :], dst[:, :]), t_dst)
            t_store = dma("sync", lambda e: e.dma_start(
                dst_float.rearrange("a b -> (a b)").rearrange("(p c) -> p c", c=EC), dst_f[:, :]),
                sem_dstf, t_f)
            t_i = op("gpsimd", lambda e: e.iota(iot[:, :], [[1, NJ + 1]], base=-1, channel_multiplier=NJ))
            t_i2 = op("gpsimd", lambda e: e.iota(col_i[:, :], [[1, P]], base=0, channel_multiplier=-1))
            t_i3 = op("gpsimd", lambda e: e.iota(row_i[:, :], [[EC, P]], base=0, channel_multiplier=0))
            t_i4 = op("gpsimd", lambda e: e.iota(own_i[:, :], [[0, 1]], base=0, channel_multiplier=EC))
            V(lambda e: e.tensor_scalar(ident[:, :], col_i[:, :], 0.0, None, ALU.is_equal), t_i2)
            V(lambda e: e.memset(ones[:, :], 1.0))
            V(lambda e: e.tensor_copy(row_f[:, :], row_i[:, :]), t_i3)
            t_own = V(lambda e: e.tensor_copy(own_f[:, :], own_i[:, :]), t_i4)
            t_v = V(lambda e: e.tensor_copy(v[:, :], iot[:, :]), t_i)
            t_lf = V(lambda e: e.tensor_copy(last_f[:, :], last_i[:, :]), t_last)
            for j in range(NJ + 1):
                t = V(lambda e, j=j: e.tensor_scalar(
                    junk[:, j % 2, 0:NCH], last_f[:, :], v[:, j:j + 1], None, ALU.is_le, ALU.add,
                    accum_out=q[:, j:j + 1]), t_v, t_lf)
            t = V(lambda e: e.tensor_scalar(q[:, :], q[:, :], float(NCH - 1), None, ALU.min), t)
            t_q = V(lambda e: e.tensor_copy(q_i[:, :], q[:, :]), t)
            sem_piece = [flow.dma_sem(f"piece{k}") for k in range(NPIECE)]
            used = {}
            for j in range(NJ + 1):
                t = dma("gpsimd", lambda e, j=j: e.indirect_dma_start(
                    out=piece[:, j % NPIECE, :], out_offset=None, in_=dst_float,
                    in_offset=bass.IndirectOffsetOnAxis(ap=q_i[:, j:j + 1], axis=0)),
                    sem_piece[j % NPIECE], t_q, t_store, used[j - NPIECE] if j >= NPIECE else None)
                used[j] = V(lambda e, j=j: e.tensor_scalar(
                    junk[:, j % 2, 0:CH], piece[:, j % NPIECE, :], v[:, j:j + 1], None, ALU.is_le,
                    ALU.add, accum_out=cnt[:, j:j + 1]), t)
            t = V(lambda e: e.scalar_tensor_tensor(cnt[:, :], q[:, :], float(CH), cnt[:, :], ALU.mult,
                                                   ALU.add), used[NJ])
            start, end = cnt[:, 0:NJ], cnt[:, 1:NJ + 1]
            t_has = V(lambda e: e.tensor_tensor(has[:, :], end, start, ALU.is_gt), t)
            t_deg = V(lambda e: e.tensor_tensor(s4[:, :], end, start, ALU.subtract), t)
            t_l = V(lambda e: e.tensor_scalar(s1[:, :], end, -1.0, 0.0, ALU.add, ALU.max), t)
            V(lambda e: e.tensor_scalar(no_edge[:, :], has[:, :], BIG, -BIG, ALU.mult, ALU.add), t_has)
            t_deg = V(lambda e: e.tensor_scalar(s4[:, :], s4[:, :], 1.0, None, ALU.max), t_deg)
            t_deg = V(lambda e: e.reciprocal(s4[:, :], s4[:, :]), t_deg)
            V(lambda e: e.tensor_tensor(inv_deg[:, :], s4[:, :], has[:, :], ALU.mult), t_deg)
            t = V(lambda e: e.tensor_tensor(
                big[:, :, :], bc(s1[:, :].unsqueeze(2), [P, NJ, P]),
                bc(row_f[:, :].unsqueeze(1), [P, NJ, P]), ALU.is_ge), t_l)
            t_p1 = V(lambda e: e.tensor_reduce(s2[:, :], big[:, :, :], AX, ALU.add), t)
            t = V(lambda e: e.tensor_scalar(s3[:, :], s2[:, :], float(EC), float(-EC), ALU.mult, ALU.add), t_p1)
            t = V(lambda e: e.tensor_tensor(s3[:, :], start, s3[:, :], ALU.is_lt), t)
            t = V(lambda e: e.tensor_tensor(s3[:, :], s3[:, :], has[:, :], ALU.mult), t)
            t2 = V(lambda e: e.scalar_tensor_tensor(s2[:, :], s2[:, :], float(EP - 1), s1[:, :], ALU.add,
                                                    ALU.subtract), t)
            t = V(lambda e: e.tensor_tensor(s2[:, :], s2[:, :], s3[:, :], ALU.mult), t2)
            t = V(lambda e: e.tensor_tensor(s2[:, :], s2[:, :], s1[:, :], ALU.add), t)
            t = V(lambda e: e.tensor_copy(sum_row[:, :], s2[:, :]), t)
            t_n = V(lambda e: e.tensor_scalar(s1[:, :], v[:, 0:NJ], float(EP + 1), None, ALU.add), t)
            t = V(lambda e: e.tensor_tensor(s2[:, :], start, s1[:, :], ALU.subtract), t_n)
            t = V(lambda e: e.tensor_tensor(s2[:, :], s2[:, :], has[:, :], ALU.mult), t)
            t = V(lambda e: e.tensor_tensor(s2[:, :], s2[:, :], s1[:, :], ALU.add), t)
            V(lambda e: e.tensor_copy(start_row[:, :], s2[:, :]), t)
            V(lambda e: e.memset(keep[:, 0:1], 0.0))
            t = V(lambda e: e.tensor_tensor(keep[:, 1:EC], dst_f[:, 1:EC], dst_f[:, 0:EC - 1], ALU.is_equal),
                  t_f)
            V(lambda e: e.tensor_scalar(cut[:, :], keep[:, :], BIG, -BIG, ALU.mult, ALU.add), t)
            t = V(lambda e: e.tensor_copy(prev_f[:, :], prev_i[:, :]), t_prev)
            t = V(lambda e: e.tensor_tensor(keep_all[:, :], prev_f[:, :], dst_f[:, EC - 1:EC], ALU.is_equal), t)
            V(lambda e: e.tensor_scalar(cut_all[:, :], keep_all[:, :], BIG, -BIG, ALU.mult, ALU.add), t)
            t = V(lambda e: e.tensor_scalar(tmp_e[:, :], dst_f[:, :], dst_f[:, 0:1], None, ALU.is_equal,
                                            ALU.add, accum_out=hc[:, :]), t_f)
            t = V(lambda e: e.scalar_tensor_tensor(hc[:, :], hc[:, :], -1.0, own_f[:, :], ALU.add, ALU.add),
                  t, t_own)
            V(lambda e: e.tensor_copy(head_row[:, :], hc[:, :]), t)
            V(lambda e: e.tensor_copy(dst_first[:, :], dst[:, 0:1]))
            t = V(lambda e: e.tensor_copy(tmp_e[:, :], src[:, :]), t_idx)
            t2 = V(lambda e: e.tensor_copy(zero[:, :], typ[:, :]), (sem_zero[0], sem_zero[1]))
            t = V(lambda e: e.scalar_tensor_tensor(tmp_e[:, :], tmp_e[:, :], float(NREL), zero[:, :],
                                                   ALU.mult, ALU.add), t, t2)
            V(lambda e: e.tensor_copy(rel_row[:, :], tmp_e[:, :]), t)
            flow.barrier("table_a")

        def layer_norm_stats(k, data, rs, nb, *w):
            s = k % 2
            for b in range(JB):
                t = V(lambda e, b=b: e.bn_stats(stats[:, s, b, :], data[:, b, :]), *w)
            for b in range(JB):
                t = V(lambda e, b=b: e.bn_aggr(mv[:, s, b, :], stats[:, s, b, :]), t)
            t = V(lambda e: e.tensor_scalar(std[:, s, :], mv[:, s, :, 1], EPS, None, ALU.add), t)
            t = S(lambda e: e.activation(std[:, s, :], std[:, s, :], ACT.Sqrt), t)
            t = V(lambda e: e.reciprocal(rs, std[:, s, :]), t)
            return V(lambda e: e.scalar_tensor_tensor(nb, mv[:, s, :, 0], -1.0, rs, ALU.mult, ALU.mult), t)

        def norm_relu(k, out, data, rs, nb, *w):
            for b in range(JB):
                t = S(lambda e, b=b: e.activation(out[:, b, :], data[:, b, :], ACT.Relu,
                                                  bias=nb[:, b:b + 1], scale=rs[:, b:b + 1]), *w)
            return t

        def transposed(out, banks, data, *w):
            for b in range(JB):
                t = T(lambda e, b=b: e.transpose(ps[:, banks + b // 4, (b % 4) * P:(b % 4 + 1) * P],
                                                 data[:, b, :], ident[:, :]), *w)
            for i in range(0, JB, 4):
                n = min(4, JB - i)
                tt = V(lambda e, i=i, n=n: e.tensor_copy(out[:, i * P:(i + n) * P],
                                                         ps[:, banks + i // 4, 0:n * P]), t)
            return tt

        def load_extended_weights(L, sb, w_dram, att_src, att_dst):
            w = sb("w_plain", [P, L.H, L.C])
            att = sb("att", [P, 2, L.H, L.C])
            prod = sb("w_att", [P, L.H, L.C])
            ext = sb("w_ext", [P, L.W + L.H])
            sem_w = flow.dma_sem("w")
            dma("sync", lambda e: e.dma_start(w[:, :, :], w_dram.rearrange("k (h c) -> k h c", h=L.H)), sem_w)
            dma("sync", lambda e: e.dma_start(att[:, 0, :, :].rearrange("p h c -> p (h c)"),
                                              att_src.broadcast_to([P, D])), sem_w)
            t_w = dma("sync", lambda e: e.dma_start(att[:, 1, :, :].rearrange("p h c -> p (h c)"),
                                                    att_dst.broadcast_to([P, D])), sem_w)
            t = V(lambda e: e.memset(ext[:, :], 0.0))
            last = V(lambda e: e.tensor_copy(
                ext[:, 0:L.NW].rearrange("p (h c) -> p h c", h=L.H)[:, :, 0:L.C], w[:, :, :]), t, t_w)
            for i, at in ((0, L.M0), (1, L.W)):
                t = V(lambda e, i=i: e.tensor_tensor(prod[:, :, :], w[:, :, :], att[:, i, :, :], ALU.mult),
                      t_w, last)
                last = V(lambda e, at=at: e.tensor_reduce(ext[:, at:at + L.H], prod[:, :, :], AX, ALU.add), t)
            return ext, last

        def table_stages(L, sb, ext, t_ext, node_l, first):
            hn = sb("hn", [P, 2, JB, D])
            hT = sb("hT", [P, 2, JB * P])
            rows = sb("rows", [P, 2, JB, L.W])
            sem_rows = [flow.dma_sem(f"rows{i}") for i in range(2)]
            tok = {}
            WX = L.W + L.H

            def stats_of(k):
                j = slice(k * JB, (k + 1) * JB)
                tok["n", k] = layer_norm_stats(k, x[:, j, :], mean_rs[:, j], mean_nb[:, j], first(k))

            def norm(k):
                j = slice(k * JB, (k + 1) * JB)
                tok["h", k] = norm_relu(k, hn[:, k % 2, :, :], x[:, j, :], mean_rs[:, j], mean_nb[:, j],
                                        tok["n", k], past(tok, "T", k - 2))

            def turn(k):
                tok["T", k] = transposed(hT[:, k % 2, :], 0, hn[:, k % 2, :, :], tok["h", k],
                                         past(tok, "T", k - 1), past(tok, "P", k - 2))

            def project(k):
                for b in range(JB):
                    t = T(lambda e, b=b: e.matmul(
                        ps[:, 2 + b // 3, (b % 3) * WX:(b % 3 + 1) * WX],
                        hT[:, k % 2, b * P:(b + 1) * P], ext[:, :], start=True, stop=True),
                        tok["T", k], t_ext, past(tok, "C", k - 1))
                tok["P", k] = t
                for i in range(0, JB, 3):
                    n = min(3, JB - i)
                    src_ps = ps[:, 2 + i // 3, 0:n * WX].rearrange("p (n w) -> p n w", w=WX)
                    tok["C", k] = S(lambda e, i=i, n=n, v=src_ps: e.activation(
                        rows[:, k % 2, i:i + n, :], v[:, :, 0:L.W], ACT.Copy), t, past(tok, "D", k - 2))
                    tok["C", k] = S(lambda e, i=i, n=n, v=src_ps: e.activation(
                        node_l[:, k * JB + i:k * JB + i + n, :], v[:, :, L.W:WX], ACT.Copy))

            def store(k):
                one = rows[:, k % 2, :, 0:L.NW].rearrange("p j (h c) -> p j h c", h=L.H)[:, :, :, L.C]
                t = V(lambda e: e.memset(one, 1.0), tok["C", k])
                tok["D", k] = dma("sync", lambda e: e.dma_start(
                    L.table.rearrange("(p j) w -> p j w", j=NJ)[:, k * JB:(k + 1) * JB, :],
                    rows[:, k % 2, :, :]), sem_rows[k % 2], t)

            return [stats_of, norm, turn, project, store]

        def expand_dst_logits(L, node_l, dst_l):
            sem_nl = flow.dma_sem("node_logit")
            sem_sc = flow.dma_sem("scatter")
            sem_ld = flow.dma_sem("dst_logit")
            sem_first = flow.dma_sem("first")
            t_nl = dma("sync", lambda e: e.dma_start(
                L.node_logit.rearrange("(p j) h -> p j h", j=NJ), node_l[:, :, :]), sem_nl)
            for j in range(NJ):
                t = dma("gpsimd", lambda e, j=j: e.indirect_dma_start(
                    out=L.dst_logit, out_offset=bass.IndirectOffsetOnAxis(ap=start_row[:, j:j + 1], axis=0),
                    in_=node_l[:, j, :], in_offset=None), sem_sc)
            t = dma("sync", lambda e: e.dma_start(
                dst_l[:, :, :], L.dst_logit[0:EP, :].rearrange("(p c) h -> p c h", c=EC)), sem_ld, t)
            t = dma("gpsimd", lambda e: e.indirect_dma_start(
                out=dst_l[:, 0, :], out_offset=None, in_=L.node_logit,
                in_offset=bass.IndirectOffsetOnAxis(ap=dst_first[:, 0:1], axis=0)), sem_first, t, t_nl)
            for h in range(L.H):
                V(lambda e, h=h: e.tensor_tensor_scan(dst_l[:, :, h], keep[:, :], dst_l[:, :, h], 0.0,
                                                      ALU.mult, ALU.add), t)

        def groups_of(ap):
            return ap[0:EP, :].rearrange("(p c) w -> p c w", c=EC)

        def finish_crossing(name, sb, sums, W, tail, t_stored, L=None):
            WN = L.WN if L else D
            rest = WN - P
            head = sb(f"{name}_head", [P, W])
            xs = sb(f"{name}_state", [P, WN])
            ys = sb(f"{name}_decay", [P, WN])
            xT = sb(f"{name}_stateT", [P, 2, P])
            yT = sb(f"{name}_decayT", [P, 2, P])
            cT = sb(f"{name}_carryT", [P, 2, P + 1])
            sem_head = flow.dma_sem(f"{name}_head")
            sem_row = flow.dma_sem(f"{name}_row")
            t_head = dma("gpsimd", lambda e: e.indirect_dma_start(
                out=head[:, :], out_offset=None, in_=sums[0:EP, :],
                in_offset=bass.IndirectOffsetOnAxis(ap=head_row[:, 0:1], axis=0)), sem_head, *t_stored)
            t0 = V(lambda e: e.memset(cT[:, :, 0:1], 0.0))
            if L:
                H = L.H
                mrow = sb(f"{name}_mrow", [H, 2 * P])
                run = sb(f"{name}_run", [H, P + 1])
                mcut = sb(f"{name}_mcut", [P, H])
                m = sb(f"{name}_m", [P, 2 * H])
                ex = sb(f"{name}_ex", [P, 2 * H])
                mx = sb(f"{name}_mx", [P, H])
                tm = tail[:, L.M0:L.M0 + H]
                t = V(lambda e: e.tensor_copy(mcut[:, :], bc(cut_all[:, :], [P, H])))
                t = T(lambda e: e.transpose(ps[0:H, 0, P:2 * P], mcut[:, :], ident[:, :]), t)
                t = T(lambda e: e.transpose(ps[0:H, 0, 0:P], tm, ident[:, :]))
                t = V(lambda e: e.tensor_copy(mrow[:, :], ps[0:H, 0, 0:2 * P]), t)
                t1 = V(lambda e: e.memset(run[:, 0:1], -BIG))
                t = V(lambda e: e.tensor_tensor_scan(run[:, 1:P + 1], mrow[:, P:2 * P], mrow[:, 0:P], -BIG,
                                                     ALU.add, ALU.max), t, t1)
                T(lambda e: e.transpose(ps[:, 1, 0:H], run[:, 1:P + 1], ident[0:H, 0:H]), t)
                t = T(lambda e: e.transpose(ps[:, 1, H:2 * H], run[:, 0:P], ident[0:H, 0:H]), t)
                t = V(lambda e: e.tensor_copy(m[:, :], ps[:, 1, 0:2 * H]), t)
                V(lambda e: e.tensor_tensor(ex[:, 0:H], tm, m[:, 0:H], ALU.subtract), t)
                t = V(lambda e: e.tensor_tensor(ex[:, H:2 * H], m[:, H:2 * H], m[:, 0:H], ALU.subtract), t)
                t = V(lambda e: e.tensor_tensor(ex[:, H:2 * H], ex[:, H:2 * H], mcut[:, :], ALU.add), t)
                t = S(lambda e: e.activation(ex[:, :], ex[:, :], ACT.Exp), t)

                def heads(ap):
                    return ap.rearrange("p (h c) -> p h c", h=H)
                wide = [P, H, L.C + 1]
                V(lambda e: e.tensor_tensor(heads(xs[:, 0:L.NW]), heads(tail[:, 0:L.NW]),
                                            bc(ex[:, 0:H].unsqueeze(2), wide), ALU.mult), t)
                t = V(lambda e: e.tensor_copy(heads(ys[:, 0:L.NW]), bc(ex[:, H:2 * H].unsqueeze(2), wide)))
                if L.AE:
                    V(lambda e: e.tensor_copy(xs[:, L.NW:WN], tail[:, L.A0:L.W]))
                    t = V(lambda e: e.tensor_copy(ys[:, L.NW:WN], bc(keep_all[:, :], [P, L.AE])))
            else:
                V(lambda e: e.tensor_copy(xs[:, :], tail))
                t = V(lambda e: e.tensor_copy(ys[:, :], bc(keep_all[:, :], [P, D])))
            parts = [(0, 0, P)] + ([(1, P, rest)] if rest else [])
            for i, a, n in parts:
                T(lambda e, i=i, a=a, n=n: e.transpose(ps[0:n, 2, i * P:(i + 1) * P], xs[:, a:a + n],
                                                       ident[:, :]), t)
                t2 = T(lambda e, i=i, a=a, n=n: e.transpose(ps[0:n, 3, i * P:(i + 1) * P], ys[:, a:a + n],
                                                            ident[:, :]), t)
            for i, a, n in parts:
                V(lambda e, i=i, n=n: e.tensor_copy(xT[0:n, i, :], ps[0:n, 2, i * P:(i + 1) * P]), t2)
                t3 = V(lambda e, i=i, n=n: e.tensor_copy(yT[0:n, i, :], ps[0:n, 3, i * P:(i + 1) * P]), t2)
            for i, a, n in parts:
                t4 = V(lambda e, i=i, n=n: e.tensor_tensor_scan(cT[0:n, i, 1:P + 1], yT[0:n, i, :],
                                                                xT[0:n, i, :], 0.0, ALU.mult, ALU.add), t3)
            for i, a, n in parts:
                t5 = T(lambda e, i=i, a=a, n=n: e.transpose(ps[:, 4, a:a + n], cT[0:n, i, 0:P],
                                                            ident[0:n, 0:n]), t4, t0)
            if L:
                t = V(lambda e: e.tensor_tensor(mx[:, :], head[:, L.M0:L.M0 + H], m[:, H:2 * H], ALU.max),
                      t_head, t5)
                V(lambda e: e.tensor_tensor(ex[:, 0:H], head[:, L.M0:L.M0 + H], mx[:, :], ALU.subtract), t)
                t = V(lambda e: e.tensor_tensor(ex[:, H:2 * H], m[:, H:2 * H], mx[:, :], ALU.subtract), t)
                t = S(lambda e: e.activation(ex[:, :], ex[:, :], ACT.Exp), t)
                t1 = V(lambda e: e.tensor_tensor(heads(head[:, 0:L.NW]), heads(head[:, 0:L.NW]),
                                                 bc(ex[:, 0:H].unsqueeze(2), wide), ALU.mult), t)
                t2 = V(lambda e: e.tensor_tensor(heads(xs[:, 0:L.NW]), heads(ps[:, 4, 0:L.NW]),
                                                 bc(ex[:, H:2 * H].unsqueeze(2), wide), ALU.mult), t)
                t3 = V(lambda e: e.tensor_tensor(head[:, 0:L.NW], head[:, 0:L.NW], xs[:, 0:L.NW], ALU.add), t2)
                if L.AE:
                    V(lambda e: e.tensor_tensor(head[:, L.A0:L.W], head[:, L.A0:L.W], ps[:, 4, L.NW:WN],
                                                ALU.add))
                t3 = V(lambda e: e.tensor_copy(head[:, L.M0:L.M0 + H], mx[:, :]))
            else:
                t3 = V(lambda e: e.tensor_tensor(head[:, :], head[:, :], ps[:, 4, 0:D], ALU.add), t_head, t5)
            dma("sync", lambda e: e.dma_start(sums[EP:EP + P, :], head[:, :]), sem_row, t3)

        def attention_edges(L, sb, dst_l, attr=None, edge_terms=None):
            H, C, NW = L.H, L.C, L.NW
            NS = 4
            rows = sb("edge_rows", [P, NS, GC, L.W])
            z = sb("z", [P, 2, GC, H])
            run = sb("run_max", [P, 2, GC + 1, H])
            wd = sb("weight_decay", [P, 2, 2 * GC, H])
            old = sb("old", [P, 2, H, C + 1])
            sem_g = [flow.dma_sem(f"gather{i}") for i in range(NS)]
            sem_s = [flow.dma_sem(f"store{i}") for i in range(NS)]
            tok = {}
            stored = []
            if attr is not None:
                NA = 4
                attrs = sb("attrs", [P, NA, GC, D])
                sem_al = [flow.dma_sem(f"attr_load{i}") for i in range(NA)]
                sem_as = [flow.dma_sem(f"attr_store{i}") for i in range(NA)]
            if edge_terms is not None:
                feat_dram, proj, t_proj = edge_terms
                feats = sb("feats", [P, 2, GC, EF])
                prod = sb("feat_prod", [P, GC, H, EF])
                ae = sb("edge_logit", [P, 2, GC, H])
                sem_f = [flow.dma_sem(f"feats{i}") for i in range(2)]

            def cols(g):
                return slice(g * GC, (g + 1) * GC)

            def fetch(g):
                s = g % NS
                for c in range(GC):
                    tok["G", g] = dma("gpsimd", lambda e, c=c: e.indirect_dma_start(
                        out=rows[:, s, c, :], out_offset=None, in_=L.table,
                        in_offset=bass.IndirectOffsetOnAxis(ap=src[:, g * GC + c:g * GC + c + 1], axis=0)),
                        sem_g[s], past(tok, "S", g - NS), past(tok, "main", g - NS + 1))

            def fetch_extra(g):
                if attr is not None:
                    tok["AL", g] = dma("sync", lambda e: e.dma_start(
                        attrs[:, g % NA, :, :], attr[:, cols(g), :]), sem_al[g % NA],
                        past(tok, "AS", g - NA), past(tok, "attr", g - NA + 1))
                if edge_terms is not None:
                    tok["F", g] = dma("sync", lambda e: e.dma_start(
                        feats[:, g % 2, :, :], feat_dram[:, cols(g), :]), sem_f[g % 2], past(tok, "ae", g - 2))

            def logits(g):
                s, b = g % NS, g % 2
                R = rows[:, s, :, :]
                if edge_terms is not None:
                    t = V(lambda e: e.tensor_tensor(
                        prod[:, :, :, :], bc(feats[:, b, :, :].unsqueeze(2), [P, GC, H, EF]),
                        bc(proj[:, :, :].unsqueeze(1), [P, GC, H, EF]), ALU.mult), tok["F", g], t_proj)
                    t_ae = V(lambda e: e.tensor_reduce(ae[:, b, :, :], prod[:, :, :, :], AX, ALU.add), t)
                    tok["ae", g] = t_ae
                t = V(lambda e: e.tensor_tensor(z[:, b, :, :], R[:, :, L.M0:L.M0 + H], dst_l[:, cols(g), :],
                                                ALU.add), tok["G", g])
                if edge_terms is not None:
                    t = V(lambda e: e.tensor_tensor(z[:, b, :, :], z[:, b, :, :], ae[:, b, :, :], ALU.add), t)
                t = V(lambda e: e.scalar_tensor_tensor(z[:, b, :, :], z[:, b, :, :], SLOPE, z[:, b, :, :],
                                                       ALU.mult, ALU.max), t)
                if g == 0:
                    t0 = V(lambda e: e.memset(run[:, b, 0:1, :], -BIG))
                else:
                    t0 = V(lambda e: e.tensor_copy(run[:, b, 0:1, :], run[:, 1 - b, GC:GC + 1, :]),
                           tok["run", g - 1])
                for h in range(H):
                    init = -BIG if g == 0 else run[:, 1 - b, GC, h:h + 1]
                    t1 = V(lambda e, h=h, init=init: e.tensor_tensor_scan(
                        run[:, b, 1:GC + 1, h], cut[:, cols(g)], z[:, b, :, h], init, ALU.add, ALU.max), t)
                tok["run", g] = t1
                V(lambda e: e.tensor_tensor(wd[:, b, 0:GC, :], z[:, b, :, :], run[:, b, 1:GC + 1, :],
                                            ALU.subtract), t1)
                t2 = V(lambda e: e.tensor_tensor(wd[:, b, GC:2 * GC, :], run[:, b, 0:GC, :],
                                                 run[:, b, 1:GC + 1, :], ALU.subtract), t1, t0)
                t2 = V(lambda e: e.tensor_tensor(
                    wd[:, b, GC:2 * GC, :], wd[:, b, GC:2 * GC, :],
                    bc(cut[:, cols(g)].unsqueeze(2), [P, GC, H]), ALU.add), t2)
                tok["exp", g] = S(lambda e: e.activation(wd[:, b, :, :], wd[:, b, :, :], ACT.Exp), t2)
                V(lambda e: e.tensor_copy(R[:, :, L.M0:L.M0 + H], run[:, b, 1:GC + 1, :]))
                if edge_terms is not None:
                    for h in range(H):
                        at = L.A0 + h
                        init = 0.0 if g == 0 else rows[:, (g - 1) % NS, GC - 1, at:at + 1]
                        V(lambda e, h=h, at=at, init=init: e.tensor_tensor_scan(
                            R[:, :, at], keep[:, cols(g)], ae[:, b, :, h], init, ALU.mult, ALU.add), t_ae,
                            past(tok, "ae_run", g - 1))
                    tok["ae_run", g] = flow.last("vector")

            def running_sums(g):
                s, b = g % NS, g % 2
                R = rows[:, s, :, :]
                num = R[:, :, 0:NW].rearrange("p c (h k) -> p c h k", h=H)
                t = V(lambda e: e.tensor_tensor(num, num, bc(wd[:, b, 0:GC, :].unsqueeze(3),
                                                             [P, GC, H, C + 1]), ALU.mult), tok["exp", g])
                t_a = past(tok, "attr", g - 1)
                for c in range(GC):
                    first = g == 0 and c == 0
                    prev = rows[:, s, c - 1, 0:NW] if c else rows[:, (g - 1) % NS, GC - 1, 0:NW]
                    if not first and H == 1:
                        t = V(lambda e, c=c, prev=prev: e.scalar_tensor_tensor(
                            R[:, c, 0:NW], prev, wd[:, b, GC + c, :], R[:, c, 0:NW], ALU.mult, ALU.add), t)
                    elif not first:
                        t = V(lambda e, c=c, prev=prev: e.tensor_tensor(
                            old[:, c % 2, :, :], prev.rearrange("p (h k) -> p h k", h=H),
                            bc(wd[:, b, GC + c, :].unsqueeze(2), [P, H, C + 1]), ALU.mult), t)
                        t = V(lambda e, c=c: e.tensor_tensor(
                            R[:, c, 0:NW], R[:, c, 0:NW], old[:, c % 2, :, :].rearrange("p h k -> p (h k)"),
                            ALU.add), t)
                    if attr is not None and not first:
                        a = attrs[:, g % NA, c, :]
                        pa = attrs[:, g % NA, c - 1, :] if c else attrs[:, (g - 1) % NA, GC - 1, :]
                        t_a = V(lambda e, c=c, a=a, pa=pa: e.scalar_tensor_tensor(
                            a, pa, keep[:, g * GC + c:g * GC + c + 1], a, ALU.mult, ALU.add),
                            tok["AL", g], t_a)
                tok["main", g], tok["attr", g] = t, t_a

            def store(g):
                tok["S", g] = dma("sync", lambda e: e.dma_start(
                    groups_of(L.sums)[:, cols(g), :], rows[:, g % NS, :, :]), sem_s[g % NS], tok["main", g])
                stored.append(tok["S", g])
                if attr is not None:
                    tok["AS", g] = dma("sync", lambda e: e.dma_start(
                        groups_of(sums_attr)[:, cols(g), :], attrs[:, g % NA, :, :]), sem_as[g % NA],
                        tok["attr", g])

            AHEAD = 2
            for g in range(min(AHEAD, NG)):
                fetch(g)
                fetch_extra(g)
            logits(0)
            for g in range(NG):
                if g + AHEAD < NG:
                    fetch(g + AHEAD)
                    fetch_extra(g + AHEAD)
                if g + 1 < NG:
                    logits(g + 1)
                running_sums(g)
                store(g)
            last = (NG - 1) % NS
            t_stored = [tok["S", g] for g in range(max(0, NG - NS), NG)]
            finish_crossing("att", sb, L.sums, L.W, rows[:, last, GC - 1, :], t_stored, L)
            if attr is not None:
                t_as = [tok["AS", g] for g in range(max(0, NG - NA), NG)]
                finish_crossing("attr", sb, sums_attr, D, attrs[:, (NG - 1) % NA, GC - 1, :],
                                t_as + [flow.last("vector")])

        def node_rows(sb, name, sums, W, depth=2):
            buf = sb(name, [P, depth, JB, W])
            sems = [flow.dma_sem(f"{name}{i}") for i in range(depth)]

            def gather(k, *w):
                for b in range(JB):
                    j = k * JB + b
                    t = dma("gpsimd", lambda e, b=b, j=j: e.indirect_dma_start(
                        out=buf[:, k % depth, b, :], out_offset=None, in_=sums,
                        in_offset=bass.IndirectOffsetOnAxis(ap=sum_row[:, j:j + 1], axis=0)),
                        sems[k % depth], *w)
                return t
            return buf, gather

        def attention_nodes(L, sb, node_l, out_of):
            H, C = L.H, L.C
            R, gather = node_rows(sb, "node_sums", L.sums, L.W)
            own = sb("own_rows", [P, 2, JB, L.W])
            z = sb("self_logit", [P, 2, JB, H])
            ex = sb("self_ex", [P, 2, 2, JB, H])
            mx = sb("self_max", [P, 2, JB, H])
            den = sb("den", [P, 2, JB, H])
            sem_own = [flow.dma_sem(f"own{i}") for i in range(2)]
            tok = {}
            bj = [P, JB, H]

            def fetch(k):
                tok["R", k] = gather(k, past(tok, "O", k - 2))
                tok["own", k] = dma("sync", lambda e: e.dma_start(
                    own[:, k % 2, :, :],
                    L.table.rearrange("(p j) w -> p j w", j=NJ)[:, k * JB:(k + 1) * JB, :]),
                    sem_own[k % 2], past(tok, "O", k - 2))

            def logit(k):
                s, j = k % 2, slice(k * JB, (k + 1) * JB)
                zz, r, m = z[:, s, :, :], R[:, s, :, :], mx[:, s, :, :]
                t = V(lambda e: e.tensor_tensor(zz, own[:, s, :, L.M0:L.M0 + H], node_l[:, j, :], ALU.add),
                      tok["own", k])
                if L.AE:
                    t2 = V(lambda e: e.tensor_tensor(m, r[:, :, L.A0:L.W], bc(inv_deg[:, j].unsqueeze(2), bj),
                                                     ALU.mult), tok["R", k])
                    t = V(lambda e: e.tensor_tensor(zz, zz, m, ALU.add), t, t2)
                t = V(lambda e: e.scalar_tensor_tensor(zz, zz, SLOPE, zz, ALU.mult, ALU.max), t)
                rm = r[:, :, L.M0:L.M0 + H]
                t2 = V(lambda e: e.tensor_tensor(rm, rm, bc(has[:, j].unsqueeze(2), bj), ALU.mult), tok["R", k])
                t2 = V(lambda e: e.tensor_tensor(rm, rm, bc(no_edge[:, j].unsqueeze(2), bj), ALU.add), t2)
                t = V(lambda e: e.tensor_tensor(m, rm, zz, ALU.max), t, t2)
                V(lambda e: e.tensor_tensor(ex[:, s, 0, :, :], rm, m, ALU.subtract), t)
                t = V(lambda e: e.tensor_tensor(ex[:, s, 1, :, :], zz, m, ALU.subtract), t)
                tok["E", k] = S(lambda e: e.activation(ex[:, s, :, :, :], ex[:, s, :, :, :], ACT.Exp), t)

            def join(k):
                s = k % 2
                wide = [P, JB, H, C + 1]

                def heads(ap):
                    return ap[:, :, 0:L.NW].rearrange("p j (h c) -> p j h c", h=H)
                a, b = heads(R[:, s, :, :]), heads(own[:, s, :, :])
                V(lambda e: e.tensor_tensor(a, a, bc(ex[:, s, 0, :, :].unsqueeze(3), wide), ALU.mult),
                  tok["E", k])
                t = V(lambda e: e.tensor_tensor(b, b, bc(ex[:, s, 1, :, :].unsqueeze(3), wide), ALU.mult))
                t = V(lambda e: e.tensor_tensor(a, a, b, ALU.add), t)
                if L.AE:
                    t = V(lambda e: e.tensor_scalar(den[:, s, :, :], a[:, :, :, C], 1e-16, None, ALU.add), t)
                    t = V(lambda e: e.reciprocal(den[:, s, :, :], den[:, s, :, :]), t)
                else:
                    t = V(lambda e: e.reciprocal(den[:, s, :, :], a[:, :, :, C]), t)
                t = V(lambda e: e.tensor_tensor(
                    out_of(k).rearrange("p j (h c) -> p j h c", h=H), a[:, :, :, 0:C],
                    bc(den[:, s, :, :].unsqueeze(3), [P, JB, H, C]), ALU.mult), t)
                tok["O", k] = t

            return [fetch, logit, join], tok

        def over_nodes(ap):
            return bc(ap.unsqueeze(1), [P, JB, D])

        def chunk(ap, k):
            return ap[:, k * JB:(k + 1) * JB, :]

        node_a = sb_kept("node_logit_a", [P, NJ, A.H])
        with ExitStack() as local:
            sb = buffers(local)
            ext, t_ext = load_extended_weights(A, sb, io["a_w"], io["a_att_src"], io["a_att_dst"])
            skewed(table_stages(A, sb, ext, t_ext, node_a, lambda k: None), NK)
            flow.barrier("expand_a")
        with ExitStack() as local:
            sb = buffers(local)
            dst_l = sb("dst_logit", [P, EC, A.H])
            expand_dst_logits(A, node_a, dst_l)
            flow.barrier("edges_a")
            attention_edges(A, sb, dst_l, attr=io["ea128"])
            flow.barrier("nodes_a")

        node_b = sb_kept("node_logit_b", [P, NJ, B.H])
        with ExitStack() as local:
            sb = buffers(local)
            agg = sb("agg", [P, NJ, D])
            par = sb("bn_par", [P, 3, D])
            mean = sb("bn_mean", [P, D])
            scale = sb("bn_scale", [P, D])
            square = sb("square", [P, 2, JB, D])
            sem_par = flow.dma_sem("par")
            for i, name in enumerate(("a_bias", "a_gamma", "a_beta")):
                t_par = dma("sync", lambda e, i=i, name=name: e.dma_start(
                    par[:, i, :], io[name].broadcast_to([P, D])), sem_par)
            stages, tok = attention_nodes(A, sb, node_a, lambda k: chunk(agg, k))

            def rows_valid(j):
                return (n_nodes - j + NJ - 1) // NJ

            def column_sums(k, data, bank, *w):
                for b in range(JB):
                    j = k * JB + b
                    K = rows_valid(j)
                    t = T(lambda e, b=b, j=j, K=K: e.matmul(
                        ps[:, bank, 0:D], ones[0:K, :], data[0:K, b, :], start=(j == 0),
                        stop=(j == NJ - 1)), *w)
                return t

            def add_bias(k):
                tok["B", k] = V(lambda e: e.tensor_tensor(chunk(agg, k), chunk(agg, k),
                                                          over_nodes(par[:, 0, :]), ALU.add),
                                tok["O", k], t_par)
                tok["sum"] = column_sums(k, chunk(agg, k), 0, tok["B", k])
            skewed(stages + [add_bias], NK)
            t = V(lambda e: e.tensor_scalar(mean[:, :], ps[:, 0, 0:D], 1.0 / n_nodes, None, ALU.mult),
                  tok["sum"])
            tok["mean"] = t

            def centre(k):
                tok["c", k] = V(lambda e: e.tensor_tensor(chunk(agg, k), chunk(agg, k),
                                                          over_nodes(mean[:, :]), ALU.subtract),
                                tok["mean"])
                t = S(lambda e: e.activation(square[:, k % 2, :, :], chunk(agg, k), ACT.Square),
                      tok["c", k], past(tok, "q", k - 2))
                tok["q", k] = column_sums(k, square[:, k % 2, :, :], 1, t)
            skewed([centre], NK)
            t = V(lambda e: e.tensor_scalar(scale[:, :], ps[:, 1, 0:D], 1.0 / n_nodes, EPS, ALU.mult,
                                            ALU.add), tok["q", NK - 1])
            t = S(lambda e: e.activation(scale[:, :], scale[:, :], ACT.Sqrt), t)
            t = V(lambda e: e.reciprocal(scale[:, :], scale[:, :]), t)
            tok["scale"] = V(lambda e: e.tensor_tensor(scale[:, :], scale[:, :], par[:, 1, :], ALU.mult), t)

            def residual(k):
                t = V(lambda e: e.tensor_tensor(chunk(agg, k), chunk(agg, k), over_nodes(scale[:, :]),
                                                ALU.mult), tok["scale"])
                t = V(lambda e: e.tensor_tensor(chunk(agg, k), chunk(agg, k), over_nodes(par[:, 2, :]),
                                                ALU.add), t)
                tok["x", k] = V(lambda e: e.scalar_tensor_tensor(chunk(x, k), chunk(agg, k), 0.0,
                                                                 chunk(x, k), ALU.max, ALU.add), t)
            skewed([residual], NK)
            flow.barrier("table_b")
        with ExitStack() as local:
            sb = buffers(local)
            ext, t_ext = load_extended_weights(B, sb, io["b_w"], io["b_att_src"].rearrange(
                "h c -> (h c)").unsqueeze(0), io["b_att_dst"].rearrange("h c -> (h c)").unsqueeze(0))
            skewed(table_stages(B, sb, ext, t_ext, node_b, lambda k: None), NK)
            flow.barrier("expand_b")

        with ExitStack() as local:
            sb = buffers(local)
            dst_l = sb("dst_logit", [P, EC, B.H])
            we = sb("w_edge", [P, EF, B.H, B.C])
            att_e = sb("att_edge", [P, B.H, B.C])
            proj = sb("edge_proj", [P, B.H, EF])
            sem_we = flow.dma_sem("w_edge")
            dma("sync", lambda e: e.dma_start(
                we[:, :, :, :].rearrange("p k h c -> p (k h c)"),
                io["b_w_edge"].rearrange("k d -> (k d)").unsqueeze(0).broadcast_to([P, EF * D])), sem_we)
            t = dma("sync", lambda e: e.dma_start(
                att_e[:, :, :].rearrange("p h c -> p (h c)"),
                io["b_att_edge"].rearrange("h c -> (h c)").unsqueeze(0).broadcast_to([P, D])), sem_we)
            t = V(lambda e: e.tensor_tensor(we[:, :, :, :], we[:, :, :, :],
                                            bc(att_e[:, :, :].unsqueeze(1), [P, EF, B.H, B.C]), ALU.mult), t)
            V(lambda e: e.tensor_reduce(proj[:, :, :].rearrange("p h k -> p k h"), we[:, :, :, :], AX,
                                        ALU.add), t)
            expand_dst_logits(B, node_b, dst_l)
            flow.barrier("edges_b")
            attention_edges(B, sb, dst_l, edge_terms=(io["ea13"], proj, None))
            flow.barrier("nodes_b")

        self_out = sb_kept("self_out", [P, NJ, D])
        with ExitStack() as local:
            sb = buffers(local)
            par = sb("par", [P, 5, D])
            w1 = sb("w1", [P, 3, D])
            w2 = sb("w2", [P, D])
            w3 = sb("w3", [P, D])
            w_rel = sb("w_rel", [P, NREL, D])
            w_self = sb("w_self", [P, D])
            u0 = sb("u0", [P, 1])
            b12 = sb("b12", [P, 3])
            sem_par = flow.dma_sem("par")
            for i, name in enumerate(("b_bias", "b_gamma", "b_beta", "c_b3", "d_self_b")):
                dma("sync", lambda e, i=i, name=name: e.dma_start(
                    par[:, i, :], io[name].broadcast_to([P, D])), sem_par)
            dma("scalar", lambda e: e.dma_start(w1[:, :, :], io["c_w1"].rearrange("(a k) d -> k a d", k=P)), sem_par)
            dma("scalar", lambda e: e.dma_start(w2[:, :], io["c_w2"]), sem_par)
            dma("scalar", lambda e: e.dma_start(w3[:, :], io["c_w3"]), sem_par)
            dma("scalar", lambda e: e.dma_start(w_rel[:, :, :], io["W_rel"].rearrange("r k d -> k r d")), sem_par)
            dma("scalar", lambda e: e.dma_start(w_self[:, :], io["d_self_wT"]), sem_par)
            dma("scalar", lambda e: e.dma_start(u0[:, :], io["c_u"]), sem_par)
            dma("scalar", lambda e: e.dma_start(b12[:, 0:1], io["c_b1"]), sem_par)
            t_par = dma("scalar", lambda e: e.dma_start(b12[:, 1:2], io["c_b2"]), sem_par)
            t = T(lambda e: e.matmul(ps[:, 0, 0:1], w1[:, 2, :], u0[:, :], start=True, stop=True), t_par)
            t_b1 = V(lambda e: e.tensor_tensor(b12[:, 2:3], b12[:, 0:1], ps[:, 0, 0:1], ALU.add), t)

            out_b = sb("out_b", [P, 2, JB, D])
            h1 = sb("h1", [P, JB, D])
            rs, rs2, rs3 = (sb(f"rs{i}", [P, 2, JB]) for i in range(3))
            nb, nb2, nb3 = (sb(f"nb{i}", [P, 2, JB]) for i in range(3))
            hn = sb("hn", [P, 2, JB, D])
            hT = sb("hT", [P, 2, JB * P])
            aT = sb("aT", [P, JB * P])
            mid = sb("mid", [P, 2, JB * P])
            rel = sb("rel", [P, 2, NREL, D])
            sem_rel = [flow.dma_sem(f"rel{i}") for i in range(2)]
            stages, tok = attention_nodes(B, sb, node_b, lambda k: out_b[:, k % 2, :, :])
            sums_a, gather_a = node_rows(sb, "attr_sums", sums_attr, D)
            free = {"turn": t_b1, "mid": None, "rel0": None, "rel1": None}
            col4 = [(i, min(4, JB - i)) for i in range(0, JB, 4)]

            def residual_1(k):
                s, j = k % 2, slice(k * JB, (k + 1) * JB)
                y = out_b[:, s, :, :]
                t_h = norm_relu(k, h1[:, :, :], chunk(x, k), mean_rs[:, j], mean_nb[:, j],
                                past(tok, "y", k - 1))
                t = V(lambda e: e.tensor_tensor(y, y, over_nodes(par[:, 0, :]), ALU.add), tok["O", k], t_par)
                t = V(lambda e: e.tensor_tensor(y, y, h1[:, :, :], ALU.add), t, t_h)
                tok["y", k] = t
                tok["ln", k] = layer_norm_stats(k, y, rs[:, s, :], nb[:, s, :], t)
                gather_attr(k)

            def norm_1(k):
                s = k % 2
                y = out_b[:, s, :, :]
                for b in range(JB):
                    t = S(lambda e, b=b: e.activation(y[:, b, :], y[:, b, :], ACT.Identity,
                                                      bias=nb[:, s, b:b + 1], scale=rs[:, s, b:b + 1]),
                          tok["ln", k])
                t = V(lambda e: e.tensor_tensor(y, y, over_nodes(par[:, 1, :]), ALU.mult), t)
                t = V(lambda e: e.tensor_tensor(y, y, over_nodes(par[:, 2, :]), ALU.add), t)
                t = V(lambda e: e.scalar_tensor_tensor(chunk(x, k), y, 0.0, chunk(x, k), ALU.max, ALU.add), t)
                t = layer_norm_stats(k, chunk(x, k), rs2[:, s, :], nb2[:, s, :], t)
                tok["h2", k] = norm_relu(k, hn[:, s, :, :], chunk(x, k), rs2[:, s, :], nb2[:, s, :], t,
                                         past(tok, "T3", k - 2))

            def gather_attr(k):
                s, j = k % 2, slice(k * JB, (k + 1) * JB)
                t = gather_a(k, past(tok, "aT", k - 2))
                tok["a", k] = V(lambda e: e.tensor_tensor(
                    sums_a[:, s, :, :], sums_a[:, s, :, :], bc(has[:, j].unsqueeze(2), [P, JB, D]),
                    ALU.mult), t)

            def mlp(k):
                s = k % 2
                t_x = transposed(hT[:, s, :], 0, hn[:, s, :, :], tok["h2", k], free["turn"])
                t_a = transposed(aT[:, :], 0, sums_a[:, s, :, :], tok["a", k], t_x)
                tok["aT", k] = free["turn"] = t_a
                for i, n in col4:
                    c = slice(i * P, (i + n) * P)
                    T(lambda e, i=i, n=n, c=c: e.matmul(ps[:, 2 + i // 4, 0:n * P], w1[:, 0, :], hT[:, s, c],
                                                        start=True, stop=False), t_x, free["mid"])
                    t = T(lambda e, i=i, n=n, c=c: e.matmul(ps[:, 2 + i // 4, 0:n * P], w1[:, 1, :],
                                                            aT[:, c], start=False, stop=True), t_a)
                for i, n in col4:
                    t1 = S(lambda e, i=i, n=n: e.activation(mid[:, 0, i * P:(i + n) * P],
                                                            ps[:, 2 + i // 4, 0:n * P], ACT.Relu,
                                                            bias=b12[:, 2:3]), t, t_b1)
                for i, n in col4:
                    t = T(lambda e, i=i, n=n: e.matmul(ps[:, 2 + i // 4, 0:n * P], w2[:, :],
                                                       mid[:, 0, i * P:(i + n) * P], start=True, stop=True), t1)
                for i, n in col4:
                    t1 = S(lambda e, i=i, n=n: e.activation(mid[:, 1, i * P:(i + n) * P],
                                                            ps[:, 2 + i // 4, 0:n * P], ACT.Relu,
                                                            bias=b12[:, 1:2]), t)
                for b in range(JB):
                    t = T(lambda e, b=b: e.matmul(ps[:, 2 + b // 4, (b % 4) * P:(b % 4 + 1) * P],
                                                  mid[:, 1, b * P:(b + 1) * P], w3[:, :], start=True,
                                                  stop=True), t1)
                t1 = V(lambda e: e.tensor_tensor(chunk(x, k), chunk(x, k), over_nodes(par[:, 3, :]), ALU.add),
                       tok["h2", k])
                for i, n in col4:
                    xs = x[:, k * JB + i:k * JB + i + n, :].rearrange("p j d -> p (j d)")
                    t2 = V(lambda e, i=i, n=n, xs=xs: e.tensor_tensor(xs, xs, ps[:, 2 + i // 4, 0:n * P],
                                                                      ALU.add), t, t1)
                free["mid"] = t2
                t = layer_norm_stats(k, chunk(x, k), rs3[:, s, :], nb3[:, s, :], t2)
                tok["h3", k] = norm_relu(k, hn[:, s, :, :], chunk(x, k), rs3[:, s, :], nb3[:, s, :], t, t_x)

            def relations(k):
                s = k % 2
                t_x = transposed(hT[:, s, :], 0, hn[:, s, :, :], tok["h3", k], free["turn"], tok["aT", k])
                free["turn"] = tok["T3", k] = t_x
                half = NREL // 2
                for b in range(JB):
                    j, r, bank = k * JB + b, (k * JB + b) % 2, 4 + 2 * ((k * JB + b) % 2)
                    hb = hT[:, s, b * P:(b + 1) * P]
                    for i in range(2):
                        t = T(lambda e, i=i, hb=hb, bank=bank: e.matmul(
                            ps[:, bank + i, 0:half * D], hb,
                            w_rel[:, i * half:(i + 1) * half, :].rearrange("p r d -> p (r d)"),
                            start=True, stop=True), t_x, free[f"rel{r}"])
                    tt = T(lambda e, b=b, hb=hb: e.matmul(ps[:, 2 + b // 4, (b % 4) * P:(b % 4 + 1) * P], hb,
                                                          w_self[:, :], start=True, stop=True), free["mid"])
                    t1 = S(lambda e, r=r, bank=bank: e.activation(
                        rel[:, r, 0:half, :].rearrange("p r d -> p (r d)"), ps[:, bank, 0:half * D],
                        ACT.Copy), t, past(tok, "rel", j - 2))
                    t2 = V(lambda e, r=r, bank=bank: e.tensor_copy(
                        rel[:, r, half:NREL, :].rearrange("p r d -> p (r d)"), ps[:, bank + 1, 0:half * D]),
                        t, t1, past(tok, "rel", j - 2))
                    free[f"rel{r}"] = t2
                    tok["rel", j] = dma("sync", lambda e, j=j, r=r: e.dma_start(
                        table_rel.rearrange("(p j r) d -> p j (r d)", j=NJ, r=NREL)[:, j, :],
                        rel[:, r, :, :].rearrange("p r d -> p (r d)")), sem_rel[r], t1, t2)
                for i, n in col4:
                    so = self_out[:, k * JB + i:k * JB + i + n, :]
                    t1 = V(lambda e, i=i, n=n, so=so: e.tensor_tensor(
                        so, ps[:, 2 + i // 4, 0:n * P].rearrange("p (n d) -> p n d", d=D),
                        bc(par[:, 4, :].unsqueeze(1), [P, n, D]), ALU.add), tt)
                free["mid"] = t1

            skewed(stages + [residual_1, norm_1, mlp, relations], NK)
            flow.barrier("edges_rel")

        with ExitStack() as local:
            sb = buffers(local)
            NS = 4
            rows = sb("edge_rows", [P, NS, GC, D])
            sem_g = [flow.dma_sem(f"gather{i}") for i in range(NS)]
            sem_s = [flow.dma_sem(f"store{i}") for i in range(NS)]
            tok = {}

            def fetch(g):
                s = g % NS
                for c in range(GC):
                    tok["G", g] = dma("gpsimd", lambda e, c=c: e.indirect_dma_start(
                        out=rows[:, s, c, :], out_offset=None, in_=table_rel,
                        in_offset=bass.IndirectOffsetOnAxis(ap=rel_row[:, g * GC + c:g * GC + c + 1],
                                                            axis=0)),
                        sem_g[s], past(tok, "S", g - NS), past(tok, "main", g - NS + 1))
            for g in range(min(2, NG)):
                fetch(g)
            t = None
            for g in range(NG):
                if g + 2 < NG:
                    fetch(g + 2)
                s = g % NS
                for c in range(GC):
                    if g or c:
                        prev = rows[:, s, c - 1, :] if c else rows[:, (g - 1) % NS, GC - 1, :]
                        t = V(lambda e, s=s, c=c, g=g, prev=prev: e.scalar_tensor_tensor(
                            rows[:, s, c, :], prev, keep[:, g * GC + c:g * GC + c + 1], rows[:, s, c, :],
                            ALU.mult, ALU.add), tok["G", g], t)
                tok["main", g] = t
                tok["S", g] = dma("sync", lambda e, g=g, s=s: e.dma_start(
                    groups_of(sums_rel)[:, g * GC:(g + 1) * GC, :], rows[:, s, :, :]), sem_s[s], t)
            finish_crossing("rel", sb, sums_rel, D, rows[:, (NG - 1) % NS, GC - 1, :],
                            [tok["S", g] for g in range(max(0, NG - NS), NG)])
            flow.barrier("nodes_rel")

        with ExitStack() as local:
            sb = buffers(local)
            R, gather = node_rows(sb, "node_sums", sums_rel, D, 3)
            sem_out = [flow.dma_sem(f"out{i}") for i in range(3)]
            tok = {}

            def fetch_rel(k):
                tok["R", k] = gather(k, past(tok, "S", k - 3))

            def last(k):
                r, j = R[:, k % 3, :, :], slice(k * JB, (k + 1) * JB)
                t = V(lambda e: e.tensor_tensor(r, r, bc(inv_deg[:, j].unsqueeze(2), [P, JB, D]), ALU.mult),
                      tok["R", k])
                t = V(lambda e: e.tensor_tensor(r, r, chunk(self_out, k), ALU.add), t)
                t = V(lambda e: e.scalar_tensor_tensor(r, r, 0.0, chunk(x, k), ALU.max, ALU.add), t)
                tok["S", k] = dma("sync", lambda e: e.dma_start(
                    chunk(io["out"].rearrange("(p j) d -> p j d", j=NJ), k), r), sem_out[k % 3], t)
            skewed([fetch_rel, last], NK)
            flow.barrier("end")

        block = ctx.enter_context(nc.Block())

        @block.sync
        def _(eng):
            flow.play("sync", eng)

        @block.scalar
        def _(eng):
            flow.play("scalar", eng)

        @block.gpsimd
        def _(eng):
            flow.play("gpsimd", eng)

        @block.vector
        def _(eng):
            flow.play("vector", eng)

        @block.tensor
        def _(eng):
            flow.play("tensor", eng)


def kernel(**inputs):
    import concourse.bacc as bacc
    from concourse.bass_utils import run_bass_kernel_spmd

    a = {k: np.asarray(v) for k, v in inputs.items()}
    n_nodes, n_edges = a["x"].shape[0], a["src"].shape[0]
    nj, ec = padded_sizes(n_nodes, n_edges)
    np_, ep = P * nj, P * ec

    def padded(v, rows, fill=0):
        return np.concatenate([v, np.full((rows - v.shape[0],) + v.shape[1:], fill, v.dtype)])

    dst = padded(a["dst"], ep, np_ - 1)
    ch = chunk_len(ep)

    def row(v):
        return v.reshape(1, -1)

    arrays = {
        "x": padded(a["x"], np_).reshape(P, nj, D),
        "src": padded(a["src"], ep).reshape(P, ec),
        "dst": dst.reshape(P, ec),
        "dst_prev": np.concatenate([np.full(1, -1, dst.dtype), dst.reshape(P, ec)[:-1, -1]]).reshape(P, 1),
        "dst_last": dst.reshape(-1, ch)[:, -1].reshape(1, -1),
        "edge_type": padded(a["edge_type_8"], ep).reshape(P, ec),
        "ea128": padded(a["edge_attr_128"], ep).reshape(P, ec, D),
        "ea13": padded(a["edge_attr_13"], ep).reshape(P, ec, -1),
        "a_w": a["L0_gnn_W"],
        "a_att_src": row(a["L0_gnn_att_src"]),
        "a_att_dst": row(a["L0_gnn_att_dst"]),
        "a_bias": row(a["L0_gnn_bias"]),
        "a_gamma": row(a["L0_gnn_gamma"]),
        "a_beta": row(a["L0_gnn_beta"]),
        "b_w": a["L1_gnn_W"],
        "b_att_src": a["L1_gnn_att_src"],
        "b_att_dst": a["L1_gnn_att_dst"],
        "b_w_edge": a["L1_gnn_W_edge"],
        "b_att_edge": a["L1_gnn_att_edge"],
        "b_bias": row(a["L1_gnn_bias"]),
        "b_gamma": row(a["L1_gnn_ln_gamma"]),
        "b_beta": row(a["L1_gnn_ln_beta"]),
        "c_u": a["L2_gnn_u"][0].reshape(-1, 1),
        "c_w1": a["L2_gnn_W1"],
        "c_b1": a["L2_gnn_b1"].reshape(-1, 1),
        "c_w2": a["L2_gnn_W2"],
        "c_b2": a["L2_gnn_b2"].reshape(-1, 1),
        "c_w3": a["L2_gnn_W3"],
        "c_b3": row(a["L2_gnn_b3"]),
        "W_rel": a["L3_gnn_W_rel"],
        "d_self_wT": a["L3_gnn_W_self_w"].T,
        "d_self_b": row(a["L3_gnn_W_self_b"]),
    }
    arrays = {k: np.ascontiguousarray(v) for k, v in arrays.items()}

    nc = bacc.Bacc("TRN2", target_bir_lowering=False, num_devices=1)
    io = {k: nc.dram_tensor(f"in_{k}", v.shape, mybir.dt.from_np(v.dtype), kind="ExternalInput").ap()
          for k, v in arrays.items()}
    io["out"] = nc.dram_tensor("out_x", (np_, D), F32, kind="ExternalOutput").ap()
    build(nc, io, n_nodes, n_edges)
    result = run_bass_kernel_spmd(nc, [{f"in_{k}": v for k, v in arrays.items()}], core_ids=[0])
    return result.results[0]["out_x"][:n_nodes]
```

```python
from contextlib import ExitStack
from itertools import cycle
import math

import numpy as np
import concourse.bass as bass
from concourse import mybir

F32 = mybir.dt.float32
I32 = mybir.dt.int32
ALU = mybir.AluOpType
ACT = mybir.ActivationFunctionType
AX = mybir.AxisListType.X

P = 128
D = 128
GC = 16
BIG = 1.0e30
EPS = 1e-5
SLOPE = 0.2


def padded_sizes(n_nodes, n_edges):
    nj = -(-n_nodes // P)
    ec = -(-n_edges // (P * GC)) * GC
    return nj, ec


def chunk_len(ep):
    return min((d for d in range(1, ep + 1) if ep % d == 0), key=lambda d: abs(d - math.sqrt(ep)))


class Flow:
    ENGINES = ("sync", "scalar", "gpsimd", "vector", "tensor")

    def __init__(self, nc, ctx):
        self.nc, self.ctx = nc, ctx
        self.queue = {e: [] for e in self.ENGINES}
        self.dma_sems = []
        self.n = 0
        self.stage_name = ""
        self.begin("start")

    def begin(self, name):
        self.done = {e: [None, 0] for e in self.ENGINES}
        self.dma_sems = []
        self.stage_name = name

    def sem(self, name):
        self.n += 1
        return self.ctx.enter_context(self.nc.semaphore(f"{self.stage_name}_{name}_{self.n}"))

    def op(self, engine, fn, *waits):
        d = self.done[engine]
        if d[0] is None:
            d[0] = self.sem(engine)
        d[1] += 1
        self.queue[engine].append((waits, fn, d[0], 1))
        return (d[0], d[1])

    def last(self, engine):
        d = self.done[engine]
        return tuple(d) if d[1] else None

    def dma_sem(self, name):
        s = [self.sem(name), 0]
        self.dma_sems.append(s)
        return s

    def dma(self, engine, fn, s, *waits):
        s[1] += 16
        self.queue[engine].append((waits, fn, s[0], 16))
        return (s[0], s[1])

    def barrier(self, name):
        tokens = [tuple(d) for d in self.done.values() if d[1]] + [tuple(s) for s in self.dma_sems if s[1]]
        for e in self.ENGINES:
            self.queue[e].append((tokens, None, None, 0))
        self.begin(name)

    def play(self, name, engine):
        seen = {}
        for waits, fn, s, by in self.queue[name]:
            for w in waits:
                if w is not None and seen.get(w[0].name, 0) < w[1]:
                    engine.wait_ge(w[0], w[1])
                    seen[w[0].name] = w[1]
            if fn is not None:
                fn(engine).then_inc(s, by)


def past(tokens, what, k):
    return tokens[what, k] if k >= 0 else None


def skewed(stages, n):
    for step in range(n + len(stages) - 1):
        for s in reversed(range(len(stages))):
            if 0 <= step - s < n:
                stages[s](step - s)


def build(nc, io, n_nodes, n_edges):
    NJ, EC = padded_sizes(n_nodes, n_edges)
    NP, EP = P * NJ, P * EC
    NG = EC // GC
    CH = chunk_len(EP)
    NCH = EP // CH
    JB = max(d for d in range(1, 8) if NJ % d == 0)
    NK = NJ // JB
    NREL = io["W_rel"].shape[0]
    EF = io["ea13"].shape[-1]

    def dram(name, shape, dt=F32):
        return nc.dram_tensor(name, list(shape), dt).ap()

    class Layer:
        def __init__(self, name, heads, edge_terms):
            self.H, self.C = heads, D // heads
            self.NW = heads * (self.C + 1)
            self.M0 = self.NW
            self.A0 = self.NW + heads
            self.AE = heads if edge_terms else 0
            self.W = self.A0 + self.AE
            self.WN = self.NW + self.AE
            self.table = dram(f"table_{name}", [NP, self.W])
            self.sums = dram(f"sums_{name}", [EP + P, self.W])
            self.dst_logit = dram(f"dst_logit_{name}", [EP + NP, heads])
            self.node_logit = dram(f"node_logit_{name}", [NP, heads])

    A = Layer("a", 1, False)
    B = Layer("b", io["b_att_src"].shape[0], True)
    sums_attr = dram("sums_attr", [EP + P, D])
    table_rel = dram("table_rel", [NP * NREL, D])
    sums_rel = dram("sums_rel", [EP + P, D])
    dst_float = dram("dst_float", [NCH, CH])

    with ExitStack() as ctx:
        flow = Flow(nc, ctx)
        op, dma = flow.op, flow.dma

        def V(fn, *w):
            return op("vector", fn, *w, flow.last("vector"))

        def S(fn, *w): return op("scalar", fn, *w)
        def T(fn, *w): return op("tensor", fn, *w)

        def buffers(where):
            def sb(name, shape, dt=F32):
                flow.n += 1
                return where.enter_context(nc.sbuf_tensor(f"{name}_{flow.n}", list(shape), dt))
            return sb

        sb = sb_kept = buffers(ctx)
        ps = ctx.enter_context(nc.psum_tensor("ps", [P, 8, 512], F32))

        x = sb("x", [P, NJ, D])
        ident = sb("ident", [P, P])
        ones = sb("ones", [P, P])
        src = sb("src_i", [P, EC], I32)
        rel_row = sb("rel_row", [P, EC], I32)
        dst_first = sb("dst_first", [P, 1], I32)
        keep = sb("keep", [P, EC])
        cut = sb("cut", [P, EC])
        keep_all = sb("keep_all", [P, 1])
        cut_all = sb("cut_all", [P, 1])
        head_row = sb("head_row", [P, 1], I32)
        sum_row = sb("sum_row", [P, NJ], I32)
        start_row = sb("start_row", [P, NJ], I32)
        has = sb("has", [P, NJ])
        no_edge = sb("no_edge", [P, NJ])
        inv_deg = sb("inv_deg", [P, NJ])
        mean_rs = sb("mean_rs", [P, NJ])
        mean_nb = sb("mean_nb", [P, NJ])
        node_a = sb("node_logit_a", [P, NJ, A.H])
        node_b = sb("node_logit_b", [P, NJ, B.H])
        stats = sb("stats", [P, 2, JB, 6])
        mv = sb("mv", [P, 2, JB, 2])
        std = sb("std", [P, 2, JB])

        def bc(ap, shape):
            return ap.broadcast_to(shape)

        def layer_norm_stats(k, data, rs, nb, *w):
            s = k % 2
            for b in range(JB):
                t = op("vector", lambda e, b=b: e.bn_stats(stats[:, s, b, :], data[:, b, :]), *w)
            for b in range(JB):
                op("vector", lambda e, b=b: e.bn_aggr(mv[:, s, b, :], stats[:, s, b, :]), t)
            t = V(lambda e: e.tensor_scalar(std[:, s, :], mv[:, s, :, 1], EPS, None, ALU.add), t)
            t = S(lambda e: e.activation(std[:, s, :], std[:, s, :], ACT.Sqrt), t)
            t = V(lambda e: e.reciprocal(rs, std[:, s, :]), t)
            return V(lambda e: e.scalar_tensor_tensor(nb, mv[:, s, :, 0], -1.0, rs, ALU.mult, ALU.mult), t)

        def norm_relu(k, out, data, rs, nb, *w):
            for b in range(JB):
                t = S(lambda e, b=b: e.activation(out[:, b, :], data[:, b, :], ACT.Relu,
                                                  bias=nb[:, b:b + 1], scale=rs[:, b:b + 1]), *w)
            return t

        def transposed(out, banks, data, *w):
            for b in range(JB):
                t = T(lambda e, b=b: e.transpose(ps[:, banks + b // 4, (b % 4) * P:(b % 4 + 1) * P],
                                                 data[:, b, :], ident[:, :]), *w)
            for i in range(0, JB, 4):
                n = min(4, JB - i)
                tt = V(lambda e, i=i, n=n: e.tensor_copy(out[:, i * P:(i + n) * P],
                                                         ps[:, banks + i // 4, 0:n * P]), t)
            return tt

        def load_extended_weights(L, sb, w_dram, att_src, att_dst):
            w = sb("w_plain", [P, L.H, L.C])
            att = sb("att", [P, 2, L.H, L.C])
            prod = sb("w_att", [P, L.H, L.C])
            ext = sb("w_ext", [P, L.W + L.H])
            sem_w = flow.dma_sem("w")
            dma("sync", lambda e: e.dma_start(w[:, :, :], w_dram.rearrange("k (h c) -> k h c", h=L.H)), sem_w)
            dma("sync", lambda e: e.dma_start(att[:, 0, :, :].rearrange("p h c -> p (h c)"),
                                              att_src.broadcast_to([P, D])), sem_w)
            t_w = dma("sync", lambda e: e.dma_start(att[:, 1, :, :].rearrange("p h c -> p (h c)"),
                                                    att_dst.broadcast_to([P, D])), sem_w)
            t = V(lambda e: e.memset(ext[:, :], 0.0))
            last = V(lambda e: e.tensor_copy(
                ext[:, 0:L.NW].rearrange("p (h c) -> p h c", h=L.H)[:, :, 0:L.C], w[:, :, :]), t, t_w)
            for i, at in ((0, L.M0), (1, L.W)):
                t = V(lambda e, i=i: e.tensor_tensor(prod[:, :, :], w[:, :, :], att[:, i, :, :], ALU.mult),
                      t_w, last)
                last = V(lambda e, at=at: e.tensor_reduce(ext[:, at:at + L.H], prod[:, :, :], AX, ALU.add), t)
            return ext, last

        def table_stages(L, sb, ext, t_ext, node_l, first, sem_scatter=None):
            hn = sb("hn", [P, 2, JB, D])
            hT = sb("hT", [P, 2, JB * P])
            rows = sb("rows", [P, 2, JB, L.W])
            sem_rows = [flow.dma_sem(f"rows{i}") for i in range(2)]
            tok = {}
            WX = L.W + L.H

            def stats_of(k):
                j = slice(k * JB, (k + 1) * JB)
                tok["n", k] = layer_norm_stats(k, x[:, j, :], mean_rs[:, j], mean_nb[:, j], first(k))

            def norm(k):
                j = slice(k * JB, (k + 1) * JB)
                tok["h", k] = norm_relu(k, hn[:, k % 2, :, :], x[:, j, :], mean_rs[:, j], mean_nb[:, j],
                                        tok["n", k], past(tok, "T", k - 2))

            def turn(k):
                tok["T", k] = transposed(hT[:, k % 2, :], 0, hn[:, k % 2, :, :], tok["h", k],
                                         past(tok, "T", k - 1), past(tok, "P", k - 2))

            def project(k):
                for b in range(JB):
                    t = T(lambda e, b=b: e.matmul(
                        ps[:, 2 + b // 3, (b % 3) * WX:(b % 3 + 1) * WX],
                        hT[:, k % 2, b * P:(b + 1) * P], ext[:, :], start=True, stop=True),
                        tok["T", k], t_ext, past(tok, "C", k - 1))
                tok["P", k] = t
                for i in range(0, JB, 3):
                    n = min(3, JB - i)
                    src_ps = ps[:, 2 + i // 3, 0:n * WX].rearrange("p (n w) -> p n w", w=WX)
                    tok["C", k] = S(lambda e, i=i, n=n, v=src_ps: e.activation(
                        rows[:, k % 2, i:i + n, :], v[:, :, 0:L.W], ACT.Copy), t, past(tok, "D", k - 2))
                    tok["C", k] = S(lambda e, i=i, n=n, v=src_ps: e.activation(
                        node_l[:, k * JB + i:k * JB + i + n, :], v[:, :, L.W:WX], ACT.Copy))

            def store(k):
                one = rows[:, k % 2, :, 0:L.NW].rearrange("p j (h c) -> p j h c", h=L.H)[:, :, :, L.C]
                t = V(lambda e: e.memset(one, 1.0), tok["C", k])
                tok["D", k] = dma("sync", lambda e: e.dma_start(
                    L.table.rearrange("(p j) w -> p j w", j=NJ)[:, k * JB:(k + 1) * JB, :],
                    rows[:, k % 2, :, :]), sem_rows[k % 2], t)
                if sem_scatter:
                    scatter_logits(L, node_l, range(k * JB, (k + 1) * JB), sem_scatter, tok["C", k])

            return [stats_of, norm, turn, project, store]

        def scatter_logits(L, node_l, blocks, sem, *w):
            for j in blocks:
                t = dma("gpsimd", lambda e, j=j: e.indirect_dma_start(
                    out=L.dst_logit, out_offset=bass.IndirectOffsetOnAxis(ap=start_row[:, j:j + 1], axis=0),
                    in_=node_l[:, j, :], in_offset=None), sem, *w)
            return t

        def expand_dst_logits(L, dst_l):
            sem_ld = flow.dma_sem("dst_logit")
            sem_first = flow.dma_sem("first")
            t = dma("sync", lambda e: e.dma_start(
                dst_l[:, :, :], L.dst_logit[0:EP, :].rearrange("(p c) h -> p c h", c=EC)), sem_ld)
            t = dma("gpsimd", lambda e: e.indirect_dma_start(
                out=dst_l[:, 0, :], out_offset=None, in_=L.node_logit,
                in_offset=bass.IndirectOffsetOnAxis(ap=dst_first[:, 0:1], axis=0)), sem_first, t)
            for h in range(L.H):
                V(lambda e, h=h: e.tensor_tensor_scan(dst_l[:, :, h], keep[:, :], dst_l[:, :, h], 0.0,
                                                      ALU.mult, ALU.add), t)

        def store_node_logits(L, node_l, t):
            dma("sync", lambda e: e.dma_start(
                L.node_logit.rearrange("(p j) h -> p j h", j=NJ), node_l[:, :, :]),
                flow.dma_sem("node_logit"), t)

        flow.begin("graph")
        with ExitStack() as local:
            sb = buffers(local)
            dst = sb("dst_i", [P, EC], I32)
            typ = sb("typ_i", [P, EC], I32)
            dst_f = sb("dst_f", [P, EC])
            last_i = sb("last_i", [P, NCH], I32)
            last_f = sb("last_f", [P, NCH])
            zero = sb("zero", [P, EC])
            tmp_e = sb("tmp_e", [P, EC])
            prev_i = sb("prev_i", [P, 1], I32)
            prev_f = sb("prev_f", [P, 1])
            iot = sb("iot", [P, NJ + 1], I32)
            v = sb("v", [P, NJ + 1])
            col_i = sb("col_i", [P, P], I32)
            row_i = sb("row_i", [P, P], I32)
            row_f = sb("row_f", [P, P])
            own_i = sb("own_i", [P, 1], I32)
            own_f = sb("own_f", [P, 1])
            junk = sb("junk", [P, 2, max(NCH, CH)])
            q = sb("q", [P, NJ + 1])
            q_i = sb("q_i", [P, NJ + 1], I32)
            cnt = sb("cnt", [P, NJ + 1])
            NPIECE = 5
            piece = sb("piece", [P, NPIECE, CH])
            big = sb("big", [P, NJ, P])
            s1 = sb("s1", [P, NJ])
            s2 = sb("s2", [P, NJ])
            s3 = sb("s3", [P, NJ])
            s4 = sb("s4", [P, NJ])
            s5 = sb("s5", [P, NJ])
            s6 = sb("s6", [P, NJ])
            hc = sb("hc", [P, 1])

            sem_dst = flow.dma_sem("dst")
            sem_last = flow.dma_sem("last")
            sem_x = flow.dma_sem("x")
            sem_idx = flow.dma_sem("idx")
            sem_prev = flow.dma_sem("prev")
            sem_zero = flow.dma_sem("zero")
            sem_dstf = flow.dma_sem("dstf")
            t_dst = dma("sync", lambda e: e.dma_start(dst[:, :], io["dst"]), sem_dst)
            t_last = dma("scalar", lambda e: e.dma_start(
                last_i[:, :], io["dst_last"][0:1, :].broadcast_to([P, NCH])), sem_last)
            t_idx = dma("sync", lambda e: e.dma_start(src[:, :], io["src"]), sem_idx)
            t_idx = dma("scalar", lambda e: e.dma_start(typ[:, :], io["edge_type"]), sem_idx)
            t_x = dma("sync", lambda e: e.dma_start(x[:, :, :], io["x"]), sem_x)
            t_prev = dma("scalar", lambda e: e.dma_start(prev_i[:, :], io["dst_prev"]), sem_prev)
            t_z = V(lambda e: e.memset(zero[:, :], 0.0))
            for L in (A, B):
                flat = L.dst_logit[0:EP, :].rearrange("(p c) h -> p (c h)", c=EC)
                for k in range(L.H):
                    dma("scalar", lambda e, o=flat[:, k * EC:(k + 1) * EC]: e.dma_start(o, zero[:, :]),
                        sem_zero, t_z)
            t_f = V(lambda e: e.tensor_copy(dst_f[:, :], dst[:, :]), t_dst)
            t_store = dma("sync", lambda e: e.dma_start(
                dst_float.rearrange("a b -> (a b)").rearrange("(p c) -> p c", c=EC), dst_f[:, :]),
                sem_dstf, t_f)
            t_i = op("gpsimd", lambda e: e.iota(iot[:, :], [[1, NJ + 1]], base=-1, channel_multiplier=NJ))
            t_i2 = op("gpsimd", lambda e: e.iota(col_i[:, :], [[1, P]], base=0, channel_multiplier=-1))
            t_i3 = op("gpsimd", lambda e: e.iota(row_i[:, :], [[EC, P]], base=0, channel_multiplier=0))
            t_i4 = op("gpsimd", lambda e: e.iota(own_i[:, :], [[0, 1]], base=0, channel_multiplier=EC))
            V(lambda e: e.tensor_scalar(ident[:, :], col_i[:, :], 0.0, None, ALU.is_equal), t_i2)
            V(lambda e: e.memset(ones[:, :], 1.0))
            V(lambda e: e.tensor_copy(row_f[:, :], row_i[:, :]), t_i3)
            t_own = V(lambda e: e.tensor_copy(own_f[:, :], own_i[:, :]), t_i4)
            t_v = V(lambda e: e.tensor_copy(v[:, :], iot[:, :]), t_i)
            t_lf = V(lambda e: e.tensor_copy(last_f[:, :], last_i[:, :]), t_last)
            t_junk = [t_v, t_v]
            for j in range(NJ + 1):
                t = t_junk[j % 2] = op("vector", lambda e, j=j: e.tensor_scalar(
                    junk[:, j % 2, 0:NCH], last_f[:, :], v[:, j:j + 1], None, ALU.is_le, ALU.add,
                    accum_out=q[:, j:j + 1]), t_junk[j % 2], t_lf)
            t = V(lambda e: e.tensor_scalar(q[:, :], q[:, :], float(NCH - 1), None, ALU.min), t)
            t_q = V(lambda e: e.tensor_copy(q_i[:, :], q[:, :]), t)
            sem_piece = [flow.dma_sem(f"piece{k}") for k in range(NPIECE)]
            used = {}

            def count_in_pieces(k):
                for j in range(k * JB, (k + 1) * JB + (k == NK - 1)):
                    t = dma("gpsimd", lambda e, j=j: e.indirect_dma_start(
                        out=piece[:, j % NPIECE, :], out_offset=None, in_=dst_float,
                        in_offset=bass.IndirectOffsetOnAxis(ap=q_i[:, j:j + 1], axis=0)),
                        sem_piece[j % NPIECE], t_q, t_store, past(used, "piece", j - NPIECE))
                    used["piece", j] = op("vector", lambda e, j=j: e.tensor_scalar(
                        junk[:, j % 2, 0:CH], piece[:, j % NPIECE, :], v[:, j:j + 1], None, ALU.is_le,
                        ALU.add, accum_out=cnt[:, j:j + 1]), t, past(used, "piece", j - 2))
            ext_a, t_ext_a = load_extended_weights(A, sb, io["a_w"], io["a_att_src"], io["a_att_dst"])
            table_a = table_stages(A, sb, ext_a, t_ext_a, node_a, lambda k: t_x)
            skewed([count_in_pieces] + table_a, NK)
            store_node_logits(A, node_a, flow.last("scalar"))
            t = V(lambda e: e.scalar_tensor_tensor(cnt[:, :], q[:, :], float(CH), cnt[:, :], ALU.mult,
                                                   ALU.add))
            start, end = cnt[:, 0:NJ], cnt[:, 1:NJ + 1]
            t_has = V(lambda e: e.tensor_tensor(has[:, :], end, start, ALU.is_gt), t)
            t_n = V(lambda e: e.tensor_scalar(s5[:, :], v[:, 0:NJ], float(EP + 1), None, ALU.add), t)
            t = V(lambda e: e.tensor_tensor(s6[:, :], start, s5[:, :], ALU.subtract), t_n)
            t = V(lambda e: e.tensor_tensor(s6[:, :], s6[:, :], has[:, :], ALU.mult), t)
            t = V(lambda e: e.tensor_tensor(s6[:, :], s6[:, :], s5[:, :], ALU.add), t)
            t_start = V(lambda e: e.tensor_copy(start_row[:, :], s6[:, :]), t)
            scatter_logits(A, node_a, range(NJ), flow.dma_sem("scatter"), t_start,
                           (sem_zero[0], sem_zero[1]))
            t_deg = V(lambda e: e.tensor_tensor(s4[:, :], end, start, ALU.subtract), t)
            t_l = V(lambda e: e.tensor_scalar(s1[:, :], end, -1.0, 0.0, ALU.add, ALU.max))
            V(lambda e: e.tensor_scalar(no_edge[:, :], has[:, :], BIG, -BIG, ALU.mult, ALU.add), t_has)
            t_deg = V(lambda e: e.tensor_scalar(s4[:, :], s4[:, :], 1.0, None, ALU.max), t_deg)
            t_deg = V(lambda e: e.reciprocal(s4[:, :], s4[:, :]), t_deg)
            V(lambda e: e.tensor_tensor(inv_deg[:, :], s4[:, :], has[:, :], ALU.mult), t_deg)
            t = V(lambda e: e.tensor_tensor(
                big[:, :, :], bc(s1[:, :].unsqueeze(2), [P, NJ, P]),
                bc(row_f[:, :].unsqueeze(1), [P, NJ, P]), ALU.is_ge), t_l)
            t_p1 = V(lambda e: e.tensor_reduce(s2[:, :], big[:, :, :], AX, ALU.add), t)
            t = V(lambda e: e.tensor_scalar(s3[:, :], s2[:, :], float(EC), float(-EC), ALU.mult, ALU.add), t_p1)
            t = V(lambda e: e.tensor_tensor(s3[:, :], start, s3[:, :], ALU.is_lt), t)
            t = V(lambda e: e.tensor_tensor(s3[:, :], s3[:, :], has[:, :], ALU.mult), t)
            t2 = V(lambda e: e.scalar_tensor_tensor(s2[:, :], s2[:, :], float(EP - 1), s1[:, :], ALU.add,
                                                    ALU.subtract), t)
            t = V(lambda e: e.tensor_tensor(s2[:, :], s2[:, :], s3[:, :], ALU.mult), t2)
            t = V(lambda e: e.tensor_tensor(s2[:, :], s2[:, :], s1[:, :], ALU.add), t)
            t = V(lambda e: e.tensor_copy(sum_row[:, :], s2[:, :]), t)
            V(lambda e: e.memset(keep[:, 0:1], 0.0))
            t = V(lambda e: e.tensor_tensor(keep[:, 1:EC], dst_f[:, 1:EC], dst_f[:, 0:EC - 1], ALU.is_equal),
                  t_f)
            V(lambda e: e.tensor_scalar(cut[:, :], keep[:, :], BIG, -BIG, ALU.mult, ALU.add), t)
            t = V(lambda e: e.tensor_copy(prev_f[:, :], prev_i[:, :]), t_prev)
            t = V(lambda e: e.tensor_tensor(keep_all[:, :], prev_f[:, :], dst_f[:, EC - 1:EC], ALU.is_equal), t)
            V(lambda e: e.tensor_scalar(cut_all[:, :], keep_all[:, :], BIG, -BIG, ALU.mult, ALU.add), t)
            t = V(lambda e: e.tensor_scalar(tmp_e[:, :], dst_f[:, :], dst_f[:, 0:1], None, ALU.is_equal,
                                            ALU.add, accum_out=hc[:, :]), t_f)
            t = V(lambda e: e.scalar_tensor_tensor(hc[:, :], hc[:, :], -1.0, own_f[:, :], ALU.add, ALU.add),
                  t, t_own)
            V(lambda e: e.tensor_copy(head_row[:, :], hc[:, :]), t)
            V(lambda e: e.tensor_copy(dst_first[:, :], dst[:, 0:1]))
            t = V(lambda e: e.tensor_copy(tmp_e[:, :], src[:, :]), t_idx)
            t2 = V(lambda e: e.tensor_copy(zero[:, :], typ[:, :]), (sem_zero[0], sem_zero[1]))
            t = V(lambda e: e.scalar_tensor_tensor(tmp_e[:, :], tmp_e[:, :], float(NREL), zero[:, :],
                                                   ALU.mult, ALU.add), t, t2)
            V(lambda e: e.tensor_copy(rel_row[:, :], tmp_e[:, :]), t)
            flow.barrier("expand_a")

        def groups_of(ap):
            return ap[0:EP, :].rearrange("(p c) w -> p c w", c=EC)

        def finish_crossing(name, sb, sums, W, tail, t_stored, L=None):
            WN = L.WN if L else D
            rest = WN - P
            head = sb(f"{name}_head", [P, W])
            xs = sb(f"{name}_state", [P, WN])
            ys = sb(f"{name}_decay", [P, WN])
            xT = sb(f"{name}_stateT", [P, 2, P])
            yT = sb(f"{name}_decayT", [P, 2, P])
            cT = sb(f"{name}_carryT", [P, 2, P + 1])
            sem_head = flow.dma_sem(f"{name}_head")
            sem_row = flow.dma_sem(f"{name}_row")
            t_head = dma("gpsimd", lambda e: e.indirect_dma_start(
                out=head[:, :], out_offset=None, in_=sums[0:EP, :],
                in_offset=bass.IndirectOffsetOnAxis(ap=head_row[:, 0:1], axis=0)), sem_head, *t_stored)
            t0 = V(lambda e: e.memset(cT[:, :, 0:1], 0.0))
            if L:
                H = L.H
                mrow = sb(f"{name}_mrow", [H, 2 * P])
                run = sb(f"{name}_run", [H, P + 1])
                mcut = sb(f"{name}_mcut", [P, H])
                m = sb(f"{name}_m", [P, 2 * H])
                ex = sb(f"{name}_ex", [P, 2 * H])
                mx = sb(f"{name}_mx", [P, H])
                tm = tail[:, L.M0:L.M0 + H]
                t = V(lambda e: e.tensor_copy(mcut[:, :], bc(cut_all[:, :], [P, H])))
                t = T(lambda e: e.transpose(ps[0:H, 0, P:2 * P], mcut[:, :], ident[:, :]), t)
                t = T(lambda e: e.transpose(ps[0:H, 0, 0:P], tm, ident[:, :]))
                t = V(lambda e: e.tensor_copy(mrow[:, :], ps[0:H, 0, 0:2 * P]), t)
                t1 = V(lambda e: e.memset(run[:, 0:1], -BIG))
                t = V(lambda e: e.tensor_tensor_scan(run[:, 1:P + 1], mrow[:, P:2 * P], mrow[:, 0:P], -BIG,
                                                     ALU.add, ALU.max), t, t1)
                T(lambda e: e.transpose(ps[:, 1, 0:H], run[:, 1:P + 1], ident[0:H, 0:H]), t)
                t = T(lambda e: e.transpose(ps[:, 1, H:2 * H], run[:, 0:P], ident[0:H, 0:H]), t)
                t = V(lambda e: e.tensor_copy(m[:, :], ps[:, 1, 0:2 * H]), t)
                V(lambda e: e.tensor_tensor(ex[:, 0:H], tm, m[:, 0:H], ALU.subtract), t)
                t = V(lambda e: e.tensor_tensor(ex[:, H:2 * H], m[:, H:2 * H], m[:, 0:H], ALU.subtract), t)
                t = V(lambda e: e.tensor_tensor(ex[:, H:2 * H], ex[:, H:2 * H], mcut[:, :], ALU.add), t)
                t = S(lambda e: e.activation(ex[:, :], ex[:, :], ACT.Exp), t)

                def heads(ap):
                    return ap.rearrange("p (h c) -> p h c", h=H)
                wide = [P, H, L.C + 1]
                V(lambda e: e.tensor_tensor(heads(xs[:, 0:L.NW]), heads(tail[:, 0:L.NW]),
                                            bc(ex[:, 0:H].unsqueeze(2), wide), ALU.mult), t)
                t = V(lambda e: e.tensor_copy(heads(ys[:, 0:L.NW]), bc(ex[:, H:2 * H].unsqueeze(2), wide)))
                if L.AE:
                    V(lambda e: e.tensor_copy(xs[:, L.NW:WN], tail[:, L.A0:L.W]))
                    t = V(lambda e: e.tensor_copy(ys[:, L.NW:WN], bc(keep_all[:, :], [P, L.AE])))
            else:
                V(lambda e: e.tensor_copy(xs[:, :], tail))
                t = V(lambda e: e.tensor_copy(ys[:, :], bc(keep_all[:, :], [P, D])))
            parts = [(0, 0, P)] + ([(1, P, rest)] if rest else [])
            for i, a, n in parts:
                T(lambda e, i=i, a=a, n=n: e.transpose(ps[0:n, 2, i * P:(i + 1) * P], xs[:, a:a + n],
                                                       ident[:, :]), t)
                t2 = T(lambda e, i=i, a=a, n=n: e.transpose(ps[0:n, 3, i * P:(i + 1) * P], ys[:, a:a + n],
                                                            ident[:, :]), t)
            for i, a, n in parts:
                V(lambda e, i=i, n=n: e.tensor_copy(xT[0:n, i, :], ps[0:n, 2, i * P:(i + 1) * P]), t2)
                t3 = V(lambda e, i=i, n=n: e.tensor_copy(yT[0:n, i, :], ps[0:n, 3, i * P:(i + 1) * P]), t2)
            for i, a, n in parts:
                t4 = V(lambda e, i=i, n=n: e.tensor_tensor_scan(cT[0:n, i, 1:P + 1], yT[0:n, i, :],
                                                                xT[0:n, i, :], 0.0, ALU.mult, ALU.add), t3)
            for i, a, n in parts:
                t5 = T(lambda e, i=i, a=a, n=n: e.transpose(ps[:, 4, a:a + n], cT[0:n, i, 0:P],
                                                            ident[0:n, 0:n]), t4, t0)
            if L:
                t = V(lambda e: e.tensor_tensor(mx[:, :], head[:, L.M0:L.M0 + H], m[:, H:2 * H], ALU.max),
                      t_head, t5)
                V(lambda e: e.tensor_tensor(ex[:, 0:H], head[:, L.M0:L.M0 + H], mx[:, :], ALU.subtract), t)
                t = V(lambda e: e.tensor_tensor(ex[:, H:2 * H], m[:, H:2 * H], mx[:, :], ALU.subtract), t)
                t = S(lambda e: e.activation(ex[:, :], ex[:, :], ACT.Exp), t)
                t1 = V(lambda e: e.tensor_tensor(heads(head[:, 0:L.NW]), heads(head[:, 0:L.NW]),
                                                 bc(ex[:, 0:H].unsqueeze(2), wide), ALU.mult), t)
                t2 = V(lambda e: e.tensor_tensor(heads(xs[:, 0:L.NW]), heads(ps[:, 4, 0:L.NW]),
                                                 bc(ex[:, H:2 * H].unsqueeze(2), wide), ALU.mult), t)
                t3 = V(lambda e: e.tensor_tensor(head[:, 0:L.NW], head[:, 0:L.NW], xs[:, 0:L.NW], ALU.add), t2)
                if L.AE:
                    V(lambda e: e.tensor_tensor(head[:, L.A0:L.W], head[:, L.A0:L.W], ps[:, 4, L.NW:WN],
                                                ALU.add))
                t3 = V(lambda e: e.tensor_copy(head[:, L.M0:L.M0 + H], mx[:, :]))
            else:
                t3 = V(lambda e: e.tensor_tensor(head[:, :], head[:, :], ps[:, 4, 0:D], ALU.add), t_head, t5)
            dma("sync", lambda e: e.dma_start(sums[EP:EP + P, :], head[:, :]), sem_row, t3)

        def attention_edges(L, sb, dst_l, attr=None, terms=None, edge_logit=None):
            H, C, NW = L.H, L.C, L.NW
            NS = 6 if attr is None else 5
            AHEAD = NS - 2
            rows = sb("edge_rows", [P, NS, GC, L.W])
            z = sb("z", [P, 2, GC, H])
            run = sb("run_max", [P, 2, GC + 1, H])
            wd = sb("weight_decay", [P, 2, 2 * GC, H])
            old = sb("old", [P, 2, H, C + 1])
            sem_g = [flow.dma_sem(f"gather{i}") for i in range(NS)]
            sem_s = [flow.dma_sem(f"store{i}") for i in range(NS)]
            tok = {}
            if attr is not None:
                NA = 4
                attrs = sb("attrs", [P, NA, GC, D])
                sem_al = [flow.dma_sem(f"attr_load{i}") for i in range(NA)]
                sem_as = [flow.dma_sem(f"attr_store{i}") for i in range(NA)]
            if terms is not None:
                feat_dram, proj = terms
                feats = sb("feats", [P, 2, GC, EF])
                prod = sb("feat_prod", [P, GC, B.H, EF])
                sem_f = [flow.dma_sem(f"feats{i}") for i in range(2)]

            def U(fn, *w):
                return op("vector", fn, *w)

            def cols(g):
                return slice(g * GC, (g + 1) * GC)

            def fetch(g):
                s = g % NS
                for c in range(GC):
                    tok["G", g] = dma("gpsimd", lambda e, c=c: e.indirect_dma_start(
                        out=rows[:, s, c, :], out_offset=None, in_=L.table,
                        in_offset=bass.IndirectOffsetOnAxis(ap=src[:, g * GC + c:g * GC + c + 1], axis=0)),
                        sem_g[s], past(tok, "S", g - NS), past(tok, "main", g - NS + 1))

            def fetch_extra(g):
                if attr is not None:
                    tok["AL", g] = dma("sync", lambda e: e.dma_start(
                        attrs[:, g % NA, :, :], attr[:, cols(g), :]), sem_al[g % NA],
                        past(tok, "AS", g - NA), past(tok, "attr", g - NA + 1))
                if terms is not None:
                    tok["F", g] = dma("sync", lambda e: e.dma_start(
                        feats[:, g % 2, :, :], feat_dram[:, cols(g), :]), sem_f[g % 2], past(tok, "ae", g - 2))

            def logits(g):
                s, b = g % NS, g % 2
                R = rows[:, s, :, :]
                tz = U(lambda e: e.tensor_tensor(z[:, b, :, :], R[:, :, L.M0:L.M0 + H], dst_l[:, cols(g), :],
                                                 ALU.add), tok["G", g])
                yield
                if L.AE:
                    tz = U(lambda e: e.tensor_tensor(z[:, b, :, :], z[:, b, :, :], edge_logit[:, cols(g), :],
                                                     ALU.add), tz)
                    yield
                tz = U(lambda e: e.scalar_tensor_tensor(z[:, b, :, :], z[:, b, :, :], SLOPE, z[:, b, :, :],
                                                        ALU.mult, ALU.max), tz)
                yield
                if g == 0:
                    t0 = U(lambda e: e.memset(run[:, b, 0:1, :], -BIG))
                else:
                    t0 = U(lambda e: e.tensor_copy(run[:, b, 0:1, :], run[:, 1 - b, GC:GC + 1, :]),
                           tok["run", g - 1])
                yield
                for h in range(H):
                    init = -BIG if g == 0 else run[:, 1 - b, GC, h:h + 1]
                    tr = U(lambda e, h=h, init=init: e.tensor_tensor_scan(
                        run[:, b, 1:GC + 1, h], cut[:, cols(g)], z[:, b, :, h], init, ALU.add, ALU.max),
                        tz, past(tok, "run", g - 1))
                    yield
                tok["run", g] = tr
                if L.AE:
                    for h in range(H):
                        at = L.A0 + h
                        init = 0.0 if g == 0 else rows[:, (g - 1) % NS, GC - 1, at:at + 1]
                        t_ae = U(lambda e, h=h, at=at, init=init: e.tensor_tensor_scan(
                            R[:, :, at], keep[:, cols(g)], edge_logit[:, cols(g), h], init, ALU.mult,
                            ALU.add), past(tok, "ae_run", g - 1))
                        yield
                    tok["ae_run", g] = t_ae
                U(lambda e: e.tensor_tensor(wd[:, b, 0:GC, :], z[:, b, :, :], run[:, b, 1:GC + 1, :],
                                            ALU.subtract), tr)
                yield
                td = U(lambda e: e.tensor_tensor(wd[:, b, GC:2 * GC, :], run[:, b, 0:GC, :],
                                                 run[:, b, 1:GC + 1, :], ALU.subtract), tr, t0)
                yield
                td = U(lambda e: e.tensor_tensor(
                    wd[:, b, GC:2 * GC, :], wd[:, b, GC:2 * GC, :],
                    bc(cut[:, cols(g)].unsqueeze(2), [P, GC, H]), ALU.add), td)
                tok["exp", g] = S(lambda e: e.activation(wd[:, b, :, :], wd[:, b, :, :], ACT.Exp), td)
                yield
                U(lambda e: e.tensor_copy(R[:, :, L.M0:L.M0 + H], run[:, b, 1:GC + 1, :]), tr)
                if terms is not None:
                    yield
                    t = U(lambda e: e.tensor_tensor(
                        prod[:, :, :, :], bc(feats[:, b, :, :].unsqueeze(2), [P, GC, B.H, EF]),
                        bc(proj[:, :, :].unsqueeze(1), [P, GC, B.H, EF]), ALU.mult), tok["F", g])
                    yield
                    tok["ae", g] = U(lambda e: e.tensor_reduce(edge_logit[:, cols(g), :], prod[:, :, :, :], AX,
                                                               ALU.add), t)

            def running_sums(g):
                s, b = g % NS, g % 2
                R = rows[:, s, :, :]
                num = R[:, :, 0:NW].rearrange("p c (h k) -> p c h k", h=H)
                if H == 1:
                    weighted = [S(lambda e, c=c: e.activation(R[:, c, 0:NW], R[:, c, 0:NW], ACT.Copy,
                                                              scale=wd[:, b, c, :]), tok["exp", g])
                                for c in range(GC)]
                    t = past(tok, "main", g - 1)
                else:
                    t = U(lambda e: e.tensor_tensor(num, num, bc(wd[:, b, 0:GC, :].unsqueeze(3),
                                                                 [P, GC, H, C + 1]), ALU.mult),
                          tok["exp", g], past(tok, "main", g - 1))
                    yield
                t_a = past(tok, "attr", g - 1)
                for c in range(GC):
                    if g == 0 and c == 0:
                        continue
                    prev = rows[:, s, c - 1, 0:NW] if c else rows[:, (g - 1) % NS, GC - 1, 0:NW]
                    if H == 1:
                        t = U(lambda e, c=c, prev=prev: e.scalar_tensor_tensor(
                            R[:, c, 0:NW], prev, wd[:, b, GC + c, :], R[:, c, 0:NW], ALU.mult, ALU.add),
                            t, weighted[c])
                        yield
                    else:
                        t = U(lambda e, c=c, prev=prev: e.tensor_tensor(
                            old[:, c % 2, :, :], prev.rearrange("p (h k) -> p h k", h=H),
                            bc(wd[:, b, GC + c, :].unsqueeze(2), [P, H, C + 1]), ALU.mult), t)
                        yield
                        t = U(lambda e, c=c: e.tensor_tensor(
                            R[:, c, 0:NW], R[:, c, 0:NW], old[:, c % 2, :, :].rearrange("p h k -> p (h k)"),
                            ALU.add), t)
                        yield
                    if attr is not None:
                        a = attrs[:, g % NA, c, :]
                        pa = attrs[:, g % NA, c - 1, :] if c else attrs[:, (g - 1) % NA, GC - 1, :]
                        t_a = U(lambda e, c=c, a=a, pa=pa: e.scalar_tensor_tensor(
                            a, pa, keep[:, g * GC + c:g * GC + c + 1], a, ALU.mult, ALU.add),
                            tok["AL", g], t_a)
                        yield
                tok["main", g], tok["attr", g] = t, t_a

            def store(g):
                tok["S", g] = dma("sync", lambda e: e.dma_start(
                    groups_of(L.sums)[:, cols(g), :], rows[:, g % NS, :, :]), sem_s[g % NS], tok["main", g])
                if attr is not None:
                    tok["AS", g] = dma("sync", lambda e: e.dma_start(
                        groups_of(sums_attr)[:, cols(g), :], attrs[:, g % NA, :, :]), sem_as[g % NA],
                        tok["attr", g])

            for g in range(min(AHEAD, NG)):
                fetch(g)
            for g in range(min(2, NG)):
                fetch_extra(g)
            for _ in logits(0):
                pass
            for g in range(NG):
                if g + AHEAD < NG:
                    fetch(g + AHEAD)
                if g + 2 < NG:
                    fetch_extra(g + 2)
                both = [running_sums(g)] + ([logits(g + 1)] if g + 1 < NG else [])
                while both:
                    both = [x for x in both if next(x, "over") != "over"]
                store(g)
            last = (NG - 1) % NS
            t_stored = [tok["S", g] for g in range(max(0, NG - NS), NG)]
            finish_crossing("att", sb, L.sums, L.W, rows[:, last, GC - 1, :], t_stored, L)
            if attr is not None:
                t_as = [tok["AS", g] for g in range(max(0, NG - NA), NG)]
                finish_crossing("attr", sb, sums_attr, D, attrs[:, (NG - 1) % NA, GC - 1, :],
                                t_as + [flow.last("vector")])

        def node_rows(sb, name, sums, W, depth=2):
            buf = sb(name, [P, depth, JB, W])
            sems = [flow.dma_sem(f"{name}{i}") for i in range(depth)]

            def gather(k, *w):
                for b in range(JB):
                    j = k * JB + b
                    t = dma("gpsimd", lambda e, b=b, j=j: e.indirect_dma_start(
                        out=buf[:, k % depth, b, :], out_offset=None, in_=sums,
                        in_offset=bass.IndirectOffsetOnAxis(ap=sum_row[:, j:j + 1], axis=0)),
                        sems[k % depth], *w)
                return t
            return buf, gather

        def attention_nodes(L, sb, node_l, out_of):
            H, C = L.H, L.C
            R, gather = node_rows(sb, "node_sums", L.sums, L.W)
            own = sb("own_rows", [P, 2, JB, L.W])
            z = sb("self_logit", [P, 2, JB, H])
            ex = sb("self_ex", [P, 2, 2, JB, H])
            mx = sb("self_max", [P, 2, JB, H])
            den = sb("den", [P, 2, JB, H])
            sem_own = [flow.dma_sem(f"own{i}") for i in range(2)]
            tok = {}
            bj = [P, JB, H]

            def fetch(k):
                tok["R", k] = gather(k, past(tok, "O", k - 2))
                tok["own", k] = dma("sync", lambda e: e.dma_start(
                    own[:, k % 2, :, :],
                    L.table.rearrange("(p j) w -> p j w", j=NJ)[:, k * JB:(k + 1) * JB, :]),
                    sem_own[k % 2], past(tok, "O", k - 2))

            def logit(k):
                s, j = k % 2, slice(k * JB, (k + 1) * JB)
                zz, r, m = z[:, s, :, :], R[:, s, :, :], mx[:, s, :, :]
                t = V(lambda e: e.tensor_tensor(zz, own[:, s, :, L.M0:L.M0 + H], node_l[:, j, :], ALU.add),
                      tok["own", k])
                if L.AE:
                    t2 = V(lambda e: e.tensor_tensor(m, r[:, :, L.A0:L.W], bc(inv_deg[:, j].unsqueeze(2), bj),
                                                     ALU.mult), tok["R", k])
                    t = V(lambda e: e.tensor_tensor(zz, zz, m, ALU.add), t, t2)
                t = V(lambda e: e.scalar_tensor_tensor(zz, zz, SLOPE, zz, ALU.mult, ALU.max), t)
                rm = r[:, :, L.M0:L.M0 + H]
                t2 = V(lambda e: e.tensor_tensor(rm, rm, bc(has[:, j].unsqueeze(2), bj), ALU.mult), tok["R", k])
                t2 = V(lambda e: e.tensor_tensor(rm, rm, bc(no_edge[:, j].unsqueeze(2), bj), ALU.add), t2)
                t = V(lambda e: e.tensor_tensor(m, rm, zz, ALU.max), t, t2)
                V(lambda e: e.tensor_tensor(ex[:, s, 0, :, :], rm, m, ALU.subtract), t)
                t = V(lambda e: e.tensor_tensor(ex[:, s, 1, :, :], zz, m, ALU.subtract), t)
                tok["E", k] = S(lambda e: e.activation(ex[:, s, :, :, :], ex[:, s, :, :, :], ACT.Exp), t)

            def join(k):
                s = k % 2
                wide = [P, JB, H, C + 1]

                def heads(ap):
                    return ap[:, :, 0:L.NW].rearrange("p j (h c) -> p j h c", h=H)
                a, b = heads(R[:, s, :, :]), heads(own[:, s, :, :])
                V(lambda e: e.tensor_tensor(a, a, bc(ex[:, s, 0, :, :].unsqueeze(3), wide), ALU.mult),
                  tok["E", k])
                t = V(lambda e: e.tensor_tensor(b, b, bc(ex[:, s, 1, :, :].unsqueeze(3), wide), ALU.mult))
                t = V(lambda e: e.tensor_tensor(a, a, b, ALU.add), t)
                if L.AE:
                    t = V(lambda e: e.tensor_scalar(den[:, s, :, :], a[:, :, :, C], 1e-16, None, ALU.add), t)
                    t = V(lambda e: e.reciprocal(den[:, s, :, :], den[:, s, :, :]), t)
                else:
                    t = V(lambda e: e.reciprocal(den[:, s, :, :], a[:, :, :, C]), t)
                t = V(lambda e: e.tensor_tensor(
                    out_of(k).rearrange("p j (h c) -> p j h c", h=H), a[:, :, :, 0:C],
                    bc(den[:, s, :, :].unsqueeze(3), [P, JB, H, C]), ALU.mult), t)
                tok["O", k] = t

            return [fetch, logit, join], tok

        def over_nodes(ap):
            return bc(ap.unsqueeze(1), [P, JB, D])

        def chunk(ap, k):
            return ap[:, k * JB:(k + 1) * JB, :]

        until_edges_b = ExitStack()
        edge_logit = buffers(until_edges_b)("edge_logit", [P, EC, B.H])
        with ExitStack() as local:
            sb = buffers(local)
            dst_l = sb("dst_logit", [P, EC, A.H])
            proj = sb("edge_proj", [P, B.H, EF])
            weights = ExitStack()
            we = buffers(weights)("w_edge", [P, EF, B.H, B.C])
            att_e = buffers(weights)("att_edge", [P, B.H, B.C])
            sem_we = flow.dma_sem("w_edge")
            dma("sync", lambda e: e.dma_start(
                we[:, :, :, :].rearrange("p k h c -> p (k h c)"),
                io["b_w_edge"].rearrange("k d -> (k d)").unsqueeze(0).broadcast_to([P, EF * D])), sem_we)
            t = dma("sync", lambda e: e.dma_start(
                att_e[:, :, :].rearrange("p h c -> p (h c)"),
                io["b_att_edge"].rearrange("h c -> (h c)").unsqueeze(0).broadcast_to([P, D])), sem_we)
            t = V(lambda e: e.tensor_tensor(we[:, :, :, :], we[:, :, :, :],
                                            bc(att_e[:, :, :].unsqueeze(1), [P, EF, B.H, B.C]), ALU.mult), t)
            V(lambda e: e.tensor_reduce(proj[:, :, :].rearrange("p h k -> p k h"), we[:, :, :, :], AX,
                                        ALU.add), t)
            expand_dst_logits(A, dst_l)
            flow.barrier("edges_a")
            weights.close()
            attention_edges(A, sb, dst_l, attr=io["ea128"], terms=(io["ea13"], proj), edge_logit=edge_logit)
            flow.barrier("nodes_a")

        with ExitStack() as local:
            sb = buffers(local)
            agg = sb("agg", [P, NJ, D])
            bn_par = sb("bn_par", [P, 3, D])
            mean = sb("bn_mean", [P, D])
            scale = sb("bn_scale", [P, D])
            square = sb("square", [P, 2, JB, D])
            sem_par = flow.dma_sem("par")
            ext_b, t_ext_b = load_extended_weights(B, sb, io["b_w"], io["b_att_src"].rearrange(
                "h c -> (h c)").unsqueeze(0), io["b_att_dst"].rearrange("h c -> (h c)").unsqueeze(0))
            for i, name in enumerate(("a_bias", "a_gamma", "a_beta")):
                t_par = dma("sync", lambda e, i=i, name=name: e.dma_start(
                    bn_par[:, i, :], io[name].broadcast_to([P, D])), sem_par)
            stages, tok = attention_nodes(A, sb, node_a, lambda k: chunk(agg, k))

            def rows_valid(j):
                return (n_nodes - j + NJ - 1) // NJ

            def column_sums(k, data, bank, *w):
                for b in range(JB):
                    j = k * JB + b
                    K = rows_valid(j)
                    t = T(lambda e, b=b, j=j, K=K: e.matmul(
                        ps[:, bank, 0:D], ones[0:K, :], data[0:K, b, :], start=(j == 0),
                        stop=(j == NJ - 1)), *w)
                return t

            def add_bias(k):
                tok["B", k] = V(lambda e: e.tensor_tensor(chunk(agg, k), chunk(agg, k),
                                                          over_nodes(bn_par[:, 0, :]), ALU.add),
                                tok["O", k], t_par)
                tok["sum"] = column_sums(k, chunk(agg, k), 0, tok["B", k])
            skewed(stages + [add_bias], NK)
            t = V(lambda e: e.tensor_scalar(mean[:, :], ps[:, 0, 0:D], 1.0 / n_nodes, None, ALU.mult),
                  tok["sum"])
            tok["mean"] = t

            def centre(k):
                tok["c", k] = V(lambda e: e.tensor_tensor(chunk(agg, k), chunk(agg, k),
                                                          over_nodes(mean[:, :]), ALU.subtract),
                                tok["mean"])
                t = S(lambda e: e.activation(square[:, k % 2, :, :], chunk(agg, k), ACT.Square),
                      tok["c", k], past(tok, "q", k - 2))
                tok["q", k] = column_sums(k, square[:, k % 2, :, :], 1, t)
            skewed([centre], NK)
            t = V(lambda e: e.tensor_scalar(scale[:, :], ps[:, 1, 0:D], 1.0 / n_nodes, EPS, ALU.mult,
                                            ALU.add), tok["q", NK - 1])
            t = S(lambda e: e.activation(scale[:, :], scale[:, :], ACT.Sqrt), t)
            t = V(lambda e: e.reciprocal(scale[:, :], scale[:, :]), t)
            tok["scale"] = V(lambda e: e.tensor_tensor(scale[:, :], scale[:, :], bn_par[:, 1, :], ALU.mult), t)

            def residual(k):
                t = V(lambda e: e.tensor_tensor(chunk(agg, k), chunk(agg, k), over_nodes(scale[:, :]),
                                                ALU.mult), tok["scale"])
                t = V(lambda e: e.tensor_tensor(chunk(agg, k), chunk(agg, k), over_nodes(bn_par[:, 2, :]),
                                                ALU.add), t)
                tok["x", k] = V(lambda e: e.scalar_tensor_tensor(chunk(x, k), chunk(agg, k), 0.0,
                                                                 chunk(x, k), ALU.max, ALU.add), t)
            sem_scatter = flow.dma_sem("scatter")
            table_b = table_stages(B, sb, ext_b, t_ext_b, node_b, lambda k: tok["x", k], sem_scatter)
            skewed([residual] + table_b, NK)
            store_node_logits(B, node_b, flow.last("scalar"))
            flow.barrier("expand_b")

        with ExitStack() as local:
            sb = buffers(local)
            dst_l = sb("dst_logit", [P, EC, B.H])
            expand_dst_logits(B, dst_l)
            flow.barrier("edges_b")
            attention_edges(B, sb, dst_l, edge_logit=edge_logit)
            flow.barrier("nodes_b")
        until_edges_b.close()

        self_out = dram("self_out", [NP, D])
        with ExitStack() as local:
            sb = buffers(local)
            par = sb("par", [P, 5, D])
            w1 = sb("w1", [P, 3, D])
            w2 = sb("w2", [P, D])
            w3 = sb("w3", [P, D])
            w_rel = sb("w_rel", [P, NREL, D])
            w_self = sb("w_self", [P, D])
            u0 = sb("u0", [P, 1])
            b12 = sb("b12", [P, 3])
            sem_par = flow.dma_sem("par")
            for i, name in enumerate(("b_bias", "b_gamma", "b_beta", "c_b3", "d_self_b")):
                dma("sync", lambda e, i=i, name=name: e.dma_start(
                    par[:, i, :], io[name].broadcast_to([P, D])), sem_par)
            dma("scalar", lambda e: e.dma_start(w1[:, :, :], io["c_w1"].rearrange("(a k) d -> k a d", k=P)), sem_par)
            dma("scalar", lambda e: e.dma_start(w2[:, :], io["c_w2"]), sem_par)
            dma("scalar", lambda e: e.dma_start(w3[:, :], io["c_w3"]), sem_par)
            dma("scalar", lambda e: e.dma_start(w_rel[:, :, :], io["W_rel"].rearrange("r k d -> k r d")), sem_par)
            dma("scalar", lambda e: e.dma_start(w_self[:, :], io["d_self_wT"]), sem_par)
            dma("scalar", lambda e: e.dma_start(u0[:, :], io["c_u"]), sem_par)
            dma("scalar", lambda e: e.dma_start(b12[:, 0:1], io["c_b1"]), sem_par)
            t_par = dma("scalar", lambda e: e.dma_start(b12[:, 1:2], io["c_b2"]), sem_par)
            t = T(lambda e: e.matmul(ps[:, 0, 0:1], w1[:, 2, :], u0[:, :], start=True, stop=True), t_par)
            t_b1 = V(lambda e: e.tensor_tensor(b12[:, 2:3], b12[:, 0:1], ps[:, 0, 0:1], ALU.add), t)

            out_b = sb("out_b", [P, 3, JB, D])
            h1 = sb("h1", [P, 2, JB, D])
            hn2, hn3 = sb("hn2", [P, 2, JB, D]), sb("hn3", [P, 2, JB, D])
            hT2, hT3, aT = sb("hT2", [P, 2, JB * P]), sb("hT3", [P, 2, JB * P]), sb("aT", [P, 2, JB * P])
            mid1, mid2 = sb("mid1", [P, 2, JB * P]), sb("mid2", [P, 2, JB * P])
            rel = sb("rel", [P, 2, NREL, D])
            own_part = sb("self_part", [P, 2, JB, D])
            sem_rel = [flow.dma_sem(f"rel{i}") for i in range(2)]
            sem_own_part = [flow.dma_sem(f"self_part{i}") for i in range(2)]
            stages, tok = attention_nodes(B, sb, node_b, lambda k: out_b[:, k % 3, :, :])
            sums_a, gather_a = node_rows(sb, "attr_sums", sums_attr, D)
            bank_free = {i: t_b1 for i in range(8)}
            halves = [(0, min(4, JB))] + ([(4, JB - 4)] if JB > 4 else [])
            pairs = cycle([(0, 1), (2, 3)])
            waiting = []

            def read_later(fn):
                read_now()
                waiting.append(fn)

            def read_now():
                if waiting:
                    waiting.pop()()

            class Norm:
                def __init__(self, name):
                    self.name = name
                    self.mv, self.std = sb(f"{name}_mv", [P, 2, JB, 2]), sb(f"{name}_std", [P, 2, JB])
                    self.rs, self.nb = sb(f"{name}_rs", [P, 2, JB]), sb(f"{name}_nb", [P, 2, JB])

                def begin(self, k, data, t):
                    s = k % 2
                    for b in range(JB):
                        t2 = op("vector", lambda e, b=b: e.bn_stats(stats[:, s, b, :], data[:, b, :]), t)
                    for b in range(JB):
                        op("vector", lambda e, b=b: e.bn_aggr(self.mv[:, s, b, :], stats[:, s, b, :]), t2)
                    t3 = V(lambda e: e.tensor_scalar(self.std[:, s, :], self.mv[:, s, :, 1], EPS, None, ALU.add))
                    tok[self.name, "root", k] = S(lambda e: e.activation(self.std[:, s, :], self.std[:, s, :],
                                                                         ACT.Sqrt), t3)

                def end(self, k, out, data, func, *w):
                    s = k % 2
                    t = V(lambda e: e.reciprocal(self.rs[:, s, :], self.std[:, s, :]),
                          tok[self.name, "root", k], tok.get((self.name, "out", k - 2)))
                    t = V(lambda e: e.scalar_tensor_tensor(self.nb[:, s, :], self.mv[:, s, :, 0], -1.0,
                                                           self.rs[:, s, :], ALU.mult, ALU.mult), t)
                    for b in range(JB):
                        t2 = S(lambda e, b=b: e.activation(out[:, b, :], data[:, b, :], func,
                                                           bias=self.nb[:, s, b:b + 1],
                                                           scale=self.rs[:, s, b:b + 1]), t, *w)
                    tok[self.name, "out", k] = t2
                    return t2

            norm1, norm2, norm3 = Norm("norm1"), Norm("norm2"), Norm("norm3")

            def turned(k, name, out, data, *w):
                banks, t_half = next(pairs), []
                for bank, (i, n) in zip(banks, halves):
                    for m in range(n):
                        t = T(lambda e, bank=bank, i=i, m=m: e.transpose(
                            ps[:, bank, m * P:(m + 1) * P], data[:, i + m, :], ident[:, :]),
                            bank_free[bank], *w)
                    t_half.append(t)
                tok["T" + name, k] = t

                def read():
                    for at, (bank, (i, n)) in enumerate(zip(banks, halves)):
                        o = out[:, i * P:(i + n) * P]
                        if at:
                            bank_free[bank] = S(lambda e, bank=bank, o=o, n=n: e.activation(
                                o, ps[:, bank, 0:n * P], ACT.Copy), t_half[at])
                        else:
                            bank_free[bank] = op("vector", lambda e, bank=bank, o=o, n=n: e.tensor_copy(
                                o, ps[:, bank, 0:n * P]), t_half[at])
                        tok["turned" + name, at, k] = bank_free[bank]
                read_later(read)

            def both(name, k):
                return [tok["turned" + name, at, k] for at in range(len(halves))]

            def residual_input(k):
                s, j = k % 2, slice(k * JB, (k + 1) * JB)
                stages_join(k)
                t = norm_relu(k, h1[:, s, :, :], chunk(x, k), mean_rs[:, j], mean_nb[:, j],
                              past(tok, "y", k - 2))
                tok["h1", k] = op("gpsimd", lambda e: e.tensor_tensor(
                    h1[:, s, :, :], h1[:, s, :, :], over_nodes(par[:, 0, :]), ALU.add), t, t_par)

            def residual_1(k):
                y = out_b[:, k % 3, :, :]
                t = op("vector", lambda e: e.tensor_tensor(y, y, h1[:, k % 2, :, :], ALU.add),
                       tok["O", k], tok["h1", k])
                tok["y", k] = t
                norm1.begin(k, y, t)

            def norm_1(k):
                y = out_b[:, k % 3, :, :]
                norm1.end(k, y, y, ACT.Identity)

            def residual_2(k):
                y = out_b[:, k % 3, :, :]
                t = V(lambda e: e.tensor_tensor(y, y, over_nodes(par[:, 1, :]), ALU.mult),
                      tok["norm1", "out", k])
                t = V(lambda e: e.tensor_tensor(y, y, over_nodes(par[:, 2, :]), ALU.add), t)
                t = V(lambda e: e.scalar_tensor_tensor(chunk(x, k), y, 0.0, chunk(x, k), ALU.max, ALU.add), t)
                norm2.begin(k, chunk(x, k), t)

            def norm_2(k):
                norm2.end(k, hn2[:, k % 2, :, :], chunk(x, k), ACT.Relu, past(tok, "Th2", k - 2))
                tok["a", k] = gather_a(k, past(tok, "Ta", k - 2))

            def turn_2(k):
                turned(k, "h2", hT2[:, k % 2, :], hn2[:, k % 2, :, :], tok["norm2", "out", k])
                j = slice(k * JB, (k + 1) * JB)
                tok["am", k] = op("gpsimd", lambda e: e.tensor_tensor(
                    sums_a[:, k % 2, :, :], sums_a[:, k % 2, :, :], bc(has[:, j].unsqueeze(2), [P, JB, D]),
                    ALU.mult), tok["a", k])
                tok["xb", k] = op("gpsimd", lambda e: e.tensor_tensor(
                    chunk(x, k), chunk(x, k), over_nodes(par[:, 3, :]), ALU.add), tok["norm2", "out", k])

            def turn_sums(k):
                turned(k, "a", aT[:, k % 2, :], sums_a[:, k % 2, :, :], tok["am", k])

            def product(k, name, weights, out, bias, *w):
                banks, t_half = next(pairs), []
                for bank, (i, n) in zip(banks, halves):
                    c = slice(i * P, (i + n) * P)
                    for m, (wt, data) in enumerate(weights):
                        t = T(lambda e, bank=bank, n=n, c=c, m=m, wt=wt, data=data: e.matmul(
                            ps[:, bank, 0:n * P], wt, data[:, c], start=(m == 0),
                            stop=(m == len(weights) - 1)), bank_free[bank], *w)
                    t_half.append(t)

                def read():
                    for t, bank, (i, n) in zip(t_half, banks, halves):
                        c = slice(i * P, (i + n) * P)
                        tok[name, k] = bank_free[bank] = S(lambda e, bank=bank, n=n, c=c: e.activation(
                            out[:, c], ps[:, bank, 0:n * P], ACT.Relu, bias=bias), t)
                read_later(read)

            def hidden_1(k):
                s = k % 2
                product(k, "m1", [(w1[:, 0, :], hT2[:, s, :]), (w1[:, 1, :], aT[:, s, :])],
                        mid1[:, s, :], b12[:, 2:3], *both("h2", k), *both("a", k))

            def hidden_2(k):
                s = k % 2
                product(k, "m2", [(w2[:, :], mid1[:, s, :])], mid2[:, s, :], b12[:, 1:2], tok["m1", k])

            def mlp_out(k):
                s = k % 2
                banks, t_half = next(pairs), []
                for bank, (i, n) in zip(banks, halves):
                    for m in range(n):
                        t = T(lambda e, bank=bank, i=i, m=m: e.matmul(
                            ps[:, bank, m * P:(m + 1) * P], mid2[:, s, (i + m) * P:(i + m + 1) * P],
                            w3[:, :], start=True, stop=True), bank_free[bank], tok["m2", k])
                    t_half.append(t)

                def read():
                    for t, bank, (i, n) in zip(t_half, banks, halves):
                        xs = x[:, k * JB + i:k * JB + i + n, :].rearrange("p j d -> p (j d)")
                        bank_free[bank] = op("vector", lambda e, bank=bank, n=n, xs=xs: e.tensor_tensor(
                            xs, xs, ps[:, bank, 0:n * P], ALU.add), t, tok["xb", k])
                    norm3.begin(k, chunk(x, k), bank_free[bank])
                read_later(read)

            def norm_3(k):
                norm3.end(k, hn3[:, k % 2, :, :], chunk(x, k), ACT.Relu, past(tok, "Th3", k - 2))

            def turn_3(k):
                turned(k, "h3", hT3[:, k % 2, :], hn3[:, k % 2, :, :], tok["norm3", "out", k])

            def relations(k):
                s, half = k % 2, NREL // 2
                late = None
                for b in range(JB):
                    j = k * JB + b
                    r, bank = j % 2, 4 + 2 * (j % 2)
                    block = hT3[:, s, b * P:(b + 1) * P]
                    for i in range(2):
                        t = T(lambda e, i=i, block=block, bank=bank: e.matmul(
                            ps[:, bank + i, 0:half * D], block,
                            w_rel[:, i * half:(i + 1) * half, :].rearrange("p r d -> p (r d)"),
                            start=True, stop=True), *both("h3", k), bank_free[bank + i])
                    if late:
                        late()

                    def late(j=j, r=r, bank=bank, t=t):
                        t1 = bank_free[bank] = S(lambda e: e.activation(
                            rel[:, r, 0:half, :].rearrange("p r d -> p (r d)"),
                            ps[:, bank, 0:half * D], ACT.Copy), t, past(tok, "rel", j - 2))
                        t2 = bank_free[bank + 1] = op("vector", lambda e: e.tensor_copy(
                            rel[:, r, half:NREL, :].rearrange("p r d -> p (r d)"),
                            ps[:, bank + 1, 0:half * D]), t, past(tok, "rel", j - 2))
                        tok["rel", j] = dma("sync", lambda e: e.dma_start(
                            table_rel.rearrange("(p j r) d -> p j (r d)", j=NJ, r=NREL)[:, j, :],
                            rel[:, r, :, :].rearrange("p r d -> p (r d)")), sem_rel[r], t1, t2)
                    yield
                late()
                banks, t_half = next(pairs), []
                for bank, (i, n) in zip(banks, halves):
                    for m in range(n):
                        t = T(lambda e, b=i + m, m=m, bank=bank: e.matmul(
                            ps[:, bank, m * P:(m + 1) * P], hT3[:, s, b * P:(b + 1) * P],
                            w_self[:, :], start=True, stop=True), bank_free[bank])
                    t_half.append(t)

                def read():
                    for t, bank, (i, n) in zip(t_half, banks, halves):
                        so = own_part[:, s, i:i + n, :]
                        t3 = bank_free[bank] = op("vector", lambda e, bank=bank, n=n, so=so: e.tensor_tensor(
                            so, ps[:, bank, 0:n * P].rearrange("p (n d) -> p n d", d=D),
                            bc(par[:, 4, :].unsqueeze(1), [P, n, D]), ALU.add),
                            t, past(tok, "self_part", k - 2))
                    tok["self_part", k] = dma("sync", lambda e: e.dma_start(
                        chunk(self_out.rearrange("(p j) d -> p j d", j=NJ), k), own_part[:, s, :, :]),
                        sem_own_part[s], t3)
                read_later(read)

            stages_join = stages[2]
            before = stages[:2] + [residual_input, residual_1, norm_1, residual_2, norm_2, turn_2,
                                   turn_sums, hidden_1, hidden_2, mlp_out, norm_3, turn_3]
            for step in range(NK + len(before)):
                k_last = step - len(before)
                blocks = relations(k_last) if k_last >= 0 else iter(())
                for s in reversed(range(len(before))):
                    if 0 <= step - s < NK:
                        before[s](step - s)
                        if s % 2:
                            next(blocks, None)
                for _ in blocks:
                    pass
                read_now()
            flow.barrier("edges_rel")

        with ExitStack() as local:
            sb = buffers(local)
            NS, AHEAD = 6, 4
            rows = sb("edge_rows", [P, NS, GC, D])
            sem_g = [flow.dma_sem(f"gather{i}") for i in range(NS)]
            sem_s = [flow.dma_sem(f"store{i}") for i in range(NS)]
            tok = {}

            def fetch(g):
                s = g % NS
                for c in range(GC):
                    tok["G", g] = dma("gpsimd", lambda e, c=c: e.indirect_dma_start(
                        out=rows[:, s, c, :], out_offset=None, in_=table_rel,
                        in_offset=bass.IndirectOffsetOnAxis(ap=rel_row[:, g * GC + c:g * GC + c + 1],
                                                            axis=0)),
                        sem_g[s], past(tok, "S", g - NS), past(tok, "main", g - NS + 1))
            for g in range(min(AHEAD, NG)):
                fetch(g)
            t = None
            for g in range(NG):
                if g + AHEAD < NG:
                    fetch(g + AHEAD)
                s = g % NS
                for c in range(GC):
                    if g or c:
                        prev = rows[:, s, c - 1, :] if c else rows[:, (g - 1) % NS, GC - 1, :]
                        t = V(lambda e, s=s, c=c, g=g, prev=prev: e.scalar_tensor_tensor(
                            rows[:, s, c, :], prev, keep[:, g * GC + c:g * GC + c + 1], rows[:, s, c, :],
                            ALU.mult, ALU.add), tok["G", g], t)
                tok["main", g] = t
                tok["S", g] = dma("sync", lambda e, g=g, s=s: e.dma_start(
                    groups_of(sums_rel)[:, g * GC:(g + 1) * GC, :], rows[:, s, :, :]), sem_s[s], t)
            finish_crossing("rel", sb, sums_rel, D, rows[:, (NG - 1) % NS, GC - 1, :],
                            [tok["S", g] for g in range(max(0, NG - NS), NG)])
            flow.barrier("nodes_rel")

        with ExitStack() as local:
            sb = buffers(local)
            R, gather = node_rows(sb, "node_sums", sums_rel, D, 3)
            sem_out = [flow.dma_sem(f"out{i}") for i in range(3)]
            tok = {}

            own3 = sb("self_part", [P, 3, JB, D])
            sem_self = [flow.dma_sem(f"self{i}") for i in range(3)]

            def fetch_rel(k):
                tok["R", k] = gather(k, past(tok, "S", k - 3))
                tok["self", k] = dma("sync", lambda e: e.dma_start(
                    own3[:, k % 3, :, :], chunk(self_out.rearrange("(p j) d -> p j d", j=NJ), k)),
                    sem_self[k % 3], past(tok, "S", k - 3))

            def last(k):
                r, j = R[:, k % 3, :, :], slice(k * JB, (k + 1) * JB)
                t = V(lambda e: e.tensor_tensor(r, r, bc(inv_deg[:, j].unsqueeze(2), [P, JB, D]), ALU.mult),
                      tok["R", k])
                t = V(lambda e: e.tensor_tensor(r, r, own3[:, k % 3, :, :], ALU.add), t, tok["self", k])
                t = V(lambda e: e.scalar_tensor_tensor(r, r, 0.0, chunk(x, k), ALU.max, ALU.add), t)
                tok["S", k] = dma("sync", lambda e: e.dma_start(
                    chunk(io["out"].rearrange("(p j) d -> p j d", j=NJ), k), r), sem_out[k % 3], t)
            skewed([fetch_rel, last], NK)
            flow.barrier("end")

        block = ctx.enter_context(nc.Block())

        @block.sync
        def _(eng):
            flow.play("sync", eng)

        @block.scalar
        def _(eng):
            flow.play("scalar", eng)

        @block.gpsimd
        def _(eng):
            flow.play("gpsimd", eng)

        @block.vector
        def _(eng):
            flow.play("vector", eng)

        @block.tensor
        def _(eng):
            flow.play("tensor", eng)


def kernel(**inputs):
    import concourse.bacc as bacc
    from concourse.bass_utils import run_bass_kernel_spmd

    a = {k: np.asarray(v) for k, v in inputs.items()}
    n_nodes, n_edges = a["x"].shape[0], a["src"].shape[0]
    nj, ec = padded_sizes(n_nodes, n_edges)
    np_, ep = P * nj, P * ec

    def padded(v, rows, fill=0):
        return np.concatenate([v, np.full((rows - v.shape[0],) + v.shape[1:], fill, v.dtype)])

    dst = padded(a["dst"], ep, np_ - 1)
    ch = chunk_len(ep)

    def row(v):
        return v.reshape(1, -1)

    arrays = {
        "x": padded(a["x"], np_).reshape(P, nj, D),
        "src": padded(a["src"], ep).reshape(P, ec),
        "dst": dst.reshape(P, ec),
        "dst_prev": np.concatenate([np.full(1, -1, dst.dtype), dst.reshape(P, ec)[:-1, -1]]).reshape(P, 1),
        "dst_last": dst.reshape(-1, ch)[:, -1].reshape(1, -1),
        "edge_type": padded(a["edge_type_8"], ep).reshape(P, ec),
        "ea128": padded(a["edge_attr_128"], ep).reshape(P, ec, D),
        "ea13": padded(a["edge_attr_13"], ep).reshape(P, ec, -1),
        "a_w": a["L0_gnn_W"],
        "a_att_src": row(a["L0_gnn_att_src"]),
        "a_att_dst": row(a["L0_gnn_att_dst"]),
        "a_bias": row(a["L0_gnn_bias"]),
        "a_gamma": row(a["L0_gnn_gamma"]),
        "a_beta": row(a["L0_gnn_beta"]),
        "b_w": a["L1_gnn_W"],
        "b_att_src": a["L1_gnn_att_src"],
        "b_att_dst": a["L1_gnn_att_dst"],
        "b_w_edge": a["L1_gnn_W_edge"],
        "b_att_edge": a["L1_gnn_att_edge"],
        "b_bias": row(a["L1_gnn_bias"]),
        "b_gamma": row(a["L1_gnn_ln_gamma"]),
        "b_beta": row(a["L1_gnn_ln_beta"]),
        "c_u": a["L2_gnn_u"][0].reshape(-1, 1),
        "c_w1": a["L2_gnn_W1"],
        "c_b1": a["L2_gnn_b1"].reshape(-1, 1),
        "c_w2": a["L2_gnn_W2"],
        "c_b2": a["L2_gnn_b2"].reshape(-1, 1),
        "c_w3": a["L2_gnn_W3"],
        "c_b3": row(a["L2_gnn_b3"]),
        "W_rel": a["L3_gnn_W_rel"],
        "d_self_wT": a["L3_gnn_W_self_w"].T,
        "d_self_b": row(a["L3_gnn_W_self_b"]),
    }
    arrays = {k: np.ascontiguousarray(v) for k, v in arrays.items()}

    nc = bacc.Bacc("TRN2", target_bir_lowering=False, num_devices=1)
    io = {k: nc.dram_tensor(f"in_{k}", v.shape, mybir.dt.from_np(v.dtype), kind="ExternalInput").ap()
          for k, v in arrays.items()}
    io["out"] = nc.dram_tensor("out_x", (np_, D), F32, kind="ExternalOutput").ap()
    build(nc, io, n_nodes, n_edges)
    result = run_bass_kernel_spmd(nc, [{f"in_{k}": v for k, v in arrays.items()}], core_ids=[0])
    return result.results[0]["out_x"][:n_nodes]
```

```python
from contextlib import ExitStack
from itertools import cycle
import math

import numpy as np
import concourse.bass as bass
from concourse import mybir

F32 = mybir.dt.float32
I32 = mybir.dt.int32
ALU = mybir.AluOpType
ACT = mybir.ActivationFunctionType
AX = mybir.AxisListType.X

P = 128
D = 128
GC = 16
BIG = 1.0e30
EPS = 1e-5
SLOPE = 0.2


def padded_sizes(n_nodes, n_edges):
    nj = -(-n_nodes // P)
    ec = -(-n_edges // (P * GC)) * GC
    return nj, ec


def chunk_len(ep):
    return min((d for d in range(1, ep + 1) if ep % d == 0), key=lambda d: abs(d - math.sqrt(ep)))


class Flow:
    ENGINES = ("sync", "scalar", "gpsimd", "vector", "tensor")

    def __init__(self, nc, ctx):
        self.nc, self.ctx = nc, ctx
        self.queue = {e: [] for e in self.ENGINES}
        self.dma_sems = []
        self.n = 0
        self.stage_name = ""
        self.begin("start")

    def begin(self, name):
        self.done = {e: [None, 0] for e in self.ENGINES}
        self.dma_sems = []
        self.stage_name = name

    def sem(self, name):
        self.n += 1
        return self.ctx.enter_context(self.nc.semaphore(f"{self.stage_name}_{name}_{self.n}"))

    def op(self, engine, fn, *waits):
        d = self.done[engine]
        if d[0] is None:
            d[0] = self.sem(engine)
        d[1] += 1
        self.queue[engine].append((waits, fn, d[0], 1))
        return (d[0], d[1])

    def last(self, engine):
        d = self.done[engine]
        return tuple(d) if d[1] else None

    def dma_sem(self, name):
        s = [self.sem(name), 0]
        self.dma_sems.append(s)
        return s

    def dma(self, engine, fn, s, *waits):
        s[1] += 16
        self.queue[engine].append((waits, fn, s[0], 16))
        return (s[0], s[1])

    def barrier(self, name):
        tokens = [tuple(d) for d in self.done.values() if d[1]] + [tuple(s) for s in self.dma_sems if s[1]]
        for e in self.ENGINES:
            self.queue[e].append((tokens, None, None, 0))
        self.begin(name)

    def play(self, name, engine):
        seen = {}
        for waits, fn, s, by in self.queue[name]:
            for w in waits:
                if w is not None and seen.get(w[0].name, 0) < w[1]:
                    engine.wait_ge(w[0], w[1])
                    seen[w[0].name] = w[1]
            if fn is not None:
                fn(engine).then_inc(s, by)


def past(tokens, what, k):
    return tokens[what, k] if k >= 0 else None


def skewed(stages, n):
    for step in range(n + len(stages) - 1):
        for s in reversed(range(len(stages))):
            if 0 <= step - s < n:
                stages[s](step - s)


def build(nc, io, n_nodes, n_edges):
    NJ, EC = padded_sizes(n_nodes, n_edges)
    NP, EP = P * NJ, P * EC
    NG = EC // GC
    CH = chunk_len(EP)
    NCH = EP // CH
    JB = max(d for d in range(1, 8) if NJ % d == 0)
    NK = NJ // JB
    NREL = io["W_rel"].shape[0]
    EF = io["ea13"].shape[-1]

    def dram(name, shape, dt=F32):
        return nc.dram_tensor(name, list(shape), dt).ap()

    class Layer:
        def __init__(self, name, heads, edge_terms):
            self.H, self.C = heads, D // heads
            self.NW = heads * (self.C + 1)
            self.M0 = self.NW
            self.A0 = self.NW + heads
            self.AE = heads if edge_terms else 0
            self.W = self.A0 + self.AE
            self.WN = self.NW + self.AE
            self.table = dram(f"table_{name}", [NP, self.W])
            self.sums = dram(f"sums_{name}", [EP + P, self.W])
            self.dst_logit = dram(f"dst_logit_{name}", [EP + NP, heads])
            self.node_logit = dram(f"node_logit_{name}", [NP, heads])

    A = Layer("a", 1, False)
    B = Layer("b", io["b_att_src"].shape[0], True)
    sums_attr = dram("sums_attr", [EP + P, D])
    table_rel = dram("table_rel", [NP * NREL, D])
    sums_rel = dram("sums_rel", [EP + P, D])
    dst_float = dram("dst_float", [NCH, CH])

    with ExitStack() as ctx:
        flow = Flow(nc, ctx)
        op, dma = flow.op, flow.dma

        def V(fn, *w):
            return op("vector", fn, *w, flow.last("vector"))

        def S(fn, *w): return op("scalar", fn, *w)
        def T(fn, *w): return op("tensor", fn, *w)

        def buffers(where):
            def sb(name, shape, dt=F32):
                flow.n += 1
                return where.enter_context(nc.sbuf_tensor(f"{name}_{flow.n}", list(shape), dt))
            return sb

        sb = sb_kept = buffers(ctx)
        ps = ctx.enter_context(nc.psum_tensor("ps", [P, 8, 512], F32))

        x = sb("x", [P, NJ, D])
        ident = sb("ident", [P, P])
        ones = sb("ones", [P, P])
        rel_row = sb("rel_row", [P, EC], I32)
        dst_first = sb("dst_first", [P, 1], I32)
        keep = sb("keep", [P, EC])
        keep_all = sb("keep_all", [P, 1])
        cut_all = sb("cut_all", [P, 1])
        head_row = sb("head_row", [P, 1], I32)
        sum_row = sb("sum_row", [P, NJ], I32)
        start_row = sb("start_row", [P, NJ], I32)
        has = sb("has", [P, NJ])
        no_edge = sb("no_edge", [P, NJ])
        inv_deg = sb("inv_deg", [P, NJ])
        mean_rs = sb("mean_rs", [P, NJ])
        mean_nb = sb("mean_nb", [P, NJ])
        node_a = sb("node_logit_a", [P, NJ, A.H])
        node_b = sb("node_logit_b", [P, NJ, B.H])
        stats = sb("stats", [P, 2, JB, 6])
        mv = sb("mv", [P, 2, JB, 2])
        std = sb("std", [P, 2, JB])

        until_edges_b = ExitStack()
        sb_edges = buffers(until_edges_b)
        src = sb_edges("src_i", [P, EC], I32)
        cut = sb_edges("cut", [P, EC])

        def bc(ap, shape):
            return ap.broadcast_to(shape)

        def over_nodes(ap):
            return bc(ap.unsqueeze(1), [P, JB, D])

        def chunk(ap, k):
            return ap[:, k * JB:(k + 1) * JB, :]

        def layer_norm_begin(k, data, mv, std, *w):
            for b in range(JB):
                t = op("vector", lambda e, b=b: e.bn_stats(stats[:, k % 2, b, :], data[:, b, :]), *w)
            for b in range(JB):
                op("vector", lambda e, b=b: e.bn_aggr(mv[:, b, :], stats[:, k % 2, b, :]), t)
            t = V(lambda e: e.tensor_scalar(std, mv[:, :, 1], EPS, None, ALU.add))
            return S(lambda e: e.activation(std, std, ACT.Sqrt), t)

        def layer_norm_end(mv, std, rs, nb, *w):
            t = V(lambda e: e.reciprocal(rs, std), *w)
            return V(lambda e: e.scalar_tensor_tensor(nb, mv[:, :, 0], -1.0, rs, ALU.mult, ALU.mult), t)

        def norm_relu(k, out, data, rs, nb, *w):
            for b in range(JB):
                t = S(lambda e, b=b: e.activation(out[:, b, :], data[:, b, :], ACT.Relu,
                                                  bias=nb[:, b:b + 1], scale=rs[:, b:b + 1]), *w)
            return t

        def load_extended_weights(L, sb, w_dram, att_src, att_dst):
            w = sb("w_plain", [P, L.H, L.C])
            att = sb("att", [P, 2, L.H, L.C])
            prod = sb("w_att", [P, L.H, L.C])
            ext = sb("w_ext", [P, L.W + L.H])
            sem_w = flow.dma_sem("w")
            dma("sync", lambda e: e.dma_start(w[:, :, :], w_dram.rearrange("k (h c) -> k h c", h=L.H)), sem_w)
            dma("sync", lambda e: e.dma_start(att[:, 0, :, :].rearrange("p h c -> p (h c)"),
                                              att_src.broadcast_to([P, D])), sem_w)
            t_w = dma("sync", lambda e: e.dma_start(att[:, 1, :, :].rearrange("p h c -> p (h c)"),
                                                    att_dst.broadcast_to([P, D])), sem_w)
            t = V(lambda e: e.memset(ext[:, :], 0.0))
            last = V(lambda e: e.tensor_copy(
                ext[:, 0:L.NW].rearrange("p (h c) -> p h c", h=L.H)[:, :, 0:L.C], w[:, :, :]), t, t_w)
            for i, at in ((0, L.M0), (1, L.W)):
                t = V(lambda e, i=i: e.tensor_tensor(prod[:, :, :], w[:, :, :], att[:, i, :, :], ALU.mult),
                      t_w, last)
                last = V(lambda e, at=at: e.tensor_reduce(ext[:, at:at + L.H], prod[:, :, :], AX, ALU.add), t)
            return ext, last

        def table_stages(L, sb, ext, t_ext, node_l, first, sem_scatter=None):
            hn = sb("hn", [P, 2, JB, D])
            hT = sb("hT", [P, 2, JB * P])
            rows = sb("rows", [P, 2, JB, L.W])
            sem_rows = [flow.dma_sem(f"rows{i}") for i in range(2)]
            tok, turned = {}, {}
            WX = L.W + L.H

            def stats_of(k):
                s = k % 2
                tok["root", k] = layer_norm_begin(k, chunk(x, k), mv[:, s, :, :], std[:, s, :], first(k))

            def norm(k):
                s, j = k % 2, slice(k * JB, (k + 1) * JB)
                tok["n", k] = layer_norm_end(mv[:, s, :, :], std[:, s, :], mean_rs[:, j], mean_nb[:, j],
                                             tok["root", k])
                tok["h", k] = norm_relu(k, hn[:, s, :, :], x[:, j, :], mean_rs[:, j], mean_nb[:, j],
                                        tok["n", k], past(tok, "T", k - 2))

            def turn(k):
                for b in range(JB):
                    tok["T", k] = T(lambda e, b=b: e.transpose(
                        ps[:, b // 4, (b % 4) * P:(b % 4 + 1) * P], hn[:, k % 2, b, :], ident[:, :]),
                        tok["h", k], *turned.get(k - 1, ()))

                for i in range(0, JB, 4):
                    n = min(4, JB - i)
                    out, data = hT[:, k % 2, i * P:(i + n) * P], ps[:, i // 4, 0:n * P]
                    if i:
                        t = S(lambda e, out=out, data=data: e.activation(out, data, ACT.Copy),
                              tok["T", k], past(tok, "P", k - 2))
                    else:
                        t = op("vector", lambda e, out=out, data=data: e.tensor_copy(out, data),
                               tok["T", k], past(tok, "P", k - 2))
                    turned.setdefault(k, []).append(t)

            def project(k):
                for b in range(JB):
                    t = T(lambda e, b=b: e.matmul(
                        ps[:, 2 + b // 3, (b % 3) * WX:(b % 3 + 1) * WX],
                        hT[:, k % 2, b * P:(b + 1) * P], ext[:, :], start=True, stop=True),
                        *turned[k], t_ext, past(tok, "C", k - 1))
                tok["P", k] = t
                for i in range(0, JB, 3):
                    n = min(3, JB - i)
                    src_ps = ps[:, 2 + i // 3, 0:n * WX].rearrange("p (n w) -> p n w", w=WX)
                    tok["C", k] = S(lambda e, i=i, n=n, v=src_ps: e.activation(
                        rows[:, k % 2, i:i + n, :], v[:, :, 0:L.W], ACT.Copy), t, past(tok, "D", k - 2))
                    tok["C", k] = S(lambda e, i=i, n=n, v=src_ps: e.activation(
                        node_l[:, k * JB + i:k * JB + i + n, :], v[:, :, L.W:WX], ACT.Copy))

            def store(k):
                one = rows[:, k % 2, :, 0:L.NW].rearrange("p j (h c) -> p j h c", h=L.H)[:, :, :, L.C]
                t = V(lambda e: e.memset(one, 1.0), tok["C", k])
                tok["D", k] = dma("sync", lambda e: e.dma_start(
                    L.table.rearrange("(p j) w -> p j w", j=NJ)[:, k * JB:(k + 1) * JB, :],
                    rows[:, k % 2, :, :]), sem_rows[k % 2], t)
                if sem_scatter:
                    scatter_logits(L, node_l, range(k * JB, (k + 1) * JB), sem_scatter, tok["C", k])

            return [stats_of, norm, turn, project, store]

        def scatter_logits(L, node_l, blocks, sem, *w):
            for j in blocks:
                t = dma("gpsimd", lambda e, j=j: e.indirect_dma_start(
                    out=L.dst_logit, out_offset=bass.IndirectOffsetOnAxis(ap=start_row[:, j:j + 1], axis=0),
                    in_=node_l[:, j, :], in_offset=None), sem, *w)
            return t

        def expand_dst_logits(L, dst_l):
            sem_ld = flow.dma_sem("dst_logit")
            sem_first = flow.dma_sem("first")
            t = dma("sync", lambda e: e.dma_start(
                dst_l[:, :, :], L.dst_logit[0:EP, :].rearrange("(p c) h -> p c h", c=EC)), sem_ld)
            t = dma("gpsimd", lambda e: e.indirect_dma_start(
                out=dst_l[:, 0, :], out_offset=None, in_=L.node_logit,
                in_offset=bass.IndirectOffsetOnAxis(ap=dst_first[:, 0:1], axis=0)), sem_first, t)
            for h in range(L.H):
                V(lambda e, h=h: e.tensor_tensor_scan(dst_l[:, :, h], keep[:, :], dst_l[:, :, h], 0.0,
                                                      ALU.mult, ALU.add), t)

        def store_node_logits(L, node_l, t):
            dma("sync", lambda e: e.dma_start(
                L.node_logit.rearrange("(p j) h -> p j h", j=NJ), node_l[:, :, :]),
                flow.dma_sem("node_logit"), t)

        flow.begin("graph")
        with ExitStack() as local:
            sb = buffers(local)
            dst = sb("dst_i", [P, EC], I32)
            typ = sb("typ_i", [P, EC], I32)
            dst_f = sb("dst_f", [P, EC])
            last_i = sb("last_i", [P, NCH], I32)
            last_f = sb("last_f", [P, NCH])
            zero = sb("zero", [P, EC])
            tmp_e = sb("tmp_e", [P, EC])
            prev_i = sb("prev_i", [P, 1], I32)
            prev_f = sb("prev_f", [P, 1])
            iot = sb("iot", [P, NJ + 1], I32)
            v = sb("threshold", [P, NJ + 1])
            col_i = sb("col_i", [P, P], I32)
            own_i = sb("own_i", [P, 1], I32)
            own_f = sb("own_f", [P, 1])
            junk = sb("junk", [P, 2, NCH])
            q = sb("piece_of", [P, NJ + 1])
            q_i = sb("q_i", [P, NJ + 1], I32)
            cnt = sb("cnt", [P, NJ + 1])
            NPIECE = 2 * JB
            piece = sb("piece", [P, NPIECE, CH])
            fine = sb("fine", [P, 2, CH])
            quotient = sb("quotient", [P, NJ], I32)
            s1 = sb("s1", [P, NJ])
            s2 = sb("s2", [P, NJ])
            s3 = sb("s3", [P, NJ])
            s4 = sb("s4", [P, NJ])
            s5 = sb("s5", [P, NJ])
            s6 = sb("s6", [P, NJ])
            hc = sb("head_count", [P, 1])

            sem_dst = flow.dma_sem("dst")
            sem_last = flow.dma_sem("last")
            sem_x = [flow.dma_sem(f"x{k}") for k in range(NK)]
            sem_idx = flow.dma_sem("idx")
            sem_prev = flow.dma_sem("prev")
            sem_zero = flow.dma_sem("zero")
            sem_dstf = flow.dma_sem("dstf")
            t_dst = dma("sync", lambda e: e.dma_start(dst[:, :], io["dst"]), sem_dst)
            t_last = dma("scalar", lambda e: e.dma_start(
                last_i[:, :], io["dst_last"][0:1, :].broadcast_to([P, NCH])), sem_last)
            t_idx = dma("scalar", lambda e: e.dma_start(src[:, :], io["src"]), sem_idx)
            t_idx = dma("scalar", lambda e: e.dma_start(typ[:, :], io["edge_type"]), sem_idx)
            t_prev = dma("scalar", lambda e: e.dma_start(prev_i[:, :], io["dst_prev"]), sem_prev)
            t_f = V(lambda e: e.tensor_copy(dst_f[:, :], dst[:, :]), t_dst)
            t_store = dma("sync", lambda e: e.dma_start(
                dst_float.rearrange("a b -> (a b)").rearrange("(p c) -> p c", c=EC), dst_f[:, :]),
                sem_dstf, t_f)
            ext_a, t_ext_a = load_extended_weights(A, sb, io["a_w"], io["a_att_src"], io["a_att_dst"])
            t_x = [dma("sync", lambda e, k=k: e.dma_start(chunk(x, k), chunk(io["x"], k)), sem_x[k])
                   for k in range(NK)]
            t_z = V(lambda e: e.memset(zero[:, :], 0.0))
            for L in (A, B):
                flat = L.dst_logit[0:EP, :].rearrange("(p c) h -> p (c h)", c=EC)
                for k in range(L.H):
                    dma("sync", lambda e, o=flat[:, k * EC:(k + 1) * EC]: e.dma_start(o, zero[:, :]),
                        sem_zero, t_z)
            t_i = op("gpsimd", lambda e: e.iota(iot[:, :], [[1, NJ + 1]], base=-1, channel_multiplier=NJ))
            t_i2 = op("gpsimd", lambda e: e.iota(col_i[:, :], [[1, P]], base=0, channel_multiplier=-1))
            t_i4 = op("gpsimd", lambda e: e.iota(own_i[:, :], [[0, 1]], base=0, channel_multiplier=EC))
            V(lambda e: e.tensor_scalar(ident[:, :], col_i[:, :], 0.0, None, ALU.is_equal), t_i2)
            V(lambda e: e.memset(ones[:, :], 1.0))
            t_own = V(lambda e: e.tensor_copy(own_f[:, :], own_i[:, :]), t_i4)
            t_v = V(lambda e: e.tensor_copy(v[:, :], iot[:, :]), t_i)
            t_lf = V(lambda e: e.tensor_copy(last_f[:, :], last_i[:, :]), t_last)
            sem_piece = [flow.dma_sem(f"piece{k}") for k in range(NPIECE)]
            sem_scatter = flow.dma_sem("scatter")
            used = {"threshold": t_v}

            def thresholds(k):
                return range(k * JB + (k > 0), (k + 1) * JB + 1)

            def count_pieces(k):
                js = thresholds(k)
                for j in js:
                    t = used["coarse", j] = op("vector", lambda e, j=j: e.tensor_scalar(
                        junk[:, j % 2, 0:NCH], last_f[:, :], v[:, j:j + 1], None, ALU.is_le, ALU.add,
                        accum_out=q[:, j:j + 1]), used.get(("coarse", j - 2), t_v), t_lf)
                js = slice(js[0], js[-1] + 1)
                t = V(lambda e: e.tensor_scalar(q[:, js], q[:, js], float(NCH - 1), None, ALU.min), t)
                used["q", k] = V(lambda e: e.tensor_copy(q_i[:, js], q[:, js]), t)

            def fetch_pieces(k):
                for j in thresholds(k):
                    used["fetched", j] = dma("gpsimd", lambda e, j=j: e.indirect_dma_start(
                        out=piece[:, j % NPIECE, :], out_offset=None, in_=dst_float,
                        in_offset=bass.IndirectOffsetOnAxis(ap=q_i[:, j:j + 1], axis=0)),
                        sem_piece[j % NPIECE], used["q", k], t_store, past(used, "piece", j - NPIECE))

            def count_in_pieces(k):
                js = thresholds(k)
                for j in js:
                    t = used["piece", j] = op("vector", lambda e, j=j: e.tensor_scalar(
                        fine[:, j % 2, :], piece[:, j % NPIECE, :], v[:, j:j + 1], None, ALU.is_le,
                        ALU.add, accum_out=cnt[:, j:j + 1]), used["fetched", j], past(used, "piece", j - 2))
                js = slice(js[0], js[-1] + 1)
                n = slice(k * JB, (k + 1) * JB)
                start, end = cnt[:, k * JB:(k + 1) * JB], cnt[:, k * JB + 1:(k + 1) * JB + 1]
                t = V(lambda e: e.scalar_tensor_tensor(cnt[:, js], q[:, js], float(CH), cnt[:, js], ALU.mult,
                                                       ALU.add), t)
                V(lambda e: e.tensor_tensor(has[:, n], end, start, ALU.is_gt), t)
                t = V(lambda e: e.tensor_scalar(s5[:, n], v[:, n], float(EP + 1), None, ALU.add), t)
                t = V(lambda e: e.tensor_tensor(s6[:, n], start, s5[:, n], ALU.subtract), t)
                t = V(lambda e: e.tensor_tensor(s6[:, n], s6[:, n], has[:, n], ALU.mult), t)
                t = V(lambda e: e.tensor_tensor(s6[:, n], s6[:, n], s5[:, n], ALU.add), t)
                used["start", k] = V(lambda e: e.tensor_copy(start_row[:, n], s6[:, n]), t)

            def scatter(k):
                scatter_logits(A, node_a, range(k * JB, (k + 1) * JB), sem_scatter, used["start", k],
                               used["logit", k], (sem_zero[0], sem_zero[1]))
            def edge_places():
                V(lambda e: e.memset(keep[:, 0:1], 0.0))
                t = V(lambda e: e.tensor_tensor(keep[:, 1:EC], dst_f[:, 1:EC], dst_f[:, 0:EC - 1], ALU.is_equal),
                      t_f)
                yield
                V(lambda e: e.tensor_scalar(cut[:, :], keep[:, :], BIG, -BIG, ALU.mult, ALU.add), t)
                yield
                t = V(lambda e: e.tensor_copy(prev_f[:, :], prev_i[:, :]), t_prev)
                t = V(lambda e: e.tensor_tensor(keep_all[:, :], prev_f[:, :], dst_f[:, EC - 1:EC], ALU.is_equal), t)
                V(lambda e: e.tensor_scalar(cut_all[:, :], keep_all[:, :], BIG, -BIG, ALU.mult, ALU.add), t)
                yield
                t = V(lambda e: e.tensor_scalar(tmp_e[:, :], dst_f[:, :], dst_f[:, 0:1], None, ALU.is_equal,
                                                ALU.add, accum_out=hc[:, :]), t_f)
                t = V(lambda e: e.scalar_tensor_tensor(hc[:, :], hc[:, :], -1.0, own_f[:, :], ALU.add, ALU.add),
                      t, t_own)
                V(lambda e: e.tensor_copy(head_row[:, :], hc[:, :]), t)
                V(lambda e: e.tensor_copy(dst_first[:, :], dst[:, 0:1]))
                yield
                t = V(lambda e: e.tensor_copy(tmp_e[:, :], src[:, :]), t_idx)
                t2 = V(lambda e: e.tensor_copy(zero[:, :], typ[:, :]), (sem_zero[0], sem_zero[1]))
                yield
                t = V(lambda e: e.scalar_tensor_tensor(tmp_e[:, :], tmp_e[:, :], float(NREL), zero[:, :],
                                                       ALU.mult, ALU.add), t, t2)
                yield
                V(lambda e: e.tensor_copy(rel_row[:, :], tmp_e[:, :]), t)
                yield

            table_a = table_stages(A, sb, ext_a, t_ext_a, node_a, lambda k: t_x[k])
            store_table = table_a[-1]

            def store(k):
                store_table(k)
                used["logit", k] = flow.last("scalar")
                next(places, None)
            places = edge_places()
            skewed([count_pieces, fetch_pieces, count_in_pieces] + table_a[:-1] + [store, scatter], NK)
            for step in places:
                pass
            store_node_logits(A, node_a, flow.last("scalar"))
            start, end = cnt[:, 0:NJ], cnt[:, 1:NJ + 1]
            t_deg = V(lambda e: e.tensor_tensor(s4[:, :], end, start, ALU.subtract), flow.last("vector"))
            t_l = V(lambda e: e.tensor_scalar(s1[:, :], end, -1.0, 0.0, ALU.add, ALU.max))
            V(lambda e: e.tensor_scalar(no_edge[:, :], has[:, :], BIG, -BIG, ALU.mult, ALU.add))
            t_deg = V(lambda e: e.tensor_scalar(s4[:, :], s4[:, :], 1.0, None, ALU.max), t_deg)
            t_deg = V(lambda e: e.reciprocal(s4[:, :], s4[:, :]), t_deg)
            V(lambda e: e.tensor_tensor(inv_deg[:, :], s4[:, :], has[:, :], ALU.mult), t_deg)
            V(lambda e: e.tensor_scalar(s2[:, :], s1[:, :], 1.0 / EC, None, ALU.mult), t_l)
            V(lambda e: e.tensor_copy(quotient[:, :], s2[:, :]))
            V(lambda e: e.tensor_copy(s2[:, :], quotient[:, :]))
            V(lambda e: e.scalar_tensor_tensor(s3[:, :], s2[:, :], float(-EC), s1[:, :], ALU.mult, ALU.add))
            V(lambda e: e.tensor_scalar(s6[:, :], s3[:, :], float(EC), None, ALU.is_ge))
            V(lambda e: e.tensor_tensor(s2[:, :], s2[:, :], s6[:, :], ALU.add))
            V(lambda e: e.tensor_scalar(s6[:, :], s3[:, :], 0.0, None, ALU.is_lt))
            t_p = V(lambda e: e.tensor_tensor(s2[:, :], s2[:, :], s6[:, :], ALU.subtract))
            t = V(lambda e: e.tensor_scalar(s3[:, :], s2[:, :], float(EC), None, ALU.mult), t_p)
            t = V(lambda e: e.tensor_tensor(s3[:, :], start, s3[:, :], ALU.is_lt), t)
            t = V(lambda e: e.tensor_tensor(s3[:, :], s3[:, :], has[:, :], ALU.mult), t)
            t2 = V(lambda e: e.scalar_tensor_tensor(s2[:, :], s2[:, :], float(EP), s1[:, :], ALU.add,
                                                    ALU.subtract), t)
            t = V(lambda e: e.tensor_tensor(s2[:, :], s2[:, :], s3[:, :], ALU.mult), t2)
            t = V(lambda e: e.tensor_tensor(s2[:, :], s2[:, :], s1[:, :], ALU.add), t)
            t = V(lambda e: e.tensor_copy(sum_row[:, :], s2[:, :]), t)
            flow.barrier("expand_a")

        def groups_of(ap):
            return ap[0:EP, :].rearrange("(p c) w -> p c w", c=EC)

        def finish_crossing(name, sb, sums, W, tail, t_stored, L=None):
            WN = L.WN if L else D
            rest = WN - P
            head = sb(f"{name}_head", [P, W])
            xs = sb(f"{name}_state", [P, WN])
            ys = sb(f"{name}_decay", [P, WN])
            xT = sb(f"{name}_stateT", [P, 2, P])
            yT = sb(f"{name}_decayT", [P, 2, P])
            cT = sb(f"{name}_carryT", [P, 2, P + 1])
            sem_head = flow.dma_sem(f"{name}_head")
            sem_row = flow.dma_sem(f"{name}_row")
            t_head = dma("gpsimd", lambda e: e.indirect_dma_start(
                out=head[:, :], out_offset=None, in_=sums[0:EP, :],
                in_offset=bass.IndirectOffsetOnAxis(ap=head_row[:, 0:1], axis=0)), sem_head, *t_stored)
            t0 = V(lambda e: e.memset(cT[:, :, 0:1], 0.0))
            if L:
                H = L.H
                mrow = sb(f"{name}_mrow", [H, 2 * P])
                run = sb(f"{name}_run", [H, P + 1])
                mcut = sb(f"{name}_mcut", [P, H])
                m = sb(f"{name}_m", [P, 2 * H])
                ex = sb(f"{name}_ex", [P, 2 * H])
                mx = sb(f"{name}_mx", [P, H])
                tm = tail[:, L.M0:L.M0 + H]
                t = V(lambda e: e.tensor_copy(mcut[:, :], bc(cut_all[:, :], [P, H])))
                t = T(lambda e: e.transpose(ps[0:H, 0, P:2 * P], mcut[:, :], ident[:, :]), t)
                t = T(lambda e: e.transpose(ps[0:H, 0, 0:P], tm, ident[:, :]))
                t = V(lambda e: e.tensor_copy(mrow[:, :], ps[0:H, 0, 0:2 * P]), t)
                t1 = V(lambda e: e.memset(run[:, 0:1], -BIG))
                t = V(lambda e: e.tensor_tensor_scan(run[:, 1:P + 1], mrow[:, P:2 * P], mrow[:, 0:P], -BIG,
                                                     ALU.add, ALU.max), t, t1)
                T(lambda e: e.transpose(ps[:, 1, 0:H], run[:, 1:P + 1], ident[0:H, 0:H]), t)
                t = T(lambda e: e.transpose(ps[:, 1, H:2 * H], run[:, 0:P], ident[0:H, 0:H]), t)
                t = V(lambda e: e.tensor_copy(m[:, :], ps[:, 1, 0:2 * H]), t)
                V(lambda e: e.tensor_tensor(ex[:, 0:H], tm, m[:, 0:H], ALU.subtract), t)
                t = V(lambda e: e.tensor_tensor(ex[:, H:2 * H], m[:, H:2 * H], m[:, 0:H], ALU.subtract), t)
                t = V(lambda e: e.tensor_tensor(ex[:, H:2 * H], ex[:, H:2 * H], mcut[:, :], ALU.add), t)
                t = S(lambda e: e.activation(ex[:, :], ex[:, :], ACT.Exp), t)

                def heads(ap):
                    return ap.rearrange("p (h c) -> p h c", h=H)
                wide = [P, H, L.C + 1]
                V(lambda e: e.tensor_tensor(heads(xs[:, 0:L.NW]), heads(tail[:, 0:L.NW]),
                                            bc(ex[:, 0:H].unsqueeze(2), wide), ALU.mult), t)
                t = V(lambda e: e.tensor_copy(heads(ys[:, 0:L.NW]), bc(ex[:, H:2 * H].unsqueeze(2), wide)))
                if L.AE:
                    V(lambda e: e.tensor_copy(xs[:, L.NW:WN], tail[:, L.A0:L.W]))
                    t = V(lambda e: e.tensor_copy(ys[:, L.NW:WN], bc(keep_all[:, :], [P, L.AE])))
            else:
                V(lambda e: e.tensor_copy(xs[:, :], tail))
                t = V(lambda e: e.tensor_copy(ys[:, :], bc(keep_all[:, :], [P, D])))
            parts = [(0, 0, P)] + ([(1, P, rest)] if rest else [])
            for i, a, n in parts:
                T(lambda e, i=i, a=a, n=n: e.transpose(ps[0:n, 2, i * P:(i + 1) * P], xs[:, a:a + n],
                                                       ident[:, :]), t)
                t2 = T(lambda e, i=i, a=a, n=n: e.transpose(ps[0:n, 3, i * P:(i + 1) * P], ys[:, a:a + n],
                                                            ident[:, :]), t)
            for i, a, n in parts:
                V(lambda e, i=i, n=n: e.tensor_copy(xT[0:n, i, :], ps[0:n, 2, i * P:(i + 1) * P]), t2)
                t3 = V(lambda e, i=i, n=n: e.tensor_copy(yT[0:n, i, :], ps[0:n, 3, i * P:(i + 1) * P]), t2)
            for i, a, n in parts:
                t4 = V(lambda e, i=i, n=n: e.tensor_tensor_scan(cT[0:n, i, 1:P + 1], yT[0:n, i, :],
                                                                xT[0:n, i, :], 0.0, ALU.mult, ALU.add), t3)
            for i, a, n in parts:
                t5 = T(lambda e, i=i, a=a, n=n: e.transpose(ps[:, 4, a:a + n], cT[0:n, i, 0:P],
                                                            ident[0:n, 0:n]), t4, t0)
            if L:
                t = V(lambda e: e.tensor_tensor(mx[:, :], head[:, L.M0:L.M0 + H], m[:, H:2 * H], ALU.max),
                      t_head, t5)
                V(lambda e: e.tensor_tensor(ex[:, 0:H], head[:, L.M0:L.M0 + H], mx[:, :], ALU.subtract), t)
                t = V(lambda e: e.tensor_tensor(ex[:, H:2 * H], m[:, H:2 * H], mx[:, :], ALU.subtract), t)
                t = S(lambda e: e.activation(ex[:, :], ex[:, :], ACT.Exp), t)
                t1 = V(lambda e: e.tensor_tensor(heads(head[:, 0:L.NW]), heads(head[:, 0:L.NW]),
                                                 bc(ex[:, 0:H].unsqueeze(2), wide), ALU.mult), t)
                t2 = V(lambda e: e.tensor_tensor(heads(xs[:, 0:L.NW]), heads(ps[:, 4, 0:L.NW]),
                                                 bc(ex[:, H:2 * H].unsqueeze(2), wide), ALU.mult), t)
                t3 = V(lambda e: e.tensor_tensor(head[:, 0:L.NW], head[:, 0:L.NW], xs[:, 0:L.NW], ALU.add), t2)
                if L.AE:
                    V(lambda e: e.tensor_tensor(head[:, L.A0:L.W], head[:, L.A0:L.W], ps[:, 4, L.NW:WN],
                                                ALU.add))
                t3 = V(lambda e: e.tensor_copy(head[:, L.M0:L.M0 + H], mx[:, :]))
            else:
                t3 = V(lambda e: e.tensor_tensor(head[:, :], head[:, :], ps[:, 4, 0:D], ALU.add), t_head, t5)
            dma("sync", lambda e: e.dma_start(sums[EP:EP + P, :], head[:, :]), sem_row, t3)

        def attention_edges(L, sb, dst_l, attr=None, terms=None, edge_logit=None):
            H, C, NW = L.H, L.C, L.NW
            NS = 6 if attr is None else 5
            AHEAD = NS - 2
            rows = sb("edge_rows", [P, NS, GC, L.W])
            z = sb("z", [P, 2, GC, H])
            run = sb("run_max", [P, 2, GC + 1, H])
            wd = sb("weight_decay", [P, 2, 2 * GC, H])
            old = sb("old", [P, 2, H, C + 1])
            sem_g = [flow.dma_sem(f"gather{i}") for i in range(NS)]
            sem_s = [flow.dma_sem(f"store{i}") for i in range(NS)]
            tok = {}
            if attr is not None:
                NA = 4
                attrs = sb("attrs", [P, NA, GC, D])
                sem_al = [flow.dma_sem(f"attr_load{i}") for i in range(NA)]
                sem_as = [flow.dma_sem(f"attr_store{i}") for i in range(NA)]
            if terms is not None:
                feat_dram, proj = terms
                feats = sb("feats", [P, 2, GC, EF])
                prod = sb("feat_prod", [P, GC, B.H, EF])
                sem_f = [flow.dma_sem(f"feats{i}") for i in range(2)]

            def U(fn, *w):
                return op("vector", fn, *w)

            def cols(g):
                return slice(g * GC, (g + 1) * GC)

            def fetch(g):
                s = g % NS
                for c in range(GC):
                    tok["G", g] = dma("gpsimd", lambda e, c=c: e.indirect_dma_start(
                        out=rows[:, s, c, :], out_offset=None, in_=L.table,
                        in_offset=bass.IndirectOffsetOnAxis(ap=src[:, g * GC + c:g * GC + c + 1], axis=0)),
                        sem_g[s], past(tok, "S", g - NS), past(tok, "main", g - NS + 1))

            def fetch_extra(g):
                if attr is not None:
                    tok["AL", g] = dma("sync", lambda e: e.dma_start(
                        attrs[:, g % NA, :, :], attr[:, cols(g), :]), sem_al[g % NA],
                        past(tok, "AS", g - NA), past(tok, "attr", g - NA + 1))
                if terms is not None:
                    tok["F", g] = dma("sync", lambda e: e.dma_start(
                        feats[:, g % 2, :, :], feat_dram[:, cols(g), :]), sem_f[g % 2], past(tok, "ae", g - 2))

            def logits(g):
                s, b = g % NS, g % 2
                R = rows[:, s, :, :]
                tz = U(lambda e: e.tensor_tensor(z[:, b, :, :], R[:, :, L.M0:L.M0 + H], dst_l[:, cols(g), :],
                                                 ALU.add), tok["G", g])
                yield
                if L.AE:
                    tz = U(lambda e: e.tensor_tensor(z[:, b, :, :], z[:, b, :, :], edge_logit[:, cols(g), :],
                                                     ALU.add), tz)
                    yield
                tz = U(lambda e: e.scalar_tensor_tensor(z[:, b, :, :], z[:, b, :, :], SLOPE, z[:, b, :, :],
                                                        ALU.mult, ALU.max), tz)
                yield
                if g == 0:
                    t0 = U(lambda e: e.memset(run[:, b, 0:1, :], -BIG))
                else:
                    t0 = U(lambda e: e.tensor_copy(run[:, b, 0:1, :], run[:, 1 - b, GC:GC + 1, :]),
                           tok["run", g - 1])
                yield
                for h in range(H):
                    init = -BIG if g == 0 else run[:, 1 - b, GC, h:h + 1]
                    tr = U(lambda e, h=h, init=init: e.tensor_tensor_scan(
                        run[:, b, 1:GC + 1, h], cut[:, cols(g)], z[:, b, :, h], init, ALU.add, ALU.max),
                        tz, past(tok, "run", g - 1))
                    yield
                tok["run", g] = tr
                if L.AE:
                    for h in range(H):
                        at = L.A0 + h
                        init = 0.0 if g == 0 else rows[:, (g - 1) % NS, GC - 1, at:at + 1]
                        t_ae = U(lambda e, h=h, at=at, init=init: e.tensor_tensor_scan(
                            R[:, :, at], keep[:, cols(g)], edge_logit[:, cols(g), h], init, ALU.mult,
                            ALU.add), past(tok, "ae_run", g - 1))
                        yield
                    tok["ae_run", g] = t_ae
                U(lambda e: e.tensor_tensor(wd[:, b, 0:GC, :], z[:, b, :, :], run[:, b, 1:GC + 1, :],
                                            ALU.subtract), tr)
                yield
                td = U(lambda e: e.tensor_tensor(wd[:, b, GC:2 * GC, :], run[:, b, 0:GC, :],
                                                 run[:, b, 1:GC + 1, :], ALU.subtract), tr, t0)
                yield
                td = U(lambda e: e.tensor_tensor(
                    wd[:, b, GC:2 * GC, :], wd[:, b, GC:2 * GC, :],
                    bc(cut[:, cols(g)].unsqueeze(2), [P, GC, H]), ALU.add), td)
                tok["exp", g] = S(lambda e: e.activation(wd[:, b, :, :], wd[:, b, :, :], ACT.Exp), td)
                yield
                U(lambda e: e.tensor_copy(R[:, :, L.M0:L.M0 + H], run[:, b, 1:GC + 1, :]), tr)
                if terms is not None:
                    yield
                    t = U(lambda e: e.tensor_tensor(
                        prod[:, :, :, :], bc(feats[:, b, :, :].unsqueeze(2), [P, GC, B.H, EF]),
                        bc(proj[:, :, :].unsqueeze(1), [P, GC, B.H, EF]), ALU.mult), tok["F", g])
                    yield
                    tok["ae", g] = U(lambda e: e.tensor_reduce(edge_logit[:, cols(g), :], prod[:, :, :, :], AX,
                                                               ALU.add), t)

            def running_sums(g):
                s, b = g % NS, g % 2
                R = rows[:, s, :, :]
                num = R[:, :, 0:NW].rearrange("p c (h k) -> p c h k", h=H)
                if H == 1:
                    weighted = [S(lambda e, c=c: e.activation(R[:, c, 0:NW], R[:, c, 0:NW], ACT.Copy,
                                                              scale=wd[:, b, c, :]), tok["exp", g])
                                for c in range(GC)]
                    t = past(tok, "main", g - 1)
                else:
                    t = U(lambda e: e.tensor_tensor(num, num, bc(wd[:, b, 0:GC, :].unsqueeze(3),
                                                                 [P, GC, H, C + 1]), ALU.mult),
                          tok["exp", g], past(tok, "main", g - 1))
                    yield
                t_a = past(tok, "attr", g - 1)
                for c in range(GC):
                    if g == 0 and c == 0:
                        continue
                    prev = rows[:, s, c - 1, 0:NW] if c else rows[:, (g - 1) % NS, GC - 1, 0:NW]
                    if H == 1:
                        t = U(lambda e, c=c, prev=prev: e.scalar_tensor_tensor(
                            R[:, c, 0:NW], prev, wd[:, b, GC + c, :], R[:, c, 0:NW], ALU.mult, ALU.add),
                            t, weighted[c])
                        yield
                    else:
                        t = U(lambda e, c=c, prev=prev: e.tensor_tensor(
                            old[:, c % 2, :, :], prev.rearrange("p (h k) -> p h k", h=H),
                            bc(wd[:, b, GC + c, :].unsqueeze(2), [P, H, C + 1]), ALU.mult), t)
                        yield
                        t = U(lambda e, c=c: e.tensor_tensor(
                            R[:, c, 0:NW], R[:, c, 0:NW], old[:, c % 2, :, :].rearrange("p h k -> p (h k)"),
                            ALU.add), t)
                        yield
                    if attr is not None:
                        a = attrs[:, g % NA, c, :]
                        pa = attrs[:, g % NA, c - 1, :] if c else attrs[:, (g - 1) % NA, GC - 1, :]
                        t_a = U(lambda e, c=c, a=a, pa=pa: e.scalar_tensor_tensor(
                            a, pa, keep[:, g * GC + c:g * GC + c + 1], a, ALU.mult, ALU.add),
                            tok["AL", g], t_a)
                        yield
                tok["main", g], tok["attr", g] = t, t_a

            def store(g):
                tok["S", g] = dma("sync", lambda e: e.dma_start(
                    groups_of(L.sums)[:, cols(g), :], rows[:, g % NS, :, :]), sem_s[g % NS], tok["main", g])
                if attr is not None:
                    tok["AS", g] = dma("sync", lambda e: e.dma_start(
                        groups_of(sums_attr)[:, cols(g), :], attrs[:, g % NA, :, :]), sem_as[g % NA],
                        tok["attr", g])

            for g in range(min(AHEAD, NG)):
                fetch(g)
            for g in range(min(2, NG)):
                fetch_extra(g)
            for _ in logits(0):
                pass
            for g in range(NG):
                if g + AHEAD < NG:
                    fetch(g + AHEAD)
                if g + 2 < NG:
                    fetch_extra(g + 2)
                both = [running_sums(g)] + ([logits(g + 1)] if g + 1 < NG else [])
                while both:
                    both = [x for x in both if next(x, "over") != "over"]
                store(g)
            last = (NG - 1) % NS
            t_stored = [tok["S", g] for g in range(max(0, NG - NS), NG)]
            finish_crossing("att", sb, L.sums, L.W, rows[:, last, GC - 1, :], t_stored, L)
            if attr is not None:
                t_as = [tok["AS", g] for g in range(max(0, NG - NA), NG)]
                finish_crossing("attr", sb, sums_attr, D, attrs[:, (NG - 1) % NA, GC - 1, :],
                                t_as + [flow.last("vector")])

        def node_rows(sb, name, sums, W, depth=2):
            buf = sb(name, [P, depth, JB, W])
            sems = [flow.dma_sem(f"{name}{i}") for i in range(depth)]

            def gather(k, *w):
                for b in range(JB):
                    j = k * JB + b
                    t = dma("gpsimd", lambda e, b=b, j=j: e.indirect_dma_start(
                        out=buf[:, k % depth, b, :], out_offset=None, in_=sums,
                        in_offset=bass.IndirectOffsetOnAxis(ap=sum_row[:, j:j + 1], axis=0)),
                        sems[k % depth], *w)
                return t
            return buf, gather

        def attention_nodes(L, sb, node_l, out_of):
            H, C = L.H, L.C
            R, gather = node_rows(sb, "node_sums", L.sums, L.W)
            own = sb("own_rows", [P, 2, JB, L.W])
            z = sb("self_logit", [P, 2, JB, H])
            ex = sb("self_ex", [P, 2, 2, JB, H])
            mx = sb("self_max", [P, 2, JB, H])
            den = sb("den", [P, 2, JB, H])
            sem_own = [flow.dma_sem(f"own{i}") for i in range(2)]
            tok = {}
            bj = [P, JB, H]

            def fetch(k):
                tok["R", k] = gather(k, past(tok, "O", k - 2))
                tok["own", k] = dma("sync", lambda e: e.dma_start(
                    own[:, k % 2, :, :],
                    L.table.rearrange("(p j) w -> p j w", j=NJ)[:, k * JB:(k + 1) * JB, :]),
                    sem_own[k % 2], past(tok, "O", k - 2))

            def logit(k):
                s, j = k % 2, slice(k * JB, (k + 1) * JB)
                zz, r, m = z[:, s, :, :], R[:, s, :, :], mx[:, s, :, :]
                t = V(lambda e: e.tensor_tensor(zz, own[:, s, :, L.M0:L.M0 + H], node_l[:, j, :], ALU.add),
                      tok["own", k])
                if L.AE:
                    t2 = V(lambda e: e.tensor_tensor(m, r[:, :, L.A0:L.W], bc(inv_deg[:, j].unsqueeze(2), bj),
                                                     ALU.mult), tok["R", k])
                    t = V(lambda e: e.tensor_tensor(zz, zz, m, ALU.add), t, t2)
                t = V(lambda e: e.scalar_tensor_tensor(zz, zz, SLOPE, zz, ALU.mult, ALU.max), t)
                rm = r[:, :, L.M0:L.M0 + H]
                t2 = V(lambda e: e.tensor_tensor(rm, rm, bc(has[:, j].unsqueeze(2), bj), ALU.mult), tok["R", k])
                t2 = V(lambda e: e.tensor_tensor(rm, rm, bc(no_edge[:, j].unsqueeze(2), bj), ALU.add), t2)
                t = V(lambda e: e.tensor_tensor(m, rm, zz, ALU.max), t, t2)
                V(lambda e: e.tensor_tensor(ex[:, s, 0, :, :], rm, m, ALU.subtract), t)
                t = V(lambda e: e.tensor_tensor(ex[:, s, 1, :, :], zz, m, ALU.subtract), t)
                tok["E", k] = S(lambda e: e.activation(ex[:, s, :, :, :], ex[:, s, :, :, :], ACT.Exp), t)

            def join(k):
                s = k % 2
                wide = [P, JB, H, C + 1]

                def heads(ap):
                    return ap[:, :, 0:L.NW].rearrange("p j (h c) -> p j h c", h=H)
                a, b = heads(R[:, s, :, :]), heads(own[:, s, :, :])
                V(lambda e: e.tensor_tensor(a, a, bc(ex[:, s, 0, :, :].unsqueeze(3), wide), ALU.mult),
                  tok["E", k])
                t = V(lambda e: e.tensor_tensor(b, b, bc(ex[:, s, 1, :, :].unsqueeze(3), wide), ALU.mult))
                t = V(lambda e: e.tensor_tensor(a, a, b, ALU.add), t)
                if L.AE:
                    t = V(lambda e: e.tensor_scalar(den[:, s, :, :], a[:, :, :, C], 1e-16, None, ALU.add), t)
                    t = V(lambda e: e.reciprocal(den[:, s, :, :], den[:, s, :, :]), t)
                else:
                    t = V(lambda e: e.reciprocal(den[:, s, :, :], a[:, :, :, C]), t)
                t = V(lambda e: e.tensor_tensor(
                    out_of(k).rearrange("p j (h c) -> p j h c", h=H), a[:, :, :, 0:C],
                    bc(den[:, s, :, :].unsqueeze(3), [P, JB, H, C]), ALU.mult), t)
                tok["O", k] = t

            return [fetch, logit, join], tok

        edge_logit = sb_edges("edge_logit", [P, EC, B.H])
        with ExitStack() as local:
            sb = buffers(local)
            dst_l = sb("dst_logit", [P, EC, A.H])
            proj = sb("edge_proj", [P, B.H, EF])
            weights = ExitStack()
            we = buffers(weights)("w_edge", [P, EF, B.H, B.C])
            att_e = buffers(weights)("att_edge", [P, B.H, B.C])
            sem_we = flow.dma_sem("w_edge")
            dma("sync", lambda e: e.dma_start(
                we[:, :, :, :].rearrange("p k h c -> p (k h c)"),
                io["b_w_edge"].rearrange("k d -> (k d)").unsqueeze(0).broadcast_to([P, EF * D])), sem_we)
            t = dma("sync", lambda e: e.dma_start(
                att_e[:, :, :].rearrange("p h c -> p (h c)"),
                io["b_att_edge"].rearrange("h c -> (h c)").unsqueeze(0).broadcast_to([P, D])), sem_we)
            t = V(lambda e: e.tensor_tensor(we[:, :, :, :], we[:, :, :, :],
                                            bc(att_e[:, :, :].unsqueeze(1), [P, EF, B.H, B.C]), ALU.mult), t)
            V(lambda e: e.tensor_reduce(proj[:, :, :].rearrange("p h k -> p k h"), we[:, :, :, :], AX,
                                        ALU.add), t)
            expand_dst_logits(A, dst_l)
            flow.barrier("edges_a")
            weights.close()
            attention_edges(A, sb, dst_l, attr=io["ea128"], terms=(io["ea13"], proj), edge_logit=edge_logit)
            flow.barrier("nodes_a")

        with ExitStack() as local:
            sb = buffers(local)
            agg = sb("agg", [P, NJ, D])
            bn_par = sb("bn_par", [P, 3, D])
            mean = sb("bn_mean", [P, D])
            scale = sb("bn_scale", [P, D])
            square = sb("square", [P, 2, JB, D])
            sem_par = flow.dma_sem("par")
            ext_b, t_ext_b = load_extended_weights(B, sb, io["b_w"], io["b_att_src"].rearrange(
                "h c -> (h c)").unsqueeze(0), io["b_att_dst"].rearrange("h c -> (h c)").unsqueeze(0))
            for i, name in enumerate(("a_bias", "a_gamma", "a_beta")):
                t_par = dma("sync", lambda e, i=i, name=name: e.dma_start(
                    bn_par[:, i, :], io[name].broadcast_to([P, D])), sem_par)
            stages, tok = attention_nodes(A, sb, node_a, lambda k: chunk(agg, k))

            def rows_valid(j):
                return (n_nodes - j + NJ - 1) // NJ

            def column_sums(k, data, bank, *w):
                for b in range(JB):
                    j = k * JB + b
                    K = rows_valid(j)
                    t = T(lambda e, b=b, j=j, K=K: e.matmul(
                        ps[:, bank, 0:D], ones[0:K, :], data[0:K, b, :], start=(j == 0),
                        stop=(j == NJ - 1)), *w)
                return t

            def add_bias(k):
                tok["B", k] = V(lambda e: e.tensor_tensor(chunk(agg, k), chunk(agg, k),
                                                          over_nodes(bn_par[:, 0, :]), ALU.add),
                                tok["O", k], t_par)
                tok["sum"] = column_sums(k, chunk(agg, k), 0, tok["B", k])
            skewed(stages + [add_bias], NK)
            t = V(lambda e: e.tensor_scalar(mean[:, :], ps[:, 0, 0:D], 1.0 / n_nodes, None, ALU.mult),
                  tok["sum"])
            tok["mean"] = t

            def centre(k):
                tok["c", k] = V(lambda e: e.tensor_tensor(chunk(agg, k), chunk(agg, k),
                                                          over_nodes(mean[:, :]), ALU.subtract),
                                tok["mean"])
                t = S(lambda e: e.activation(square[:, k % 2, :, :], chunk(agg, k), ACT.Square),
                      tok["c", k], past(tok, "q", k - 2))
                tok["q", k] = column_sums(k, square[:, k % 2, :, :], 1, t)
            skewed([centre], NK)
            t = V(lambda e: e.tensor_scalar(scale[:, :], ps[:, 1, 0:D], 1.0 / n_nodes, EPS, ALU.mult,
                                            ALU.add), tok["q", NK - 1])
            t = S(lambda e: e.activation(scale[:, :], scale[:, :], ACT.Sqrt), t)
            t = V(lambda e: e.reciprocal(scale[:, :], scale[:, :]), t)
            tok["scale"] = V(lambda e: e.tensor_tensor(scale[:, :], scale[:, :], bn_par[:, 1, :], ALU.mult), t)

            def residual(k):
                t = V(lambda e: e.tensor_tensor(chunk(agg, k), chunk(agg, k), over_nodes(scale[:, :]),
                                                ALU.mult), tok["scale"])
                t = V(lambda e: e.tensor_tensor(chunk(agg, k), chunk(agg, k), over_nodes(bn_par[:, 2, :]),
                                                ALU.add), t)
                tok["x", k] = V(lambda e: e.scalar_tensor_tensor(chunk(x, k), chunk(agg, k), 0.0,
                                                                 chunk(x, k), ALU.max, ALU.add), t)
            sem_scatter = flow.dma_sem("scatter")
            table_b = table_stages(B, sb, ext_b, t_ext_b, node_b, lambda k: tok["x", k], sem_scatter)
            skewed([residual] + table_b, NK)
            store_node_logits(B, node_b, flow.last("scalar"))
            flow.barrier("expand_b")

        with ExitStack() as local:
            sb = buffers(local)
            dst_l = sb("dst_logit", [P, EC, B.H])
            expand_dst_logits(B, dst_l)
            flow.barrier("edges_b")
            attention_edges(B, sb, dst_l, edge_logit=edge_logit)
            flow.barrier("nodes_b")
        until_edges_b.close()

        own_part = sb_kept("own_part", [P, NJ, D])
        with ExitStack() as local:
            sb = buffers(local)
            par = sb("par", [P, 4, D])
            w1 = sb("w1", [P, 3, D])
            w2 = sb("w2", [P, D])
            w3 = sb("w3", [P, D])
            w_rel = sb("w_rel", [P, NREL, D])
            u0 = sb("u0", [P, 1])
            b12 = sb("b12", [P, 3])
            sem_par = flow.dma_sem("par")
            for i, name in enumerate(("b_bias", "b_gamma", "b_beta", "c_b3")):
                dma("sync", lambda e, i=i, name=name: e.dma_start(
                    par[:, i, :], io[name].broadcast_to([P, D])), sem_par)
            dma("scalar", lambda e: e.dma_start(w1[:, :, :], io["c_w1"].rearrange("(a k) d -> k a d", k=P)), sem_par)
            dma("scalar", lambda e: e.dma_start(w2[:, :], io["c_w2"]), sem_par)
            dma("scalar", lambda e: e.dma_start(w3[:, :], io["c_w3"]), sem_par)
            dma("scalar", lambda e: e.dma_start(w_rel[:, :, :], io["W_rel"].rearrange("r k d -> k r d")), sem_par)
            dma("scalar", lambda e: e.dma_start(u0[:, :], io["c_u"]), sem_par)
            dma("scalar", lambda e: e.dma_start(b12[:, 0:1], io["c_b1"]), sem_par)
            t_par = dma("scalar", lambda e: e.dma_start(b12[:, 1:2], io["c_b2"]), sem_par)
            t = T(lambda e: e.matmul(ps[:, 0, 0:1], w1[:, 2, :], u0[:, :], start=True, stop=True), t_par)
            t_b1 = V(lambda e: e.tensor_tensor(b12[:, 2:3], b12[:, 0:1], ps[:, 0, 0:1], ALU.add), t)

            out_b = sb("out_b", [P, 3, JB, D])
            h1 = sb("h1", [P, 2, JB, D])
            hn2, hn3 = sb("hn2", [P, 2, JB, D]), sb("hn3", [P, JB, D])
            hT2, aT = sb("hT2", [P, 2, JB * P]), sb("aT", [P, JB * P])
            mid1, mid2 = sb("mid1", [P, JB * P]), sb("mid2", [P, JB * P])
            NSR = 3
            rel = sb("rel", [P, NSR, NREL, D])
            sem_rel = [flow.dma_sem(f"rel{i}") for i in range(NSR)]
            stages, tok = attention_nodes(B, sb, node_b, lambda k: out_b[:, k % 3, :, :])
            sums_a, gather_a = node_rows(sb, "attr_sums", sums_attr, D)
            bank_free = {i: t_b1 for i in range(8)}
            halves = [(0, min(4, JB))] + ([(4, JB - 4)] if JB > 4 else [])
            pairs = cycle([(0, 1), (2, 3)])
            waiting = []

            def read_later(fn):
                read_now()
                waiting.append(fn)

            def read_now():
                if waiting:
                    waiting.pop()()

            class Norm:
                def __init__(self, name):
                    self.name = name
                    self.mv, self.std = sb(f"{name}_mv", [P, 2, JB, 2]), sb(f"{name}_std", [P, 2, JB])
                    self.rs, self.nb = sb(f"{name}_rs", [P, 2, JB]), sb(f"{name}_nb", [P, 2, JB])

                def begin(self, k, data, t):
                    s = k % 2
                    tok[self.name, "root", k] = layer_norm_begin(k, data, self.mv[:, s, :, :],
                                                                 self.std[:, s, :], t)

                def end(self, k, out, data, func, *w):
                    s = k % 2
                    t = layer_norm_end(self.mv[:, s, :, :], self.std[:, s, :], self.rs[:, s, :],
                                       self.nb[:, s, :], tok[self.name, "root", k],
                                       tok.get((self.name, "out", k - 2)))
                    for b in range(JB):
                        t2 = S(lambda e, b=b: e.activation(out[:, b, :], data[:, b, :], func,
                                                           bias=self.nb[:, s, b:b + 1],
                                                           scale=self.rs[:, s, b:b + 1]), t, *w)
                    tok[self.name, "out", k] = t2
                    return t2

            norm1, norm2, norm3 = Norm("norm1"), Norm("norm2"), Norm("norm3")

            def turned(k, name, out, data, *w):
                banks, t_half = next(pairs), []
                for bank, (i, n) in zip(banks, halves):
                    for m in range(n):
                        t = T(lambda e, bank=bank, i=i, m=m: e.transpose(
                            ps[:, bank, m * P:(m + 1) * P], data[:, i + m, :], ident[:, :]),
                            bank_free[bank], *w)
                    t_half.append(t)
                tok["T" + name, k] = t

                def read():
                    for at, (bank, (i, n)) in enumerate(zip(banks, halves)):
                        o = out[:, i * P:(i + n) * P]
                        if at:
                            bank_free[bank] = S(lambda e, bank=bank, o=o, n=n: e.activation(
                                o, ps[:, bank, 0:n * P], ACT.Copy), t_half[at])
                        else:
                            bank_free[bank] = op("vector", lambda e, bank=bank, o=o, n=n: e.tensor_copy(
                                o, ps[:, bank, 0:n * P]), t_half[at])
                        tok["turned" + name, at, k] = bank_free[bank]
                read_later(read)

            def both(name, k):
                return [tok["turned" + name, at, k] for at in range(len(halves))]

            def residual_input(k):
                s, j = k % 2, slice(k * JB, (k + 1) * JB)
                stages_join(k)
                t = norm_relu(k, h1[:, s, :, :], chunk(x, k), mean_rs[:, j], mean_nb[:, j],
                              past(tok, "y", k - 2))
                tok["h1", k] = op("gpsimd", lambda e: e.tensor_tensor(
                    h1[:, s, :, :], h1[:, s, :, :], over_nodes(par[:, 0, :]), ALU.add), t, t_par)

            def residual_1(k):
                y = out_b[:, k % 3, :, :]
                t = op("vector", lambda e: e.tensor_tensor(y, y, h1[:, k % 2, :, :], ALU.add),
                       tok["O", k], tok["h1", k])
                tok["y", k] = t
                norm1.begin(k, y, t)

            def norm_1(k):
                y = out_b[:, k % 3, :, :]
                norm1.end(k, y, y, ACT.Identity)

            def residual_2(k):
                y = out_b[:, k % 3, :, :]
                t = V(lambda e: e.tensor_tensor(y, y, over_nodes(par[:, 1, :]), ALU.mult),
                      tok["norm1", "out", k])
                t = V(lambda e: e.tensor_tensor(y, y, over_nodes(par[:, 2, :]), ALU.add), t)
                t = V(lambda e: e.scalar_tensor_tensor(chunk(x, k), y, 0.0, chunk(x, k), ALU.max, ALU.add), t)
                norm2.begin(k, chunk(x, k), t)

            def norm_2(k):
                norm2.end(k, hn2[:, k % 2, :, :], chunk(x, k), ACT.Relu, past(tok, "Th2", k - 2))
                tok["a", k] = gather_a(k, past(tok, "Ta", k - 2))

            def turn_2(k):
                turned(k, "h2", hT2[:, k % 2, :], hn2[:, k % 2, :, :], tok["norm2", "out", k])
                j = slice(k * JB, (k + 1) * JB)
                tok["am", k] = op("gpsimd", lambda e: e.tensor_tensor(
                    sums_a[:, k % 2, :, :], sums_a[:, k % 2, :, :], bc(has[:, j].unsqueeze(2), [P, JB, D]),
                    ALU.mult), tok["a", k])
                tok["xb", k] = op("gpsimd", lambda e: e.tensor_tensor(
                    chunk(x, k), chunk(x, k), over_nodes(par[:, 3, :]), ALU.add), tok["norm2", "out", k])

            def turn_sums(k):
                turned(k, "a", aT[:, :], sums_a[:, k % 2, :, :], tok["am", k])

            def product(k, name, weights, out, bias, *w):
                banks, t_half = next(pairs), []
                for bank, (i, n) in zip(banks, halves):
                    c = slice(i * P, (i + n) * P)
                    for m, (wt, data) in enumerate(weights):
                        t = T(lambda e, bank=bank, n=n, c=c, m=m, wt=wt, data=data: e.matmul(
                            ps[:, bank, 0:n * P], wt, data[:, c], start=(m == 0),
                            stop=(m == len(weights) - 1)), bank_free[bank], *w)
                    t_half.append(t)

                def read():
                    for t, bank, (i, n) in zip(t_half, banks, halves):
                        c = slice(i * P, (i + n) * P)
                        tok[name, k] = bank_free[bank] = S(lambda e, bank=bank, n=n, c=c: e.activation(
                            out[:, c], ps[:, bank, 0:n * P], ACT.Relu, bias=bias), t)
                read_later(read)

            def hidden_1(k):
                product(k, "m1", [(w1[:, 0, :], hT2[:, k % 2, :]), (w1[:, 1, :], aT[:, :])],
                        mid1[:, :], b12[:, 2:3], *both("h2", k), *both("a", k))

            def hidden_2(k):
                product(k, "m2", [(w2[:, :], mid1[:, :])], mid2[:, :], b12[:, 1:2], tok["m1", k])

            def mlp_out(k):
                banks, t_half = next(pairs), []
                for bank, (i, n) in zip(banks, halves):
                    for m in range(n):
                        t = T(lambda e, bank=bank, i=i, m=m: e.matmul(
                            ps[:, bank, m * P:(m + 1) * P], mid2[:, (i + m) * P:(i + m + 1) * P],
                            w3[:, :], start=True, stop=True), bank_free[bank], tok["m2", k])
                    t_half.append(t)

                def read():
                    for t, bank, (i, n) in zip(t_half, banks, halves):
                        xs = x[:, k * JB + i:k * JB + i + n, :].rearrange("p j d -> p (j d)")
                        bank_free[bank] = op("vector", lambda e, bank=bank, n=n, xs=xs: e.tensor_tensor(
                            xs, xs, ps[:, bank, 0:n * P], ALU.add), t, tok["xb", k])
                    norm3.begin(k, chunk(x, k), bank_free[bank])
                read_later(read)

            def norm_3(k):
                norm3.end(k, hn3[:, :, :], chunk(x, k), ACT.Relu, past(tok, "Th3", k - 1))

            def turn_3(k):
                turned(k, "h3", chunk(own_part, k).rearrange("p j d -> p (j d)"), hn3[:, :, :], tok["norm3", "out", k])

            def relations(k):
                half = NREL // 2
                late = None
                for b in range(JB):
                    j = k * JB + b
                    r, bank = j % NSR, 4 + 2 * (j % 2)
                    block = own_part[:, j, :]
                    for i in range(2):
                        t = T(lambda e, i=i, block=block, bank=bank: e.matmul(
                            ps[:, bank + i, 0:half * D], block,
                            w_rel[:, i * half:(i + 1) * half, :].rearrange("p r d -> p (r d)"),
                            start=True, stop=True), *both("h3", k), bank_free[bank + i])
                    if late:
                        late()

                    def late(j=j, r=r, bank=bank, t=t):
                        t1 = bank_free[bank] = S(lambda e: e.activation(
                            rel[:, r, 0:half, :].rearrange("p r d -> p (r d)"),
                            ps[:, bank, 0:half * D], ACT.Copy), t, past(tok, "rel", j - NSR))
                        t2 = bank_free[bank + 1] = op("vector", lambda e: e.tensor_copy(
                            rel[:, r, half:NREL, :].rearrange("p r d -> p (r d)"),
                            ps[:, bank + 1, 0:half * D]), t, past(tok, "rel", j - NSR))
                        tok["rel", j] = dma("sync", lambda e: e.dma_start(
                            table_rel.rearrange("(p j r) d -> p j (r d)", j=NJ, r=NREL)[:, j, :],
                            rel[:, r, :, :].rearrange("p r d -> p (r d)")), sem_rel[r], t1, t2)
                    yield
                late()

            stages_join = stages[2]
            before = stages[:2] + [residual_input, residual_1, norm_1, residual_2, norm_2, turn_2,
                                   turn_sums, hidden_1, hidden_2, mlp_out, norm_3, turn_3]
            for step in range(NK + len(before)):
                k_last = step - len(before)
                blocks = relations(k_last) if k_last >= 0 else iter(())
                for s in reversed(range(len(before))):
                    if 0 <= step - s < NK:
                        before[s](step - s)
                        if s % 2:
                            next(blocks, None)
                for _ in blocks:
                    pass
                read_now()
            flow.barrier("edges_rel")

        with ExitStack() as local:
            sb = buffers(local)
            NS, AHEAD = 6, 4
            rows = sb("edge_rows", [P, NS, GC, D])
            sem_g = [flow.dma_sem(f"gather{i}") for i in range(NS)]
            sem_s = [flow.dma_sem(f"store{i}") for i in range(NS)]
            tok = {}

            def fetch(g):
                s = g % NS
                for c in range(GC):
                    tok["G", g] = dma("gpsimd", lambda e, c=c: e.indirect_dma_start(
                        out=rows[:, s, c, :], out_offset=None, in_=table_rel,
                        in_offset=bass.IndirectOffsetOnAxis(ap=rel_row[:, g * GC + c:g * GC + c + 1],
                                                            axis=0)),
                        sem_g[s], past(tok, "S", g - NS), past(tok, "main", g - NS + 1))

            def own_parts():
                for i, j0 in enumerate(range(0, NJ, 4)):
                    n, bank = min(4, NJ - j0), 6 + i % 2
                    for j in range(j0, j0 + n):
                        t = T(lambda e, j=j, j0=j0, bank=bank: e.matmul(
                            ps[:, bank, (j - j0) * P:(j - j0 + 1) * P], own_part[:, j, :], w_self[:, :],
                            start=True, stop=True), t_self, past(tok, "own", i - 2))
                    tok["own", i] = op("vector", lambda e, j0=j0, n=n, bank=bank: e.tensor_tensor(
                        own_part[:, j0:j0 + n, :], ps[:, bank, 0:n * P].rearrange("p (n d) -> p n d", d=D),
                        bc(b_self[:, :].unsqueeze(1), [P, n, D]), ALU.add), t)
                    yield

            w_self = sb("w_self", [P, D])
            b_self = sb("b_self", [P, D])
            sem_self = flow.dma_sem("self")
            dma("scalar", lambda e: e.dma_start(w_self[:, :], io["d_self_wT"]), sem_self)
            t_self = dma("scalar", lambda e: e.dma_start(b_self[:, :], io["d_self_b"].broadcast_to([P, D])),
                         sem_self)
            own_steps = own_parts()
            for g in range(min(AHEAD, NG)):
                fetch(g)
            t = None
            for g in range(NG):
                if g + AHEAD < NG:
                    fetch(g + AHEAD)
                next(own_steps, None)
                s = g % NS
                for c in range(GC):
                    if g or c:
                        prev = rows[:, s, c - 1, :] if c else rows[:, (g - 1) % NS, GC - 1, :]
                        t = V(lambda e, s=s, c=c, g=g, prev=prev: e.scalar_tensor_tensor(
                            rows[:, s, c, :], prev, keep[:, g * GC + c:g * GC + c + 1], rows[:, s, c, :],
                            ALU.mult, ALU.add), tok["G", g], t)
                tok["main", g] = t
                tok["S", g] = dma("sync", lambda e, g=g, s=s: e.dma_start(
                    groups_of(sums_rel)[:, g * GC:(g + 1) * GC, :], rows[:, s, :, :]), sem_s[s], t)
            for step in own_steps:
                pass
            finish_crossing("rel", sb, sums_rel, D, rows[:, (NG - 1) % NS, GC - 1, :],
                            [tok["S", g] for g in range(max(0, NG - NS), NG)])
            flow.barrier("nodes_rel")

        with ExitStack() as local:
            sb = buffers(local)
            R, gather = node_rows(sb, "node_sums", sums_rel, D, 3)
            sem_out = [flow.dma_sem(f"out{i}") for i in range(3)]
            tok = {}

            def fetch_rel(k):
                tok["R", k] = gather(k, past(tok, "S", k - 3))

            def last(k):
                r, j = R[:, k % 3, :, :], slice(k * JB, (k + 1) * JB)
                t = V(lambda e: e.tensor_tensor(r, r, bc(inv_deg[:, j].unsqueeze(2), [P, JB, D]), ALU.mult),
                      tok["R", k])
                t = V(lambda e: e.tensor_tensor(r, r, chunk(own_part, k), ALU.add), t)
                t = V(lambda e: e.scalar_tensor_tensor(r, r, 0.0, chunk(x, k), ALU.max, ALU.add), t)
                tok["S", k] = dma("sync", lambda e: e.dma_start(
                    chunk(io["out"].rearrange("(p j) d -> p j d", j=NJ), k), r), sem_out[k % 3], t)
            skewed([fetch_rel, last], NK)
            flow.barrier("end")

        block = ctx.enter_context(nc.Block())

        @block.sync
        def _(eng):
            flow.play("sync", eng)

        @block.scalar
        def _(eng):
            flow.play("scalar", eng)

        @block.gpsimd
        def _(eng):
            flow.play("gpsimd", eng)

        @block.vector
        def _(eng):
            flow.play("vector", eng)

        @block.tensor
        def _(eng):
            flow.play("tensor", eng)


def kernel(**inputs):
    import concourse.bacc as bacc
    from concourse.bass_utils import run_bass_kernel_spmd

    a = {k: np.asarray(v) for k, v in inputs.items()}
    n_nodes, n_edges = a["x"].shape[0], a["src"].shape[0]
    nj, ec = padded_sizes(n_nodes, n_edges)
    np_, ep = P * nj, P * ec

    def padded(v, rows, fill=0):
        return np.concatenate([v, np.full((rows - v.shape[0],) + v.shape[1:], fill, v.dtype)])

    dst = padded(a["dst"], ep, np_ - 1)
    ch = chunk_len(ep)

    def row(v):
        return v.reshape(1, -1)

    arrays = {
        "x": padded(a["x"], np_).reshape(P, nj, D),
        "src": padded(a["src"], ep).reshape(P, ec),
        "dst": dst.reshape(P, ec),
        "dst_prev": np.concatenate([np.full(1, -1, dst.dtype), dst.reshape(P, ec)[:-1, -1]]).reshape(P, 1),
        "dst_last": dst.reshape(-1, ch)[:, -1].reshape(1, -1),
        "edge_type": padded(a["edge_type_8"], ep).reshape(P, ec),
        "ea128": padded(a["edge_attr_128"], ep).reshape(P, ec, D),
        "ea13": padded(a["edge_attr_13"], ep).reshape(P, ec, -1),
        "a_w": a["L0_gnn_W"],
        "a_att_src": row(a["L0_gnn_att_src"]),
        "a_att_dst": row(a["L0_gnn_att_dst"]),
        "a_bias": row(a["L0_gnn_bias"]),
        "a_gamma": row(a["L0_gnn_gamma"]),
        "a_beta": row(a["L0_gnn_beta"]),
        "b_w": a["L1_gnn_W"],
        "b_att_src": a["L1_gnn_att_src"],
        "b_att_dst": a["L1_gnn_att_dst"],
        "b_w_edge": a["L1_gnn_W_edge"],
        "b_att_edge": a["L1_gnn_att_edge"],
        "b_bias": row(a["L1_gnn_bias"]),
        "b_gamma": row(a["L1_gnn_ln_gamma"]),
        "b_beta": row(a["L1_gnn_ln_beta"]),
        "c_u": a["L2_gnn_u"][0].reshape(-1, 1),
        "c_w1": a["L2_gnn_W1"],
        "c_b1": a["L2_gnn_b1"].reshape(-1, 1),
        "c_w2": a["L2_gnn_W2"],
        "c_b2": a["L2_gnn_b2"].reshape(-1, 1),
        "c_w3": a["L2_gnn_W3"],
        "c_b3": row(a["L2_gnn_b3"]),
        "W_rel": a["L3_gnn_W_rel"],
        "d_self_wT": a["L3_gnn_W_self_w"].T,
        "d_self_b": row(a["L3_gnn_W_self_b"]),
    }
    arrays = {k: np.ascontiguousarray(v) for k, v in arrays.items()}

    nc = bacc.Bacc("TRN2", target_bir_lowering=False, num_devices=1)
    io = {k: nc.dram_tensor(f"in_{k}", v.shape, mybir.dt.from_np(v.dtype), kind="ExternalInput").ap()
          for k, v in arrays.items()}
    io["out"] = nc.dram_tensor("out_x", (np_, D), F32, kind="ExternalOutput").ap()
    build(nc, io, n_nodes, n_edges)
    result = run_bass_kernel_spmd(nc, [{f"in_{k}": v for k, v in arrays.items()}], core_ids=[0])
    return result.results[0]["out_x"][:n_nodes]
```
